# Optimizing a Trainium2 kernel written in Bass

```python
import numpy as np
import jax
import jax.numpy as jnp

def _softmax(x, axis=-1):
    return jax.nn.softmax(x, axis=axis)

def _gelu(x):
    return jax.nn.gelu(x, approximate=True)

def _silu(x):
    return jax.nn.silu(x)

def _sigmoid(x):
    return jax.nn.sigmoid(x)

def _layernorm(x, axis=-1, eps=1e-05):
    m = jnp.mean(x, axis=axis, keepdims=True)
    v = jnp.var(x, axis=axis, keepdims=True)
    return (x - m) / jnp.sqrt(v + eps)

def _scatter_add(tgt, idx, src, axis=0):
    return tgt.at[idx].add(src)

def _segment_sum(src, seg, n):
    return jax.ops.segment_sum(src, seg, n)
kernel_name = 'mk_prb_d1_jaxref_r4_e0f608'

def setup_inputs(seed: int=0):
    np.random.seed(seed)
    _w = jnp.asarray

    def _L0_attn_setup():
        import jax, jax.numpy as jnp
        import numpy as np
        DIM = 512
        HEADS = 16
        HEAD_DIM = DIM // HEADS
        CHUNK = 128
        B, N = (4, 512)

        def _rmsnorm(x, w, eps):
            return x * jax.lax.rsqrt(jnp.mean(x * x, axis=-1, keepdims=True) + eps) * w

        def _weight_quant(w):
            scale = 1.0 / jnp.clip(jnp.mean(jnp.abs(w)), 1e-05, None)
            q = jnp.clip(jnp.round(w * scale), -1.0, 1.0) / scale
            return w + jax.lax.stop_gradient(q - w)

        def _forward(x, qkv_w, qkv_norm_w, proj_w, proj_norm_w, norm_w, s):
            Bb, Nn, C = x.shape
            H, D, T = (HEADS, HEAD_DIM, CHUNK)
            nc = Nn // T
            eps = jnp.finfo(x.dtype).eps
            scale = D ** (-0.5)
            h = _rmsnorm(x, qkv_norm_w, eps)
            qkv = h @ _weight_quant(qkv_w).T
            qkv = qkv.reshape(Bb, Nn, 3, H, D)
            q, k, v = (qkv[:, :, 0], qkv[:, :, 1], qkv[:, :, 2])

            def chunks(t):
                return t.reshape(Bb, nc, T, H, D).transpose(1, 0, 3, 2, 4)
            qc, kc, vc = (chunks(q), chunks(k), chunks(v))
            tt = jnp.arange(T, dtype=x.dtype)
            lam_t = jnp.exp(-s[:, None] * tt)
            lam_rev = jnp.exp(-s[:, None] * (T - tt))
            diff = tt[:, None] - tt[None, :]
            mask = jnp.where(diff >= 0, jnp.exp(-s[:, None, None] * diff), 0.0)
            lam_T = jnp.exp(-s * T)[:, None, None]

            def step(S, qkv_c):
                qi, ki, vi = qkv_c
                scores = jnp.einsum('bhtd,bhsd,hts->bhts', qi, ki, mask)
                intra = jnp.einsum('bhts,bhsd->bhtd', scores, vi)
                cross = jnp.einsum('bhtd,ht,bhde->bhte', qi, lam_t, S)
                o = scale * (intra + cross)
                kv = jnp.einsum('bhtd,ht,bhte->bhde', ki, lam_rev, vi)
                return (lam_T * S + kv, o)
            S0 = jnp.zeros((Bb, H, D, D), x.dtype)
            _, outs = jax.lax.scan(step, S0, (qc, kc, vc))
            out = outs.transpose(1, 0, 3, 2, 4).reshape(Bb, Nn, C)
            out = _rmsnorm(out, norm_w, 1e-06)
            out = _rmsnorm(out, proj_norm_w, eps) @ _weight_quant(proj_w).T
            return out
        key = jax.random.key(seed)
        ks = jax.random.split(key, 3)
        x = jax.random.normal(ks[0], (B, N, DIM), jnp.float32)
        bound = float(1.0 / np.sqrt(DIM))
        qkv_w = jax.random.uniform(ks[1], (3 * DIM, DIM), jnp.float32, -bound, bound)
        proj_w = jax.random.uniform(ks[2], (DIM, DIM), jnp.float32, -bound, bound)
        return {'x': x, 'qkv_w': qkv_w, 'qkv_norm_w': jnp.ones((DIM,), jnp.float32), 'proj_w': proj_w, 'proj_norm_w': jnp.ones((DIM,), jnp.float32), 'norm_w': jnp.ones((DIM,), jnp.float32), 's': jnp.full((HEADS,), 0.02, jnp.float32)}
    _L0_attn_in = _L0_attn_setup()

    def _L0_ffn_setup():
        import jax, jax.numpy as jnp
        import numpy as np
        H = 512
        E = 8
        TOPK = 2
        I_MOE = 256
        I_SH = 1024

        def _silu_and_mul(gu):
            g, u = jnp.split(gu, 2, axis=-1)
            return jax.nn.silu(g) * u
        key = jax.random.key(seed)
        ks = jax.random.split(key, 6)
        s = lambda *sh: 1.0 / np.sqrt(sh[-2])
        hidden_states = jax.random.normal(ks[0], (2, 256, H), dtype=jnp.float32)
        w_gate = jax.random.normal(ks[1], (H, E), dtype=jnp.float32) * (1.0 / np.sqrt(H))
        w_gate_up = jax.random.normal(ks[2], (E, H, 2 * I_MOE), dtype=jnp.float32) * (1.0 / np.sqrt(H))
        w_down = jax.random.normal(ks[3], (E, I_MOE, H), dtype=jnp.float32) * (1.0 / np.sqrt(I_MOE))
        w_sh_gate_up = jax.random.normal(ks[4], (H, 2 * I_SH), dtype=jnp.float32) * (1.0 / np.sqrt(H))
        w_sh_down = jax.random.normal(ks[5], (I_SH, H), dtype=jnp.float32) * (1.0 / np.sqrt(I_SH))
        return {'hidden_states': hidden_states, 'w_gate': w_gate, 'w_gate_up': w_gate_up, 'w_down': w_down, 'w_sh_gate_up': w_sh_gate_up, 'w_sh_down': w_sh_down}
    _L0_ffn_in = _L0_ffn_setup()
    _d = {'L0_attn_x': _L0_attn_in['x'], 'L0_attn_qkv_w': _L0_attn_in['qkv_w'], 'L0_attn_qkv_norm_w': _L0_attn_in['qkv_norm_w'], 'L0_attn_proj_w': _L0_attn_in['proj_w'], 'L0_attn_proj_norm_w': _L0_attn_in['proj_norm_w'], 'L0_attn_norm_w': _L0_attn_in['norm_w'], 'L0_attn_s': _L0_attn_in['s'], 'L0_ffn_w_gate': _L0_ffn_in['w_gate'], 'L0_ffn_w_gate_up': _L0_ffn_in['w_gate_up'], 'L0_ffn_w_down': _L0_ffn_in['w_down'], 'L0_ffn_w_sh_gate_up': _L0_ffn_in['w_sh_gate_up'], 'L0_ffn_w_sh_down': _L0_ffn_in['w_sh_down']}
    _x0 = _d['L0_attn_x']
    _d['L0_attn_x'] = jax.random.normal(jax.random.fold_in(jax.random.key(seed), 1), (2, 2048, 512), dtype=_x0.dtype)
    del _x0
    return _d

def reference(L0_attn_x, L0_attn_qkv_w, L0_attn_qkv_norm_w, L0_attn_proj_w, L0_attn_proj_norm_w, L0_attn_norm_w, L0_attn_s, L0_ffn_w_gate, L0_ffn_w_gate_up, L0_ffn_w_down, L0_ffn_w_sh_gate_up, L0_ffn_w_sh_down):

    def _L0_attn_ref(x, qkv_w, qkv_norm_w, proj_w, proj_norm_w, norm_w, s):
        import jax, jax.numpy as jnp
        import numpy as np
        DIM = 512
        HEADS = 16
        HEAD_DIM = DIM // HEADS
        CHUNK = 128
        B, N = (4, 512)

        def _rmsnorm(x, w, eps):
            return x * jax.lax.rsqrt(jnp.mean(x * x, axis=-1, keepdims=True) + eps) * w

        def _weight_quant(w):
            scale = 1.0 / jnp.clip(jnp.mean(jnp.abs(w)), 1e-05, None)
            q = jnp.clip(jnp.round(w * scale), -1.0, 1.0) / scale
            return w + jax.lax.stop_gradient(q - w)

        def _forward(x, qkv_w, qkv_norm_w, proj_w, proj_norm_w, norm_w, s):
            Bb, Nn, C = x.shape
            H, D, T = (HEADS, HEAD_DIM, CHUNK)
            nc = Nn // T
            eps = jnp.finfo(x.dtype).eps
            scale = D ** (-0.5)
            h = _rmsnorm(x, qkv_norm_w, eps)
            qkv = h @ _weight_quant(qkv_w).T
            qkv = qkv.reshape(Bb, Nn, 3, H, D)
            q, k, v = (qkv[:, :, 0], qkv[:, :, 1], qkv[:, :, 2])

            def chunks(t):
                return t.reshape(Bb, nc, T, H, D).transpose(1, 0, 3, 2, 4)
            qc, kc, vc = (chunks(q), chunks(k), chunks(v))
            tt = jnp.arange(T, dtype=x.dtype)
            lam_t = jnp.exp(-s[:, None] * tt)
            lam_rev = jnp.exp(-s[:, None] * (T - tt))
            diff = tt[:, None] - tt[None, :]
            mask = jnp.where(diff >= 0, jnp.exp(-s[:, None, None] * diff), 0.0)
            lam_T = jnp.exp(-s * T)[:, None, None]

            def step(S, qkv_c):
                qi, ki, vi = qkv_c
                scores = jnp.einsum('bhtd,bhsd,hts->bhts', qi, ki, mask)
                intra = jnp.einsum('bhts,bhsd->bhtd', scores, vi)
                cross = jnp.einsum('bhtd,ht,bhde->bhte', qi, lam_t, S)
                o = scale * (intra + cross)
                kv = jnp.einsum('bhtd,ht,bhte->bhde', ki, lam_rev, vi)
                return (lam_T * S + kv, o)
            S0 = jnp.zeros((Bb, H, D, D), x.dtype)
            _, outs = jax.lax.scan(step, S0, (qc, kc, vc))
            out = outs.transpose(1, 0, 3, 2, 4).reshape(Bb, Nn, C)
            out = _rmsnorm(out, norm_w, 1e-06)
            out = _rmsnorm(out, proj_norm_w, eps) @ _weight_quant(proj_w).T
            return out
        return _forward(x, qkv_w, qkv_norm_w, proj_w, proj_norm_w, norm_w, s)

    def _L0_ffn_ref(hidden_states, w_gate, w_gate_up, w_down, w_sh_gate_up, w_sh_down):
        import jax, jax.numpy as jnp
        import numpy as np
        H = 512
        E = 8
        TOPK = 2
        I_MOE = 256
        I_SH = 1024

        def _silu_and_mul(gu):
            g, u = jnp.split(gu, 2, axis=-1)
            return jax.nn.silu(g) * u
        orig_shape = hidden_states.shape
        x = hidden_states.reshape(-1, orig_shape[-1])
        router_logits = x @ w_gate
        probs = jax.nn.softmax(router_logits, axis=-1)
        topk_w, topk_ids = jax.lax.top_k(probs, TOPK)
        topk_w = topk_w / jnp.sum(topk_w, axis=-1, keepdims=True)
        combine = jnp.sum(topk_w[..., None] * jax.nn.one_hot(topk_ids, E, dtype=x.dtype), axis=1)
        gu = jnp.einsum('th,ehf->etf', x, w_gate_up)
        act = _silu_and_mul(gu)
        eo = jnp.einsum('eti,eih->eth', act, w_down)
        routed = jnp.einsum('te,eth->th', combine, eo)
        shared = _silu_and_mul(x @ w_sh_gate_up) @ w_sh_down
        return (routed + shared).reshape(orig_shape)
    x = L0_attn_x
    xn = _layernorm(x, axis=-1)
    x = x + _L0_attn_ref(xn, L0_attn_qkv_w, L0_attn_qkv_norm_w, L0_attn_proj_w, L0_attn_proj_norm_w, L0_attn_norm_w, L0_attn_s) + _L0_ffn_ref(xn, L0_ffn_w_gate, L0_ffn_w_gate_up, L0_ffn_w_down, L0_ffn_w_sh_gate_up, L0_ffn_w_sh_down)
    return x

_drawn_inputs = setup_inputs


def setup_inputs(seed=0):
    import zlib

    import numpy as np

    out = dict(_drawn_inputs(seed))
    spreads = {'L0_attn_qkv_norm_w': (1.0, 0.2),
     'L0_attn_proj_norm_w': (1.0, 0.2),
     'L0_attn_norm_w': (1.0, 0.2),
     'L0_attn_s': (0.019999999552965164, 0.2)}
    factors = {}
    for name, (base, spread) in spreads.items():
        noise = np.random.default_rng([zlib.crc32(name.encode()), seed]).standard_normal(out[name].shape)
        drawn = base * np.exp(spread * noise) if base else spread * noise
        out[name] = jnp.asarray(drawn.astype(out[name].dtype))
    for name, factor in factors.items():
        out[name] = (out[name] * factor).astype(out[name].dtype)
    return out
```

```python
from contextlib import ExitStack

import concourse.bass as bass
from concourse import mybir

ALU = mybir.AluOpType
ACT = mybir.ActivationFunctionType
AX = mybir.AxisListType
F32 = mybir.dt.float32
F16 = mybir.dt.float16
I32 = mybir.dt.int32

P = 128
DIM = 512
HEADS = 16
HD = DIM // HEADS
KT = DIM // P
HPT = P // HD
LN_EPS = 1e-5
F32_EPS = float(2.0 ** -23)
NORM_EPS = 1e-6
SCALE = float(HD) ** -0.5

X_SCALE = 2.0 ** 9
H_POW = 2.0 ** 9
W_POW = 2.0 ** 13

PASSES = ((0, 0), (0, 1), (1, 0))

EXPERTS = 8
TOPK = 2
FFN = 256
FT = FFN // P
R_MAX = bass.bass_isa.ReduceOp.max


def exponent_floor(eng, out, in_):
    return eng.tensor_single_scalar(out.bitcast(I32), in_.bitcast(I32), 0x7F800000, ALU.bitwise_and)


TOKENS = 4096
SLOT_TILES = (TOKENS * TOPK // P + EXPERTS - 1 + 1) // 2 * 2
AHEAD = 4


class Ring:

    FRONT = ["xnT0", "xnT1", "rt", "q0", "q1", "k0", "k1", "v0", "v1"]
    STEP = ["xnT0", "xnT1", "kTr0", "rt", "q0", "q1", "onT0", "kTr1", "k0", "proj0", "k1", "onT1",
            "v0", "v1", "proj1"]
    LAST = ["kTr0", "onT0", "kTr1", "proj0", "onT1", "proj1"]

    @classmethod
    def at(cls, name, step):
        if step is None:
            pos = cls.FRONT.index(name)
            return pos % 2, pos // 2
        q, par, last = step
        pos = len(cls.FRONT) + len(cls.STEP) * par + (cls.LAST if last else cls.STEP).index(name)
        return pos % 2, q * len(cls.STEP) + pos // 2

    @classmethod
    def before(cls, name, step):
        names = cls.FRONT if step is None else cls.LAST if step[2] else cls.STEP
        i = names.index(name) - 2
        if i < 0:
            return None if step is None else (("v1", 0), ("proj1", -1))[i + 2]
        return names[i], int(step is not None and names[i] in cls.FRONT)


def build(nc, x, qkv_w, qkv_nw, proj_w, proj_nw, norm_w, s, w_gate, w_gu, w_dn, w_sgu, w_sdn, out):
    B, N, C = x.shape
    NCH = N // P
    QKV = qkv_w.shape[0]
    E = w_gate.shape[1]
    QT = QKV // P
    x_steps = x.rearrange("b (n p) c -> n p b c", p=P)
    x1_dram = nc.dram_tensor("x1_dram", [B * N, C], F32, kind="Internal").ap()
    xn_dram = nc.dram_tensor("xn_dram", [B * N, C], F32, kind="Internal").ap()
    xT_dram = nc.dram_tensor("xT_dram", [NCH, P, KT, 2, B * P], F16, kind="Internal").ap()
    y_dram = nc.dram_tensor("y_dram", [SLOT_TILES * P, C], F32, kind="Internal").ap()
    slot_dram = nc.dram_tensor("slot_dram", [(SLOT_TILES + AHEAD) * P, 2], I32, kind="Internal").ap()
    out_steps = out.rearrange("b (n p) c -> n p b c", p=P)
    x1_steps = x1_dram.rearrange("(b n p) c -> n p b c", b=B, p=P)
    xn_steps = xn_dram.rearrange("(b n p) c -> n p b c", b=B, p=P)

    setup_ctx = ExitStack()
    with ExitStack() as kept:
        def sb(ctx, name, shape, dt=F32):
            return ctx.enter_context(nc.sbuf_tensor(name, shape, dt))

        setup_sems = []

        def sem(ctx, name):
            s_ = ctx.enter_context(nc.semaphore(name))
            if ctx is setup_ctx:
                setup_sems.append(s_)
            return s_

        ident = sb(kept, "ident", [P, P])
        ones = sb(kept, "ones", [P, P])
        logits = sb(kept, "logits", [P, B, NCH, E])
        wmax = sb(kept, "wmax", [P, 4, NCH])

        attn = ExitStack()
        qkvT = sb(attn, "qkvT", [P, KT, QKV], F16)
        projT = sb(attn, "projT", [P, KT, DIM], F16)
        wg16 = sb(attn, "wg16", [P, KT, 2, E], F16)
        ginv = sb(attn, "ginv", [P, 1])
        mask = sb(attn, "mask", [P, HEADS, P])
        lamq = sb(attn, "lamq", [P, KT, P])
        lamrev = sb(attn, "lamrev", [P, HEADS])
        lamT = sb(attn, "lamT", [P, KT])
        bmask = sb(attn, "bmask", [P, P])
        nw_b = sb(attn, "nw_b", [P, DIM])
        pnw_b = sb(attn, "pnw_b", [P, DIM])
        hw = sb(attn, "hw", [P, KT])
        alpha = sb(attn, "alpha", [P, 2])
        state = sb(attn, "state", [P, B, KT, P])

        with setup_ctx as c:
            wg = sb(c, "wg", [P, KT, E])
            wgs = sb(c, "wgs", [P, KT, E])
            gmax = sb(c, "gmax", [P, 1])
            wnat = sb(c, "wnat", [P, QT + KT, DIM])
            tern = sb(c, "tern", [P, QT + KT, DIM], F16)
            low = sb(c, "low", [P, QT + KT, DIM], F16)
            ident16 = sb(c, "ident16", [P, P], F16)
            s_b = sb(c, "s_b", [P, HEADS])
            s_p = sb(c, "s_p", [P, KT])
            nsb = sb(c, "nsb", [P, HEADS])
            nsp = sb(c, "nsp", [P, KT])
            diff = sb(c, "diff", [P, P])
            valid = sb(c, "valid", [P, P])
            col = sb(c, "col", [P, 1])
            trow = sb(c, "trow", [P, P])
            qnw_b = sb(c, "qnw_b", [P, DIM])
            qnw_c = sb(c, "qnw_c", [P, KT])
            asum = sb(c, "asum", [P, 2])
            mean = sb(c, "mean", [P, 2])
            quant = sb(c, "quant", [P, 2])
            dequant = sb(c, "dequant", [P, 2])
            nmax = sb(c, "nmax", [P, 4])
            nprod = sb(c, "nprod", [P, 3])
            nexp = sb(c, "nexp", [P, 3])
            nrec = sb(c, "nrec", [P, 3])
            scales = sb(c, "scales", [P, 3])
            iscales = sb(c, "iscales", [P, 2])
            rows = c.enter_context(nc.psum_tensor("rows", [P, 2, 1024], F16))
            tot = c.enter_context(nc.psum_tensor("tot", [P, 2], F32))

            in_small = sem(c, "in_small")
            in_qkv = sem(c, "in_qkv")
            in_proj = sem(c, "in_proj")
            pool_chain = sem(c, "pool_chain")
            ident_ready = sem(c, "ident_ready")
            id16_ready = sem(c, "id16_ready")
            iota_ready = sem(c, "iota_ready")
            sums_ready = sem(c, "sums_ready")
            tot_ready = sem(c, "tot_ready")
            dve = sem(c, "dve_chain")
            neg_ready = sem(c, "neg_ready")
            exp_ready = sem(c, "exp_ready")
            valid_ready = sem(c, "valid_ready")
            tern_ready = sem(c, "tern_ready")
            gmax_ready = sem(c, "gmax_ready")
            gall_ready = sem(c, "gall_ready")
            rows_full = sem(c, "rows_full")
            rows_free = [sem(c, f"rows_free{i}") for i in range(2)]
            TILES = QT + KT

            def turned(t):
                w, t = (qkvT, t) if t < QT else (projT, t - QT)
                return w[:, :, t * P:(t + 1) * P]

            block = c.enter_context(nc.Block())

            @block.sync
            def _(sp):
                sp.dma_start(wnat[:, 0:QT], qkv_w.rearrange("(n p) c -> p n c", p=P)).then_inc(in_qkv, 16)
                sp.dma_start(wnat[:, QT:], proj_w.rearrange("(n p) c -> p n c", p=P)).then_inc(in_proj, 16)

            SMALL = 16 * (1 + HPT + 5)

            @block.scalar
            def _(act):
                with nc.allow_non_contiguous_dma(reason="small vectors laid out as columns"):
                    act.dma_start(s_b[:], s.rearrange("(a h) -> a h", a=1).to_broadcast([P, HEADS])).then_inc(in_small, 16)
                    for h in range(HPT):
                        act.dma_start(s_p[HD * h:HD * h + HD, :],
                                      s.rearrange("(g j) -> j g", j=HPT)[h:h + 1, :].to_broadcast([HD, KT])
                                      ).then_inc(in_small, 16)
                    for dst, src in ((qnw_b, qkv_nw), (nw_b, norm_w), (pnw_b, proj_nw)):
                        act.dma_start(dst[:], src.rearrange("(a h) -> a h", a=1).to_broadcast([P, DIM])).then_inc(in_small, 16)
                    act.dma_start(qnw_c[:], qkv_nw.rearrange("(k p) -> p k", p=P)).then_inc(in_small, 16)
                    act.dma_start(wg[:], w_gate.rearrange("(k p) e -> p k e", p=P)).then_inc(in_small, 16)
                act.wait_ge(neg_ready, 1)
                act.wait_ge(iota_ready, 1)
                act.wait_ge(valid_ready, 1)
                for g in range(KT):
                    act.activation(lamq[:, g, :], trow[:], ACT.Exp, scale=nsp[:, g:g + 1])
                act.activation(lamT[:], nsp[:], ACT.Exp, scale=float(P))
                act.activation(lamrev[:], nsb[:], ACT.Exp, scale=col[:, 0:1])
                for i, h in enumerate(mask_heads()):
                    ins = act.activation(mask[:, i, :], diff[:], ACT.Exp, scale=nsb[:, h:h + 1])
                ins.then_inc(exp_ready, 1)
                act.wait_ge(in_qkv, 16)
                act.activation(low[:, 0:QT], wnat[:, 0:QT], ACT.Abs, accum_out=asum[:, 0:1]).then_inc(sums_ready, 1)
                act.wait_ge(in_proj, 16)
                act.activation(low[:, QT:], wnat[:, QT:], ACT.Abs, accum_out=asum[:, 1:2]).then_inc(sums_ready, 1)
                for t in range(1, TILES, 2):
                    act.wait_ge(rows_full, t + 1)
                    act.activation(turned(t), rows[:, 1, 0:DIM].rearrange("p (k c) -> p k c", k=KT), ACT.Copy
                                   ).then_inc(rows_free[1], 1)

            @block.gpsimd
            def _(pool):
                pool.memset(ident[:], 0.0)
                pool.memset(ident16[:], 0.0)
                pool.memset(ones[:], 1.0)
                pool.memset(state[:], 0.0).then_inc(pool_chain, 1)
                pool.wait_ge(pool_chain, 1)
                pool.affine_select(out=ident[:], in_=ident[:], compare_op=ALU.not_equal, fill=1.0, base=0,
                                   pattern=[[-1, P]], channel_multiplier=1)
                pool.affine_select(out=ident16[:], in_=ident16[:], compare_op=ALU.not_equal, fill=1.0, base=0,
                                   pattern=[[-1, P]], channel_multiplier=1).then_inc(ident_ready, 1)
                pool.iota(diff[:], [[1, P]], base=0, channel_multiplier=-1, allow_small_or_imprecise_dtypes=True)
                pool.iota(trow[:], [[1, P]], base=0, channel_multiplier=0, allow_small_or_imprecise_dtypes=True)
                pool.iota(col[:], [[0, 1]], base=P, channel_multiplier=-1, allow_small_or_imprecise_dtypes=True
                          ).then_inc(iota_ready, 1)
                pool.wait_ge(gmax_ready, 1)
                pool.partition_all_reduce(nmax[:, 3:4], gmax[:], P, R_MAX).then_inc(gall_ready, 1)

            @block.vector
            def _(v):
                steps = [0]

                def link(ins):
                    steps[0] += 1
                    ins.then_inc(dve, 1)
                    v.wait_ge(dve, steps[0])

                link(v.memset(bmask[:], 0.0))
                for h in range(HPT):
                    v.memset(bmask[HD * h:HD * h + HD, HD * h:HD * h + HD], 1.0)
                v.wait_ge(iota_ready, 1)
                link(v.tensor_scalar(valid[:], diff[:], 0.0, SCALE, ALU.is_ge, ALU.mult))
                v.tensor_scalar(diff[:], diff[:], 0.0, None, ALU.max).then_inc(valid_ready, 1)
                v.wait_ge(in_small, SMALL)
                v.tensor_scalar(nsb[:], s_b[:], -1.0, None, ALU.mult)
                v.tensor_scalar(nsp[:], s_p[:], -1.0, None, ALU.mult).then_inc(neg_ready, 1)
                v.tensor_reduce(gmax[:], wg[:], AX.XY, ALU.max, apply_absolute_value=True).then_inc(gmax_ready, 1)
                for i, t in enumerate((qnw_b, nw_b, pnw_b)):
                    ins = v.tensor_reduce(nmax[:, i:i + 1], t[:], AX.X, ALU.max, apply_absolute_value=True)
                link(ins)
                v.wait_ge(gall_ready, 1)
                link(v.tensor_scalar(nmax[:], nmax[:], 1e-12, None, ALU.max))
                v.tensor_copy(nprod[:, 0:1], nmax[:, 0:1])
                v.tensor_copy(nprod[:, 2:3], nmax[:, 3:4])
                link(v.tensor_tensor(nprod[:, 1:2], nmax[:, 1:2], nmax[:, 2:3], ALU.mult))
                link(exponent_floor(v, nexp[:], nprod[:]))
                link(v.reciprocal(nrec[:], nexp[:]))
                v.tensor_scalar(scales[:, 2:3], nrec[:, 2:3], W_POW, None, ALU.mult)
                link(v.tensor_scalar(scales[:, 0:2], nrec[:, 0:2], H_POW, None, ALU.mult))
                v.tensor_scalar(iscales[:], nexp[:, 0:2], 1.0 / H_POW, None, ALU.mult)
                v.tensor_scalar(ginv[:], nexp[:, 2:3], 1.0 / (W_POW * X_SCALE), None, ALU.mult)
                link(v.tensor_scalar(wgs[:], wg[:], scales[:, 2:3], None, ALU.mult))
                link(v.tensor_copy(wg16[:, :, 0], wgs[:]))
                v.tensor_tensor(wg16[:, :, 1], wgs[:], wg16[:, :, 0], ALU.subtract)
                v.tensor_scalar(hw[:], qnw_c[:], scales[:, 0:1], 1.0 / X_SCALE, ALU.mult, ALU.mult)
                v.tensor_scalar(pnw_b[:], pnw_b[:], scales[:, 1:2], None, ALU.mult)
                v.wait_ge(exp_ready, 1)
                v.tensor_scalar(lamq[:], lamq[:], SCALE, None, ALU.mult)
                v.tensor_tensor(mask[:], mask[:], valid[:, None, :].to_broadcast([P, HEADS, P]), ALU.mult)
                v.wait_ge(tot_ready, 1)
                v.tensor_scalar(mean[:, 0:1], tot[:, 0:1], 1.0 / (QKV * DIM), 1e-5, ALU.mult, ALU.max)
                link(v.tensor_scalar(mean[:, 1:2], tot[:, 1:2], 1.0 / (DIM * DIM), 1e-5, ALU.mult, ALU.max))
                link(v.reciprocal(quant[:], mean[:]))
                link(v.reciprocal(dequant[:], quant[:]))
                v.tensor_tensor(alpha[:], dequant[:], iscales[:], ALU.mult)
                for i, (a, b) in enumerate(((0, QT), (QT, TILES))):
                    w, q = wnat[:, a:b], quant[:, i:i + 1]
                    v.tensor_scalar(low[:, a:b], w, q, -0.5, ALU.mult, ALU.is_lt)
                    link(v.tensor_scalar(tern[:, a:b], w, q, 0.5, ALU.mult, ALU.is_gt))
                    v.tensor_tensor(tern[:, a:b], tern[:, a:b], low[:, a:b], ALU.subtract).then_inc(tern_ready, 1)
                for t in range(0, TILES, 2):
                    v.wait_ge(rows_full, t + 1)
                    v.tensor_copy(turned(t), rows[:, 0, 0:DIM].rearrange("p (k c) -> p k c", k=KT)
                                  ).then_inc(rows_free[0], 1)

            @block.tensor
            def _(pe):
                pe.wait_ge(ident_ready, 1)
                pe.wait_ge(sums_ready, 2)
                pe.matmul(tot[:], ones[:], asum[:], start=True, stop=True).then_inc(tot_ready, 1)
                for t in range(TILES):
                    pe.wait_ge(tern_ready, 1 if t < QT else 2)
                    if t >= 2:
                        pe.wait_ge(rows_free[t % 2], t // 2)
                    for k in range(KT):
                        ins = pe.transpose(rows[:, t % 2, k * P:(k + 1) * P], tern[:, t, k * P:(k + 1) * P], ident16[:])
                    ins.then_inc(rows_full, 1)

        attention(nc, attn, sb, sem, locals())
        attn.close()
        experts(nc, sb, sem, locals())


def wait_apart(eng, sem, value, passed):
    eng.wait_ge(sem, value)
    eng.sem_inc(passed, 1)


def mask_heads():
    return [HPT * (2 * (s // 2) + gg) + 2 * (s % 2) + jj for s in range(4) for jj in range(2) for gg in range(2)]


def attention(nc, ctx, sb, sem, k):
    ident, logits = k["ident"], k["logits"]
    qkvT, projT, wg16, ginv, mask, lamq, lamrev, lamT, bmask = (k[x] for x in "qkvT projT wg16 ginv mask lamq lamrev lamT bmask".split())
    nw_b, pnw_b, hw, alpha, state = (k[x] for x in "nw_b pnw_b hw alpha state".split())
    x_steps, x1_steps, xn_steps, NCH, B = k["x_steps"], k["x1_steps"], k["xn_steps"], k["NCH"], k["B"]
    wmax, xT_dram = k["wmax"], k["xT_dram"]
    flat = [w.rearrange(f"{d} -> ({d})").rearrange("(p f) -> p f", p=P)
            for w, d in ((k["w_gu"], "e k c"), (k["w_dn"], "e k c"), (k["w_sgu"], "k c"), (k["w_sdn"], "k c"))]
    PART = [w.shape[1] // NCH for w in flat]
    START = [sum(PART[:i]) for i in range(5)]
    assert B == 2 and NCH % 2 == 0 and KT == 4

    with ExitStack() as c:
        T2 = B * P
        xl = sb(c, "xl", [P, 2, B, DIM])
        xr = sb(c, "xr", [P, 2, B, DIM])
        xn = sb(c, "xn", [P, 2, B, DIM])
        xnT = sb(c, "xnT", [P, KT, T2])
        x16 = sb(c, "x16", [P, 2, KT, 2, T2], F16)
        wraw = sb(c, "wraw", [P, 2, START[4]])
        hh = sb(c, "hh", [P, KT, T2], F16)
        hl = sb(c, "hl", [P, KT, T2], F16)
        qT = sb(c, "qT", [P, 2, KT, T2])
        kT = sb(c, "kT", [P, 2, KT, T2])
        qlam = sb(c, "qlam", [P, 2, KT, T2])
        vt = sb(c, "vt", [P, 2, B, DIM])
        probs = sb(c, "probs", [P, 4, 4, P])
        kS = sb(c, "kS", [P, B, DIM])
        kvm = sb(c, "kvm", [P, B, KT, P])
        on = sb(c, "on", [P, B, DIM])
        on3 = sb(c, "on3", [P, B, DIM])
        yh = sb(c, "yh", [P, B, KT, P], F16)
        yl = sb(c, "yl", [P, B, KT, P], F16)
        x1 = sb(c, "x1", [P, B, DIM])
        junk = sb(c, "junk", [P, DIM])
        stats = sb(c, "stats", [P, B, 6])
        mv = sb(c, "mv", [P, 2, B, 2])
        ve = sb(c, "ve", [P, 2, B])
        sd = sb(c, "sd", [P, 2, B])
        rstd = sb(c, "rstd", [P, 2, B])
        rve = sb(c, "rve", [P, 2, B])
        hv = sb(c, "hv", [P, 2, B])
        hv2 = sb(c, "hv2", [P, 2, B])
        hsd = sb(c, "hsd", [P, 2, B])
        r = sb(c, "r", [P, 2, B])
        r2 = sb(c, "r2", [P, 2, B])
        r2m = sb(c, "r2m", [P, 2, B])
        kscale = sb(c, "kscale", [P, 2, B, HEADS])
        ss1 = sb(c, "ss1", [P, B])
        z1 = sb(c, "z1", [P, B])
        sq1 = sb(c, "sq1", [P, B])
        g1a = sb(c, "g1a", [P, B])
        g1 = sb(c, "g1", [P, B])
        ss2 = sb(c, "ss2", [P, B])
        z2 = sb(c, "z2", [P, B])
        sq2 = sb(c, "sq2", [P, B])
        g2a = sb(c, "g2a", [P, B])
        g2 = sb(c, "g2", [P, B])

        ring = [c.enter_context(nc.psum_tensor(f"ring{i}", [P, DIM], F32)) for i in range(2)]
        sc = c.enter_context(nc.psum_tensor("sc", [P, 4, DIM], F32))
        o_ps = c.enter_context(nc.psum_tensor("o_ps", [P, DIM], F32))
        kv_ps = c.enter_context(nc.psum_tensor("kv_ps", [P, DIM], F32))

        full = [sem(c, f"ring_full{i}") for i in range(2)]
        xl_in = [sem(c, f"xl_in{i}") for i in range(2)]
        xr_in = [sem(c, f"xr_in{i}") for i in range(2)]
        xn_out = [sem(c, f"xn_out{i}") for i in range(2)]
        x1_out = [sem(c, f"x1_out{i}") for i in range(2)]
        xT_out = [sem(c, f"xT_out{i}") for i in range(2)]
        wraw_in = [sem(c, f"wraw_in{i}") for i in range(2)]
        names = ("xhigh_ready xlow_ready wmax_ready stats_ready stats_seen mv_ready ve_ready sd_ready rstd_ready xn_ready rve_ready hv_ready hv2_ready hsd_ready "
                 "r_ready r2_ready kscale_ready xnT_ready hh_ready h_ready q_ready k_ready v_ready qlam_ready "
                 "o_full kv_full logits_ready kvm_ready kS_ready ss1_ready z1_ready sq1_ready g1a_ready "
                 "g1_ready on_ready ss2_ready z2_ready sq2_ready g2a_ready g2_ready on3_ready yh_ready yl_ready "
                 "x1_ready decayed")
        S = {n: sem(c, n) for n in names.split()}
        sc_full = [sem(c, f"sc_full{i}") for i in range(2)]
        sc_free = [sem(c, f"sc_free{i}") for i in range(2)]
        state_ready = [sem(c, f"state_ready{i}") for i in range(B)]

        block = c.enter_context(nc.Block())

        def run_steps(eng, prologue, step):
            prologue()
            with eng.Fori(0, NCH // 2 - 1) as q:
                step(q, 0, True, True)
                step(q, 1, True, True)
            step(NCH // 2 - 1, 0, True, False)
            step(NCH // 2 - 1, 1, False, False)

        def after(q, par):
            return (q, 1) if par == 0 else (q + 1, 0)

        READ = {"xnT": "xnT_ready", "rt": "logits_ready", "q": "q_ready", "k": "k_ready", "v": "v_ready",
                "kTr": "kS_ready", "onT": "yl_ready", "proj": "x1_ready"}

        def fill(pe, name, st):
            before = Ring.before(name, st)
            if before is not None:
                held, ahead = before
                n = ahead if st is None else 2 * st[0] + st[1] + ahead
                if held == "rt":
                    pe.wait_ge(S["logits_ready"], n + 1)
                else:
                    pe.wait_ge(S[READ[held[:-1]]], 2 * n + int(held[-1]) + 1)
            b, _ = Ring.at(name, st)
            return ring[b], full[b]

        def filled(eng, name, st):
            b, n = Ring.at(name, st)
            eng.wait_ge(full[b], n + 1)
            return ring[b]

        @block.sync
        def _(sp):
            def load_xl(q, par):
                n = 2 * q + par
                sp.dma_start(xl[:, par], x_steps[n] if isinstance(n, int) else x_steps[bass.ds(n, 1)][0]
                             ).then_inc(xl_in[par], 16)

            def load_xr(q, par):
                n = 2 * q + par
                sp.dma_start(xr[:, par], x_steps[n] if isinstance(n, int) else x_steps[bass.ds(n, 1)][0]
                             ).then_inc(xr_in[par], 16)

            def store_xn(q, par):
                n = 2 * q + par
                sp.wait_ge(S["xn_ready"], 2 * n + 2)
                sp.dma_start(xn_steps[n] if isinstance(n, int) else xn_steps[bass.ds(n, 1)][0], xn[:, par]
                             ).then_inc(xn_out[par], 16)

            def load_weights(q, par):
                n = 2 * q + par
                for w, size, a in zip(flat, PART, START):
                    sp.dma_start(wraw[:, par, a:a + size], w[:, bass.ds(n * size, size)]).then_inc(wraw_in[par], 16)

            def store_xT(q, par):
                n = 2 * q + par
                sp.wait_ge(S["xlow_ready"], n + 1)
                sp.dma_start(xT_dram[n] if isinstance(n, int) else xT_dram[bass.ds(n, 1)][0], x16[:, par]
                             ).then_inc(xT_out[par], 16)

            def prologue():
                for done_sem in k["setup_sems"]:
                    sp.sem_clear(done_sem)
                load_xl(0, 0)
                load_xl(0, 1)
                load_xr(0, 0)
                store_xn(0, 0)
                load_weights(0, 0)
                store_xT(0, 0)

            def step(q, par, front, norm):
                n = 2 * q + par
                if norm:
                    sp.wait_ge(S["xn_ready"], 2 * n + 2)
                    load_xl(q + 1, par)
                if front:
                    sp.wait_ge(S["x1_ready"], 2 * n)
                    load_xr(*after(q, par))
                    store_xn(*after(q, par))
                    sp.wait_ge(S["wmax_ready"], n)
                    load_weights(*after(q, par))
                for u in range(B):
                    if u == 1 and front:
                        store_xT(*after(q, par))
                    sp.wait_ge(S["x1_ready"], 2 * n + u + 1)
                    dst = x1_steps[n] if isinstance(n, int) else x1_steps[bass.ds(n, 1)][0]
                    sp.dma_start(dst[:, u], x1[:, u]).then_inc(x1_out[u], 16)

            run_steps(sp, prologue, step)
            for par in range(2):
                sp.wait_ge(xn_out[par], 16 * (NCH // 2))
                sp.wait_ge(x1_out[par], 16 * NCH)
                sp.wait_ge(xT_out[par], 16 * (NCH // 2))

        @block.tensor
        def _(pe):
            def xn_turn(i, q, par, st):
                n = 2 * q + par
                pe.wait_ge(S["xn_ready"], 2 * n + 2)
                bank, done = fill(pe, f"xnT{i}", st)
                for kk in range(2):
                    for u in range(B):
                        a = (2 * kk + u) * P
                        ins = pe.transpose(bank[:, a:a + P], xn[:, par, u, (2 * i + kk) * P:(2 * i + kk + 1) * P], ident[:])
                ins.then_inc(done, 1)

            def router(q, par, st):
                n = 2 * q + par
                pe.wait_ge(S["xlow_ready"], n + 1)
                bank, done = fill(pe, "rt", st)
                for u in range(B):
                    for kk in range(KT):
                        for i, (a, b) in enumerate(PASSES):
                            ins = pe.matmul(bank[:, u * EXPERTS:(u + 1) * EXPERTS], x16[:, par, kk, a, u * P:(u + 1) * P],
                                            wg16[:, kk, b, :], start=(kk == 0 and i == 0), stop=(kk == KT - 1 and i == 2))
                ins.then_inc(done, 1)

            def project(name, q, par, st):
                n = 2 * q + par
                pe.wait_ge(S["h_ready"], n + 1)
                bank, done = fill(pe, name, st)
                i = int(name[1])
                if name[0] == "v":
                    for kk in range(KT):
                        for h in (hh, hl):
                            ins = pe.matmul(bank[:], h[:, kk, i * P:(i + 1) * P], qkvT[:, kk, 2 * DIM:3 * DIM],
                                            start=(kk == 0 and h is hh), stop=(kk == KT - 1 and h is hl))
                else:
                    for g in range(2):
                        a = (0 if name[0] == "q" else DIM) + (2 * i + g) * P
                        for kk in range(KT):
                            for h in (hh, hl):
                                ins = pe.matmul(bank[:, g * T2:(g + 1) * T2], qkvT[:, kk, a:a + P], h[:, kk, :],
                                                start=(kk == 0 and h is hh), stop=(kk == KT - 1 and h is hl))
                ins.then_inc(done, 1)

            def scores(u, q, par):
                n = 2 * q + par
                if u == 0:
                    pe.wait_ge(S["q_ready"], 2 * n + 2)
                    pe.wait_ge(S["k_ready"], 2 * n + 2)
                for s in range(4):
                    pair = s % 2
                    pe.wait_ge(sc_free[pair], 4 * n + 2 * u + s // 2)
                    for gg in range(2):
                        for jj in range(2):
                            g, j = 2 * (s // 2) + gg, 2 * pair + jj
                            rows = slice(HD * j, HD * j + HD)
                            ins = pe.matmul(sc[:, j, gg * P:(gg + 1) * P],
                                            kT[rows, par, g, u * P:(u + 1) * P], qT[rows, par, g, u * P:(u + 1) * P],
                                            start=True, stop=True)
                    ins.then_inc(sc_full[pair], 1)

            def k_turn(u, q, par, st):
                bank, done = fill(pe, f"kTr{u}", st)
                for g in range(KT):
                    ins = pe.transpose(bank[:, g * P:(g + 1) * P], kT[:, par, g, u * P:(u + 1) * P], ident[:])
                ins.then_inc(done, 1)

            def outputs(u, q, par):
                n = 2 * q + par
                pe.wait_ge(S["on_ready"], 2 * n + u)
                pe.wait_ge(S["qlam_ready"], n + 1)
                pe.wait_ge(state_ready[u], n)
                pe.wait_ge(S["v_ready"], 2 * n + 2)
                for g in range(KT):
                    pe.matmul(o_ps[:, g * P:(g + 1) * P], qlam[:, par, g, u * P:(u + 1) * P], state[:, u, g, :],
                              start=(g == 0), stop=False, skip_group_check=True)
                heads = mask_heads()
                for s in range(4):
                    pe.wait_ge(sc_free[s % 2], 4 * n + 2 * u + s // 2 + 1)
                    for i in range(4):
                        h = heads[4 * s + i]
                        ins = pe.matmul(o_ps[:, HD * h:HD * h + HD], probs[:, s, i, :],
                                        vt[:, par, u, HD * h:HD * h + HD],
                                        start=False, stop=(s == 3 and i == 3), skip_group_check=True)
                ins.then_inc(S["o_full"], 1)

            def outer(u, q, par):
                n = 2 * q + par
                pe.wait_ge(S["kS_ready"], 2 * n + u + 1)
                pe.wait_ge(S["kvm_ready"], 2 * n + u)
                for g in range(KT):
                    ins = pe.matmul(kv_ps[:, g * P:(g + 1) * P], kS[:, u, g * P:(g + 1) * P],
                                    vt[:, par, u, g * P:(g + 1) * P], start=True, stop=True)
                ins.then_inc(S["kv_full"], 1)

            def o_turn(u, q, par, st):
                n = 2 * q + par
                pe.wait_ge(S["on3_ready"], 2 * n + u + 1)
                bank, done = fill(pe, f"onT{u}", st)
                for g in range(KT):
                    ins = pe.transpose(bank[:, g * P:(g + 1) * P], on3[:, u, g * P:(g + 1) * P], ident[:])
                ins.then_inc(done, 1)

            def proj(u, q, par, st):
                n = 2 * q + par
                pe.wait_ge(S["yl_ready"], 2 * n + u + 1)
                bank, done = fill(pe, f"proj{u}", st)
                for g in range(KT):
                    for y in (yh, yl):
                        ins = pe.matmul(bank[:], y[:, u, g, :], projT[:, g, :],
                                        start=(g == 0 and y is yh), stop=(g == KT - 1 and y is yl))
                ins.then_inc(done, 1)

            def prologue():
                xn_turn(0, 0, 0, None)
                xn_turn(1, 0, 0, None)
                router(0, 0, None)
                for name in ("q0", "q1", "k0", "k1", "v0", "v1"):
                    project(name, 0, 0, None)

            def step(q, par, front, norm):
                st = (q, par, not front)
                nxt = after(q, par)
                scores(0, q, par)
                if front:
                    xn_turn(0, *nxt, st)
                    xn_turn(1, *nxt, st)
                k_turn(0, q, par, st)
                outputs(0, q, par)
                outer(0, q, par)
                if front:
                    router(*nxt, st)
                    project("q0", *nxt, st)
                scores(1, q, par)
                if front:
                    project("q1", *nxt, st)
                o_turn(0, q, par, st)
                k_turn(1, q, par, st)
                outputs(1, q, par)
                if front:
                    project("k0", *nxt, st)
                outer(1, q, par)
                proj(0, q, par, st)
                if front:
                    project("k1", *nxt, st)
                o_turn(1, q, par, st)
                if front:
                    project("v0", *nxt, st)
                    project("v1", *nxt, st)
                proj(1, q, par, st)

            run_steps(pe, prologue, step)

        @block.scalar
        def _(act):
            def norm_roots(q, par):
                n = 2 * q + par
                act.wait_ge(S["ve_ready"], n + 1)
                act.activation(sd[:, par], ve[:, par], ACT.Sqrt).then_inc(S["sd_ready"], 1)
                act.wait_ge(S["hv2_ready"], n + 1)
                act.activation(hsd[:, par], hv2[:, par], ACT.Sqrt).then_inc(S["hsd_ready"], 1)

            def take_xnT(i, q, par, st):
                n = 2 * q + par
                if i == 0:
                    act.wait_ge(S["h_ready"], n)
                    act.wait_ge(S["xlow_ready"], n)
                bank = filled(act, f"xnT{i}", st)
                act.activation(xnT[:, 2 * i:2 * i + 2, :], bank[:].rearrange("p (k t) -> p k t", k=2), ACT.Copy,
                               scale=X_SCALE
                               ).then_inc(S["xnT_ready"], 1)

            def x_high(q, par):
                n = 2 * q + par
                act.wait_ge(S["xnT_ready"], 2 * n + 2)
                act.wait_ge(xT_out[par], 16 * q)
                act.activation(x16[:, par, :, 0], xnT[:], ACT.Copy).then_inc(S["xhigh_ready"], 1)

            def take(name, q, par, st):
                bank = filled(act, name, st)
                i, ready = int(name[1]), S[name[0] + "_ready"]
                if name[0] == "v":
                    act.activation(vt[:, par, i, :], bank[:], ACT.Copy, scale=alpha[:, 0:1]).then_inc(ready, 1)
                else:
                    dst = qT if name[0] == "q" else kT
                    act.activation(dst[:, par, 2 * i:2 * i + 2, :], bank[:].rearrange("p (k t) -> p k t", k=2),
                                   ACT.Copy, scale=alpha[:, 0:1]).then_inc(ready, 1)

            def o_squares(u, q, par):
                n = 2 * q + par
                act.wait_ge(S["o_full"], 2 * n + u + 1)
                act.activation(junk[:], o_ps[:], ACT.Square, accum_out=ss1[:, u:u + 1]).then_inc(S["ss1_ready"], 1)
                act.wait_ge(S["z1_ready"], 2 * n + u + 1)
                act.activation(sq1[:, u:u + 1], z1[:, u:u + 1], ACT.Sqrt).then_inc(S["sq1_ready"], 1)

            def on_squares(u, q, par):
                n = 2 * q + par
                act.wait_ge(S["on_ready"], 2 * n + u + 1)
                act.activation(junk[:], on[:, u], ACT.Square, accum_out=ss2[:, u:u + 1]).then_inc(S["ss2_ready"], 1)
                act.wait_ge(S["z2_ready"], 2 * n + u + 1)
                act.activation(sq2[:, u:u + 1], z2[:, u:u + 1], ACT.Sqrt).then_inc(S["sq2_ready"], 1)

            def y_high(u, q, par, st):
                bank = filled(act, f"onT{u}", st)
                act.activation(yh[:, u], bank[:].rearrange("p (k t) -> p k t", k=KT), ACT.Copy
                               ).then_inc(S["yh_ready"], 1)

            def prologue():
                norm_roots(0, 0)
                take_xnT(0, 0, 0, None)
                take_xnT(1, 0, 0, None)
                x_high(0, 0)
                norm_roots(0, 1)
                for name in ("q0", "q1", "k0", "k1", "v0", "v1"):
                    take(name, 0, 0, None)

            def step(q, par, front, norm):
                st = (q, par, not front)
                nxt = after(q, par)
                if front:
                    take_xnT(0, *nxt, st)
                    take_xnT(1, *nxt, st)
                    x_high(*nxt)
                o_squares(0, q, par)
                if front:
                    take("q0", *nxt, st)
                on_squares(0, q, par)
                if front:
                    take("q1", *nxt, st)
                y_high(0, q, par, st)
                if norm:
                    norm_roots(q + 1, par)
                o_squares(1, q, par)
                if front:
                    take("k0", *nxt, st)
                on_squares(1, q, par)
                if front:
                    take("k1", *nxt, st)
                y_high(1, q, par, st)
                if front:
                    take("v0", *nxt, st)
                    take("v1", *nxt, st)

            run_steps(act, prologue, step)

        @block.vector
        def _(v):
            def norm(q, par):
                n = 2 * q + par
                v.wait_ge(xl_in[par], 16 * (q + 1))
                v.bn_stats(stats[:, 0], xl[:, par, 0])
                v.bn_stats(stats[:, 1], xl[:, par, 1]).then_inc(S["stats_ready"], 1)
                v.wait_ge(S["stats_ready"], n + 1)
                v.sem_inc(S["stats_seen"], 1)
                v.bn_aggr(mv[:, par, 0], stats[:, 0])
                v.bn_aggr(mv[:, par, 1], stats[:, 1]).then_inc(S["mv_ready"], 1)
                v.wait_ge(S["mv_ready"], n + 1)
                var = mv[:, par, :, 1]
                v.tensor_scalar(ve[:, par], var, LN_EPS, None, ALU.add).then_inc(S["ve_ready"], 1)
                v.wait_ge(S["ve_ready"], n + 1)
                v.reciprocal(rve[:, par], ve[:, par]).then_inc(S["rve_ready"], 1)
                v.wait_ge(S["rve_ready"], n + 1)
                v.tensor_tensor(hv[:, par], var, rve[:, par], ALU.mult).then_inc(S["hv_ready"], 1)
                v.wait_ge(S["hv_ready"], n + 1)
                v.tensor_scalar(hv2[:, par], hv[:, par], F32_EPS, None, ALU.add).then_inc(S["hv2_ready"], 1)
                v.wait_ge(S["sd_ready"], n + 1)
                v.reciprocal(rstd[:, par], sd[:, par]).then_inc(S["rstd_ready"], 1)
                v.wait_ge(S["rstd_ready"], n + 1)
                v.wait_ge(xn_out[par], 16 * q)
                for u in range(B):
                    v.tensor_scalar(xn[:, par, u], xl[:, par, u], mv[:, par, u, 0:1], rstd[:, par, u:u + 1],
                                    ALU.subtract, ALU.mult).then_inc(S["xn_ready"], 1)

            def norm_factors(q, par):
                n = 2 * q + par
                v.wait_ge(S["hsd_ready"], n + 1)
                v.reciprocal(r[:, par], hsd[:, par]).then_inc(S["r_ready"], 1)
                v.wait_ge(S["r_ready"], n + 1)
                v.tensor_tensor(r2[:, par], r[:, par], r[:, par], ALU.mult).then_inc(S["r2_ready"], 1)
                v.wait_ge(S["r2_ready"], n + 1)
                v.tensor_scalar(r2m[:, par], r2[:, par], 1.0 / DIM, None, ALU.mult)
                for u in range(B):
                    ins = v.tensor_scalar(kscale[:, par, u], lamrev[:], r2[:, par, u:u + 1], None, ALU.mult)
                ins.then_inc(S["kscale_ready"], 1)

            def split_h(q, par):
                n = 2 * q + par
                v.wait_ge(S["xnT_ready"], 2 * n + 2)
                v.wait_ge(S["v_ready"], 2 * n)
                for kk in range(KT):
                    ins = v.tensor_scalar(hh[:, kk], xnT[:, kk], hw[:, kk:kk + 1], None, ALU.mult)
                ins.then_inc(S["hh_ready"], 1)
                v.wait_ge(S["hh_ready"], n + 1)
                for kk in range(KT):
                    ins = v.scalar_tensor_tensor(out=hl[:, kk], in0=xnT[:, kk], scalar=hw[:, kk:kk + 1], in1=hh[:, kk],
                                                 op0=ALU.mult, op1=ALU.subtract)
                ins.then_inc(S["h_ready"], 1)

            def take_logits(q, par, st):
                n = 2 * q + par
                bank = filled(v, "rt", st)
                dst = logits[:, :, n, :] if isinstance(n, int) else logits[:, :, bass.ds(n, 1), :][:, :, 0, :]
                v.tensor_scalar(dst, bank[:, 0:B * EXPERTS].rearrange("p (u e) -> p u e", u=B), ginv[:, 0:1], None, ALU.mult
                                ).then_inc(S["logits_ready"], 1)

            def weight_maxima(q, par):
                n = 2 * q + par
                v.wait_ge(wraw_in[par], 64 * (q + 1))
                for i in range(4):
                    ins = v.tensor_reduce(wmax[:, i, bass.ds(n, 1)], wraw[:, par, START[i]:START[i + 1]], AX.X, ALU.max,
                                          apply_absolute_value=True)
                ins.then_inc(S["wmax_ready"], 1)

            def decayed_scores(u, q, par):
                n = 2 * q + par
                v.wait_ge(S["kscale_ready"], n + 1)
                v.wait_ge(S["o_full"], 2 * n + u)
                for s in range(4):
                    pair = s % 2
                    v.wait_ge(sc_full[pair], 4 * n + 2 * u + s // 2 + 1)
                    v.scalar_tensor_tensor(out=probs[:, s].rearrange("p (j g) t -> p j (g t)", j=2),
                                           in0=sc[:, 2 * pair:2 * pair + 2, 0:2 * P],
                                           scalar=r2[:, par, u:u + 1],
                                           in1=mask[:, 4 * s:4 * s + 4].rearrange("p (j g) t -> p j (g t)", j=2),
                                           op0=ALU.mult, op1=ALU.mult).then_inc(sc_free[pair], 1)

            def scaled_k(u, q, par, st):
                bank = filled(v, f"kTr{u}", st)
                v.tensor_tensor(kS[:, u].rearrange("p (h d) -> p h d", d=HD),
                                bank[:].rearrange("p (h d) -> p h d", d=HD),
                                kscale[:, par, u, :, None].to_broadcast([P, HEADS, HD]), ALU.mult
                                ).then_inc(S["kS_ready"], 1)

            def masked_kv(u, q, par):
                n = 2 * q + par
                v.wait_ge(S["kv_full"], 2 * n + u + 1)
                v.wait_ge(state_ready[u], n)
                v.tensor_tensor(kvm[:, u], kv_ps[:].rearrange("p (g e) -> p g e", g=KT),
                                bmask[:, None, :].to_broadcast([P, KT, P]), ALU.mult).then_inc(S["kvm_ready"], 1)

            def normed(u, q, par):
                n = 2 * q + par
                c1 = slice(u, u + 1)
                m = 2 * n + u + 1
                v.wait_ge(S["ss1_ready"], m)
                v.tensor_scalar(z1[:, c1], ss1[:, c1], r2m[:, par, c1], NORM_EPS, ALU.mult, ALU.add
                                ).then_inc(S["z1_ready"], 1)
                v.wait_ge(S["sq1_ready"], m)
                v.reciprocal(g1a[:, c1], sq1[:, c1]).then_inc(S["g1a_ready"], 1)
                v.wait_ge(S["g1a_ready"], m)
                v.tensor_tensor(g1[:, c1], g1a[:, c1], r[:, par, c1], ALU.mult).then_inc(S["g1_ready"], 1)
                v.wait_ge(S["g1_ready"], m)
                v.scalar_tensor_tensor(out=on[:, u], in0=o_ps[:], scalar=g1[:, c1], in1=nw_b[:],
                                       op0=ALU.mult, op1=ALU.mult).then_inc(S["on_ready"], 1)

            def second_norm(u, q, par):
                n = 2 * q + par
                c1 = slice(u, u + 1)
                m = 2 * n + u + 1
                v.wait_ge(S["ss2_ready"], m)
                v.tensor_scalar(z2[:, c1], ss2[:, c1], 1.0 / DIM, F32_EPS, ALU.mult, ALU.add).then_inc(S["z2_ready"], 1)
                v.wait_ge(S["sq2_ready"], m)
                v.reciprocal(g2a[:, c1], sq2[:, c1]).then_inc(S["g2a_ready"], 1)
                v.wait_ge(S["g2a_ready"], m)
                v.tensor_tensor(g2[:, c1], g2a[:, c1], alpha[:, 1:2], ALU.mult).then_inc(S["g2_ready"], 1)

            def y_low(u, q, par, st):
                n = 2 * q + par
                v.wait_ge(S["yh_ready"], 2 * n + u + 1)
                bank = filled(v, f"onT{u}", st)
                v.tensor_tensor(yl[:, u], bank[:].rearrange("p (k t) -> p k t", k=KT), yh[:, u], ALU.subtract
                                ).then_inc(S["yl_ready"], 1)

            def residual(u, q, par, st):
                n = 2 * q + par
                c1 = slice(u, u + 1)
                bank = filled(v, f"proj{u}", st)
                v.wait_ge(S["g2_ready"], 2 * n + u + 1)
                v.wait_ge(xr_in[par], 16 * (q + 1))
                v.wait_ge(x1_out[u], 16 * n)
                v.scalar_tensor_tensor(out=x1[:, u], in0=bank[:], scalar=g2[:, c1], in1=xr[:, par, u],
                                       op0=ALU.mult, op1=ALU.add).then_inc(S["x1_ready"], 1)

            def prologue():
                norm(0, 0)
                norm_factors(0, 0)
                split_h(0, 0)
                take_logits(0, 0, None)
                norm(0, 1)
                norm_factors(0, 1)

            def step(q, par, front, has_norm):
                st = (q, par, not front)
                nxt = after(q, par)
                decayed_scores(0, q, par)
                scaled_k(0, q, par, st)
                if front:
                    split_h(*nxt)
                weight_maxima(q, par)
                masked_kv(0, q, par)
                normed(0, q, par)
                if front:
                    take_logits(*nxt, st)
                decayed_scores(1, q, par)
                second_norm(0, q, par)
                y_low(0, q, par, st)
                scaled_k(1, q, par, st)
                if has_norm:
                    norm(q + 1, par)
                masked_kv(1, q, par)
                normed(1, q, par)
                residual(0, q, par, st)
                second_norm(1, q, par)
                if has_norm:
                    norm_factors(q + 1, par)
                y_low(1, q, par, st)
                residual(1, q, par, st)

            run_steps(v, prologue, step)

        @block.gpsimd
        def _(pool):
            def x_low(q, par):
                n = 2 * q + par
                pool.wait_ge(S["xhigh_ready"], n + 1)
                pool.tensor_tensor(x16[:, par, :, 1], xnT[:], x16[:, par, :, 0], ALU.subtract
                                   ).then_inc(S["xlow_ready"], 1)

            def decayed_q(q, par):
                n = 2 * q + par
                pool.wait_ge(S["q_ready"], 2 * n + 2)
                pool.tensor_tensor(qlam[:, par].rearrange("p g (u t) -> p g u t", u=B),
                                   qT[:, par].rearrange("p g (u t) -> p g u t", u=B),
                                   lamq[:, :, None, :].to_broadcast([P, KT, B, P]), ALU.mult
                                   ).then_inc(S["qlam_ready"], 1)

            def update(u, q, par):
                n = 2 * q + par
                pool.wait_ge(S["kvm_ready"], 2 * n + u + 1)
                pool.tensor_tensor(state[:, u], state[:, u], lamT[:, :, None].to_broadcast([P, KT, P]), ALU.mult
                                   ).then_inc(S["decayed"], 1)
                pool.wait_ge(S["decayed"], 2 * n + u + 1)
                pool.tensor_tensor(state[:, u], state[:, u], kvm[:, u], ALU.add).then_inc(state_ready[u], 1)

            def weighted(u, q, par):
                n = 2 * q + par
                pool.wait_ge(S["on_ready"], 2 * n + u + 1)
                pool.tensor_tensor(on3[:, u], on[:, u], pnw_b[:], ALU.mult).then_inc(S["on3_ready"], 1)

            def prologue():
                x_low(0, 0)
                decayed_q(0, 0)

            def step(q, par, front, norm):
                if front:
                    x_low(*after(q, par))
                update(0, q, par)
                weighted(0, q, par)
                if front:
                    decayed_q(*after(q, par))
                update(1, q, par)
                weighted(1, q, par)

            run_steps(pool, prologue, step)


def experts(nc, sb, sem, k):
    ident, ones, logits, wmax = k["ident"], k["ones"], k["logits"], k["wmax"]
    x1_steps, out_steps, xT_dram, xn_dram, y_dram, slot_dram = (
        k[x] for x in "x1_steps out_steps xT_dram xn_dram y_dram slot_dram".split())
    w_gu, w_dn, w_sgu, w_sdn, NCH, B = (k[x] for x in "w_gu w_dn w_sgu w_sdn NCH B".split())
    GROUPS = w_sdn.shape[0] // FFN
    HALF = NCH // 2
    TT = B * NCH
    UNITS = SLOT_TILES + AHEAD
    PIECES = KT + FT
    sgu = w_sgu.rearrange("(k p) (h g c) -> g h p k c", p=P, h=2, g=GROUPS)
    sdn = w_sdn.rearrange("(g f p) c -> g p f c", p=P, f=FT)
    rgu = w_gu.rearrange("e (k p) c -> e p k c", p=P)
    rdn = w_dn.rearrange("e (f p) c -> e p f c", p=P)

    with ExitStack() as c:
        WG = sb(c, "WG", [P, GROUPS + EXPERTS, KT, 2, 2 * FFN], F16)
        WD = sb(c, "WD", [P, GROUPS + EXPERTS, FT, 2, DIM], F16)
        posi = sb(c, "posi", [P, TOPK, TT], I32)
        slots = sb(c, "slots", [P, UNITS, 2], I32)
        unit_e = sb(c, "unit_e", [P, UNITS], I32)
        wtop = sb(c, "wtop", [P, 4])
        wall = sb(c, "wall", [P, 4])
        wexp = sb(c, "wexp", [P, 4])
        wrec = sb(c, "wrec", [P, 4])
        wscale = sb(c, "wscale", [P, 4])
        esq = sb(c, "esq", [P, 2])
        gate_inv = sb(c, "gate_inv", [P, 2])
        up_inv = sb(c, "up_inv", [P, 2])
        out_inv = sb(c, "out_inv", [P, 2])

        with ExitStack() as cc:
            chain = sem(cc, "scale_chain")
            top_ready = sem(cc, "top_ready")
            all_ready = sem(cc, "all_ready")
            with nc.Block() as block:
                @block.gpsimd
                def _(pool):
                    pool.wait_ge(top_ready, 1)
                    pool.partition_all_reduce(wall[:], wtop[:], P, R_MAX).then_inc(all_ready, 1)

                @block.vector
                def _(v):
                    steps = [0]

                    def link(ins):
                        steps[0] += 1
                        ins.then_inc(chain, 1)
                        v.wait_ge(chain, steps[0])

                    v.tensor_reduce(wtop[:], wmax[:], AX.X, ALU.max).then_inc(top_ready, 1)
                    v.wait_ge(all_ready, 1)
                    link(v.tensor_scalar(wall[:], wall[:], 1e-12, None, ALU.max))
                    link(exponent_floor(v, wexp[:], wall[:]))
                    link(v.reciprocal(wrec[:], wexp[:]))
                    v.tensor_scalar(wscale[:], wrec[:], W_POW, None, ALU.mult)
                    gu, dn = wexp[:].rearrange("p (s m) -> p m s", s=2)[:, 0], wexp[:].rearrange("p (s m) -> p m s", s=2)[:, 1]
                    v.tensor_scalar(gate_inv[:], gu, 1.0 / (W_POW * X_SCALE), None, ALU.mult)
                    v.tensor_scalar(up_inv[:], wrec[:].rearrange("p (s m) -> p m s", s=2)[:, 0],
                                    2.0 ** -5 / (W_POW * X_SCALE), None, ALU.mult)
                    link(v.tensor_tensor(esq[:], gu, gu, ALU.mult))
                    v.scalar_tensor_tensor(out=out_inv[:], in0=esq[:], scalar=2.0 ** 5 / W_POW, in1=dn,
                                           op0=ALU.mult, op1=ALU.mult)

        def gate_up(pe, gu, x, w, tokens):
            for h in range(2):
                for f in range(FT):
                    a0 = h * FFN + f * P
                    for kk in range(KT):
                        for a, b in PASSES:
                            ins = pe.matmul(gu[:, h, f * tokens:(f + 1) * tokens],
                                            w[:, kk, b, a0:a0 + P],
                                            x[:, kk, a], start=(kk == 0 and (a, b) == PASSES[0]),
                                            stop=(kk == KT - 1 and (a, b) == PASSES[-1]))
            return ins

        def gate_up_rows(pe, gu, bank, x, w, parts):
            done = [(kk, a, b) for kk in range(KT) for a, b in PASSES]
            for i in parts:
                kk, a, b = done[i]
                ins = pe.matmul(gu[bank][:], x(kk, a), w[:, 0, kk, b, :],
                                start=(i == 0), stop=(i == len(done) - 1))
            return ins

        def down(pe, y, act_hl, w, first, last):
            for f in range(FT):
                for a, b in PASSES:
                    ins = pe.matmul(y[:], act_hl[a][:, f, :], w[:, f, b, :] if len(w.shape) == 4 else w[:, 0, f, b, :],
                                    start=(first and f == 0 and (a, b) == PASSES[0]),
                                    stop=(last and f == FT - 1 and (a, b) == PASSES[-1]))
            return ins

        FIRST, REST = range(0, 6), range(6, 3 * KT)

        def shared(half):
            n0 = half * HALF
            with ExitStack() as c:
                xT = sb(c, f"xT_{half}", [P, 2, KT, 2, B * P], F16)
                x1 = sb(c, f"x1s_{half}", [P, 2, B, DIM])
                sg = sb(c, f"sg_{half}", [P, 2, FT, B * P])
                actv = sb(c, f"actv_{half}", [P, 2, FT, B * P])
                ah = sb(c, f"ah_{half}", [P, 2, FT, B * P], F16)
                al = sb(c, f"al_{half}", [P, 2, FT, B * P], F16)
                ys = sb(c, f"ys_{half}", [P, B, DIM])
                gu = [c.enter_context(nc.psum_tensor(f"gu{i}_{half}", [P, 2, FT * B * P], F32)) for i in range(2)]
                yp = [c.enter_context(nc.psum_tensor(f"yp{i}_{half}", [P, DIM], F32)) for i in range(2)]
                names = "gu_full act_ready sg_ready ah_ready al_ready y_full y_read sp_passed pool_passed"
                S = {x: sem(c, x) for x in names.split()}
                x_in = [sem(c, f"x_in{i}") for i in range(2)]
                y_out = [sem(c, f"y_out{i}") for i in range(B)]
                if half == 0:
                    raw = sb(c, f"raw_{half}", [P, 2, PIECES, DIM])
                    raw_in = [sem(c, f"raw_in{i}") for i in range(2)]
                    high = sem(c, "high")
                    split = sem(c, "split")
                    room = WG[:, GROUPS + EXPERTS - 5:].rearrange("p g k s c -> p (g k s c)").bitcast(F32)
                    R, used_room = {}, 0
                    for x, shape in dict(
                            beats=[TT, EXPERTS, EXPERTS], ties=[TT, EXPERTS, EXPERTS], mx=[TT], shifted=[TT, EXPERTS],
                            pexp=[TT, EXPERTS], psum_=[TT], prec=[TT], prob=[TT, EXPERTS], rank=[TT, EXPERTS],
                            chosen=[TOPK, TT, EXPERTS], sel=[TT, EXPERTS], wsel=[TT, EXPERTS], wsum=[TT], wrecip=[TT],
                            comb=[TT, EXPERTS], cumA=[TT, EXPERTS], cumB=[TT, EXPERTS], tots=[TT, EXPERTS],
                            used=[EXPERTS, TT], tiles=[EXPERTS], lower=[EXPERTS, EXPERTS], before=[EXPERTS, EXPERTS],
                            base=[EXPERTS], ends=[EXPERTS], pos=[TT, EXPERTS], posk=[TOPK, TT], unitf=[UNITS],
                            steps128=[TT], unit_no=[UNITS], earlier=[P]).items():
                        size = 1
                        for d in shape:
                            size *= d
                        names_ = "abc"[:len(shape)]
                        flat_ = room[:, used_room:used_room + size]
                        R[x] = flat_ if len(shape) == 1 else flat_.rearrange(
                            f"p ({' '.join(names_)}) -> p {' '.join(names_)}", **dict(zip(names_[1:], shape[1:])))
                        used_room += size
                    over = room[:, 0:2 * TT * EXPERTS * EXPERTS]
                    R["picked"] = over[:, 0:TOPK * TT * EXPERTS].rearrange("p (k t e) -> p k t e", k=TOPK, t=TT)
                    R["pickedc"] = over[:, TOPK * TT * EXPERTS:2 * TOPK * TT * EXPERTS].rearrange(
                        "p (k t e) -> p k t e", k=TOPK, t=TT)
                    R["passed"] = over[:, 2 * TOPK * TT * EXPERTS:2 * TOPK * TT * EXPERTS + UNITS * EXPERTS].rearrange(
                        "p (n e) -> p n e", e=EXPERTS)
                    payload = sb(c, f"payload_{half}", [P, TOPK, TT, 2], I32)
                    blank = sb(c, f"blank_{half}", [P, UNITS * 2], I32)
                    rp = c.enter_context(nc.psum_tensor("rp", [P, 2, TT * EXPERTS], F32))
                    rc = sem(c, "routing_chain")
                    const_ready = sem(c, "const_ready")
                    const_chain = sem(c, "const_chain")
                    shifted_ready = sem(c, "shifted_ready")
                    pexp_ready = sem(c, "pexp_ready")
                    sel_ready = sem(c, "sel_ready")
                    counts_ready = sem(c, "counts_ready")
                    payload_ready = sem(c, "payload_ready")
                    blank_out = sem(c, "blank_out")
                    slot_out = sem(c, "slot_out")
                    slot_in = sem(c, "slot_in")
                else:
                    gidx = sb(c, f"gidx_{half}", [P, B, 2 * TOPK], I32)
                    gy = sb(c, f"gy_{half}", [P, B, 2 * TOPK, DIM])
                    x1o = sb(c, f"x1o_{half}", [P, 2, B, DIM])
                    yo = sb(c, f"yo_{half}", [P, B, DIM])
                    S |= {x: sem(c, x) for x in "gidx_ready ysum_ready own_ready oldsum_ready old_ready".split()}
                    gy_in = [sem(c, f"gy_in{i}") for i in range(B)]
                    xo_in = [sem(c, f"xo_in{i}") for i in range(2)]
                    yo_out = [sem(c, f"yo_out{i}") for i in range(B)]

                def run_steps(eng, step):
                    step(0, 0, True, False)
                    step(0, 1, False, False)
                    with eng.Fori(1, HALF // 2 - 1) as q:
                        step(q, 0, False, False)
                        step(q, 1, False, False)
                    step(HALF // 2 - 1, 0, False, False)
                    step(HALF // 2 - 1, 1, False, True)

                def unit(q, par, g):
                    return GROUPS * (2 * q + par) + g

                def pieces(g):
                    more = PIECES - GROUPS
                    return range(g + min(g, more), g + 1 + min(g + 1, more))

                def at_step(a, n):
                    return a[n] if isinstance(n, int) else a[bass.ds(n, 1)][0]

                block = c.enter_context(nc.Block())

                @block.sync
                def _(sp):
                    def load(q, par):
                        n = 2 * q + par
                        sp.dma_start(xT[:, par], at_step(xT_dram, n + n0)).then_inc(x_in[par], 16)
                        sp.dma_start(x1[:, par], at_step(x1_steps, n + n0)).then_inc(x_in[par], 16)
                        if half == 1:
                            sp.dma_start(x1o[:, par], at_step(x1_steps, n)).then_inc(xo_in[par], 16)

                    def raw_shared(g):
                        b = g % 2
                        if g >= 2:
                            sp.wait_ge(split, PIECES * (g - 1))
                        for h in range(2):
                            sp.dma_start(raw[:, b, 0:KT, h * FFN:(h + 1) * FFN], sgu[g, h]).then_inc(raw_in[b], 16)
                        sp.dma_start(raw[:, b, KT:], sdn[g]).then_inc(raw_in[b], 16)

                    def raw_routed(q, par):
                        e = 2 * q + par
                        wait_apart(sp, split, PIECES * (e + GROUPS - 1), S["sp_passed"])
                        sp.dma_start(raw[:, par, 0:KT], at_step(rgu, e)).then_inc(raw_in[par], 16)
                        sp.dma_start(raw[:, par, KT:], at_step(rdn, e)).then_inc(raw_in[par], 16)
                        sp.sem_inc(raw_in[par], 16)

                    load(0, 0)
                    if half == 0:
                        for g in range(GROUPS):
                            raw_shared(g)

                    def step(q, par, first, last):
                        n = 2 * q + par
                        if half == 0:
                            raw_routed(q, par)
                        if not last:
                            q1, p1 = (q, 1) if par == 0 else (q + 1, 0)
                            if not first:
                                sp.wait_ge(S["y_read"], B * n)
                                if half == 1:
                                    sp.wait_ge(S["old_ready"], B * n)
                            load(q1, p1)
                        if first and half == 0:
                            sp.wait_ge(const_ready, 1)
                            sp.dma_start(slot_dram.rearrange("(p a) b -> p (a b)", p=P), blank[:]).then_inc(blank_out, 16)
                        for u in range(B):
                            if half == 0:
                                sp.wait_ge(S["y_read"], B * n + u + 1)
                                dst = at_step(x1_steps, n + n0)
                            else:
                                sp.wait_ge(S["own_ready"], B * n + u + 1)
                                dst = at_step(out_steps, n + n0)
                            sp.dma_start(dst[:, u], ys[:, u]).then_inc(y_out[u], 16)
                            if half == 1:
                                sp.wait_ge(S["old_ready"], B * n + u + 1)
                                sp.dma_start(at_step(out_steps, n)[:, u], yo[:, u]).then_inc(yo_out[u], 16)

                    run_steps(sp, step)
                    if half == 0:
                        sp.wait_ge(slot_out, 16 * TOPK * TT)
                        sp.dma_start(slots[:], slot_dram.rearrange("(a p) b -> p a b", p=P)).then_inc(slot_in, 16)
                        sp.wait_ge(slot_in, 16)
                    for u in range(B):
                        sp.wait_ge(y_out[u], 16 * HALF)
                        if half == 1:
                            sp.wait_ge(yo_out[u], 16 * HALF)

                @block.tensor
                def _(pe):
                    if half == 0:
                        pe.wait_ge(split, PIECES)
                    pe.wait_ge(x_in[0], 32)
                    gate_up(pe, gu[0], xT[:, 0], WG[:, 0], B * P).then_inc(S["gu_full"], 1)

                    def step(q, par, first, last):
                        n = 2 * q + par
                        for g in range(GROUPS):
                            i = unit(q, par, g)
                            if not (last and g == GROUPS - 1):
                                g1 = (g + 1) % GROUPS
                                q1, p1 = (q, par) if g1 else (q, 1) if par == 0 else (q + 1, 0)
                                if g1 == 0:
                                    pe.wait_ge(x_in[p1], 32 * (q1 + 1))
                                elif half == 0 and first:
                                    pe.wait_ge(split, PIECES * (g1 + 1))
                                if not (first and g == 0):
                                    pe.wait_ge(S["act_ready"], i)
                                gate_up(pe, gu[g1 % 2], xT[:, p1], WG[:, g1], B * P).then_inc(S["gu_full"], 1)
                            pe.wait_ge(S["al_ready"], i + 1)
                            for u in range(B):
                                if g == 0 and not first:
                                    pe.wait_ge(S["y_read"], B * (n - 1) + u + 1)
                                rows = slice(u * P, (u + 1) * P)
                                ins = down(pe, yp[u], (ah[:, g % 2, :, rows], al[:, g % 2, :, rows]), WD[:, g],
                                           g == 0, g == GROUPS - 1)
                                if g == GROUPS - 1:
                                    ins.then_inc(S["y_full"], 1)
                            if half == 0 and first and g == 0:
                                pe.wait_ge(sel_ready, 1)
                                pe.wait_ge(const_ready, 1)
                                flat = R["sel"].rearrange("p t e -> p (t e)")
                                pe.matmul(rp[:, 0, :], R["earlier"], flat, start=True, stop=True)
                                pe.matmul(rp[:, 1, :], ones[:], flat, start=True, stop=True).then_inc(counts_ready, 1)

                    run_steps(pe, step)

                @block.scalar
                def _(act):
                    def high_part(place, b, i, gu_scale, dn_scale):
                        dst = WG[:, place, i, 0, :] if i < KT else WD[:, place, i - KT, 0, :]
                        act.activation(dst, raw[:, b, i], ACT.Copy, scale=gu_scale if i < KT else dn_scale).then_inc(high, 1)

                    def high_routed(q, par, i):
                        e = 2 * q + par
                        place = e + GROUPS
                        if i == 0:
                            act.wait_ge(raw_in[par], 48 * (q + 1 + GROUPS // 2))
                        if isinstance(e, int):
                            high_part(place, par, i, wscale[:, 0:1], wscale[:, 1:2])
                            return
                        dst = WG[:, bass.ds(place, 1), i, 0, :] if i < KT else WD[:, bass.ds(place, 1), i - KT, 0, :]
                        act.activation(dst, raw[:, par:par + 1, i], ACT.Copy,
                                       scale=wscale[:, 0:1] if i < KT else wscale[:, 1:2]).then_inc(high, 1)

                    if half == 0:
                        act.wait_ge(shifted_ready, 1)
                        act.activation(R["pexp"], R["shifted"], ACT.Exp).then_inc(pexp_ready, 1)
                        for g in range(GROUPS):
                            act.wait_ge(raw_in[g % 2], 48 * (g // 2 + 1))
                            for i in range(PIECES):
                                high_part(g, g % 2, i, wscale[:, 2:3], wscale[:, 3:4])

                    def step(q, par, first, last):
                        for g in range(GROUPS):
                            i = unit(q, par, g)
                            act.wait_ge(S["gu_full"], i + 1)
                            act.activation(sg[:, g % 2], gu[g % 2][:, 0].rearrange("p (f t) -> p f t", f=FT), ACT.Silu,
                                           scale=gate_inv[:, 1:2]).then_inc(S["sg_ready"], 1)
                            act.wait_ge(S["act_ready"], i + 1)
                            act.activation(ah[:, g % 2], actv[:, g % 2], ACT.Copy).then_inc(S["ah_ready"], 1)
                            if half == 0:
                                for piece in pieces(g):
                                    high_routed(q, par, piece)

                    run_steps(act, step)

                @block.vector
                def _(v):
                    steps = [0]

                    def link(ins):
                        steps[0] += 1
                        ins.then_inc(rc, 1)
                        v.wait_ge(rc, steps[0])

                    def low_part(place, b, i, gu_scale, dn_scale):
                        w = WG[:, place, i] if i < KT else WD[:, place, i - KT]
                        v.scalar_tensor_tensor(out=w[:, 1, :], in0=raw[:, b, i], scalar=gu_scale if i < KT else dn_scale,
                                               in1=w[:, 0, :], op0=ALU.mult, op1=ALU.subtract).then_inc(split, 1)

                    def low_routed(q, par, i):
                        e = 2 * q + par
                        v.wait_ge(high, PIECES * (e + GROUPS) + i + 1)
                        if isinstance(e, int):
                            low_part(e + GROUPS, par, i, wscale[:, 0:1], wscale[:, 1:2])
                            return
                        at_e = bass.ds(e + GROUPS, 1)
                        w = (WG[:, at_e, i, :, :] if i < KT else WD[:, at_e, i - KT, :, :])
                        v.scalar_tensor_tensor(out=w[:, 0, 1, :], in0=raw[:, par, i],
                                               scalar=wscale[:, 0:1] if i < KT else wscale[:, 1:2],
                                               in1=w[:, 0, 0, :], op0=ALU.mult, op1=ALU.subtract).then_inc(split, 1)

                    lg = logits[:].rearrange("p u n e -> p (u n) e")

                    def probabilities():
                        v.wait_ge(pexp_ready, 1)
                        link(v.tensor_reduce(R["psum_"], R["pexp"], AX.X, ALU.add))
                        link(v.reciprocal(R["prec"], R["psum_"]))
                        link(v.tensor_tensor(R["prob"], R["pexp"], R["prec"][:, :, None].to_broadcast([P, TT, EXPERTS]),
                                             ALU.mult))

                    def ranks():
                        of, by = R["prob"][:, :, :, None], R["prob"][:, :, None, :]
                        full = [P, TT, EXPERTS, EXPERTS]
                        v.wait_ge(const_ready, 1)
                        v.tensor_tensor(R["beats"], by.to_broadcast(full), of.to_broadcast(full), ALU.is_gt)
                        link(v.tensor_tensor(R["ties"], by.to_broadcast(full), of.to_broadcast(full), ALU.is_equal))
                        link(v.tensor_tensor(R["ties"], R["ties"], R["lower"][:, None].to_broadcast(full), ALU.mult))
                        link(v.tensor_tensor(R["beats"], R["beats"], R["ties"], ALU.add))
                        link(v.tensor_reduce(R["rank"], R["beats"], AX.X, ALU.add))
                        for i in range(TOPK):
                            v.tensor_scalar(R["chosen"][:, i], R["rank"], float(i), None, ALU.is_equal)
                        v.tensor_scalar(R["sel"], R["rank"], float(TOPK), None, ALU.is_lt).then_inc(sel_ready, 1)
                        v.wait_ge(sel_ready, 1)

                    def combine_weights():
                        link(v.tensor_tensor(R["wsel"], R["sel"], R["prob"], ALU.mult))
                        link(v.tensor_reduce(R["wsum"], R["wsel"], AX.X, ALU.add))
                        link(v.reciprocal(R["wrecip"], R["wsum"]))
                        link(v.tensor_tensor(R["comb"], R["wsel"], R["wrecip"][:, :, None].to_broadcast([P, TT, EXPERTS]),
                                             ALU.mult))

                    def positions():
                        v.wait_ge(counts_ready, 1)
                        link(v.tensor_copy(R["tots"], rp[:, 1, :].rearrange("p (t e) -> p t e", e=EXPERTS)))
                        a, b, d = R["tots"], R["cumA"], 1
                        while d < TT:
                            v.tensor_copy(b[:, 0:d], a[:, 0:d])
                            link(v.tensor_tensor(b[:, d:], a[:, d:], a[:, 0:TT - d], ALU.add))
                            a, b, d = b, (R["cumB"] if b is R["cumA"] else R["cumA"]), 2 * d
                        v_counts = a[:, TT - 1]
                        link(v.tensor_tensor(R["used"], v_counts[:, :, None].to_broadcast([P, EXPERTS, TT]),
                                             R["steps128"][:, None, :].to_broadcast([P, EXPERTS, TT]), ALU.is_gt))
                        link(v.tensor_reduce(R["tiles"], R["used"], AX.X, ALU.add))
                        link(v.tensor_tensor(R["before"], R["lower"],
                                             R["tiles"][:, None, :].to_broadcast([P, EXPERTS, EXPERTS]), ALU.mult))
                        link(v.tensor_reduce(R["base"], R["before"], AX.X, ALU.add))
                        v.tensor_tensor(R["ends"], R["base"], R["tiles"], ALU.add)
                        link(v.tensor_tensor(R["pos"], a[:], R["tots"], ALU.subtract))
                        link(v.tensor_tensor(R["pos"], R["pos"], rp[:, 0, :].rearrange("p (t e) -> p t e", e=EXPERTS),
                                             ALU.add))
                        link(v.tensor_scalar(R["base"], R["base"], float(P), None, ALU.mult))
                        link(v.tensor_tensor(R["pos"], R["pos"], R["base"][:, None, :].to_broadcast([P, TT, EXPERTS]),
                                             ALU.add))

                    def send():
                        whole = [P, TOPK, TT, EXPERTS]
                        v.tensor_tensor(R["picked"], R["chosen"], R["pos"][:, None].to_broadcast(whole), ALU.mult)
                        link(v.tensor_tensor(R["pickedc"], R["chosen"], R["comb"][:, None].to_broadcast(whole), ALU.mult))
                        v.tensor_reduce(payload[:].bitcast(F32)[:, :, :, 1], R["pickedc"], AX.X, ALU.add)
                        link(v.tensor_reduce(R["posk"], R["picked"], AX.X, ALU.add))
                        v.tensor_copy(posi[:], R["posk"]).then_inc(payload_ready, 1)

                    def unit_experts():
                        full = [P, UNITS, EXPERTS]
                        link(v.tensor_tensor(R["passed"], R["ends"][:, None, :].to_broadcast(full),
                                             R["unit_no"][:, :, None].to_broadcast(full), ALU.is_le))
                        link(v.tensor_reduce(R["unitf"], R["passed"], AX.X, ALU.add))
                        v.tensor_scalar(unit_e[:], R["unitf"], float(EXPERTS - 1), float(GROUPS), ALU.min, ALU.add)

                    if half == 0:
                        link(v.tensor_reduce(R["mx"], lg, AX.X, ALU.max))
                        v.tensor_tensor(R["shifted"], lg, R["mx"][:, :, None].to_broadcast([P, TT, EXPERTS]), ALU.subtract
                                        ).then_inc(shifted_ready, 1)
                        for g in range(GROUPS):
                            for i in range(PIECES):
                                v.wait_ge(high, PIECES * g + i + 1)
                                low_part(g, g % 2, i, wscale[:, 2:3], wscale[:, 3:4])
                            if g == 1:
                                probabilities()
                                ranks()

                    def token_outputs(q, par):
                        n = 2 * q + par
                        for u in range(B):
                            v.wait_ge(S["y_full"], B * n + u + 1)
                            v.wait_ge(x_in[par], 32 * (q + 1))
                            v.wait_ge(y_out[u], 16 * n)
                            v.scalar_tensor_tensor(out=ys[:, u], in0=yp[u][:], scalar=out_inv[:, 1:2], in1=x1[:, par, u],
                                                   op0=ALU.mult, op1=ALU.add).then_inc(S["y_read"], 1)
                        if half == 1:
                            for u in range(B):
                                v.wait_ge(S["y_read"], B * n + u + 1)
                                v.wait_ge(gy_in[u], 64 * (n + 1))
                                v.tensor_tensor(ys[:, u], ys[:, u], gy[:, u, 0], ALU.add).then_inc(S["ysum_ready"], 1)
                                v.wait_ge(S["ysum_ready"], B * n + u + 1)
                                v.tensor_tensor(ys[:, u], ys[:, u], gy[:, u, 1], ALU.add).then_inc(S["own_ready"], 1)

                    def gather_places(q, par, u):
                        n = 2 * q + par
                        v.wait_ge(gy_in[u], 64 * n)
                        for i, m in enumerate((n + n0, n)):
                            col = posi[:].rearrange("p k (u n) -> p k u n", u=B)[:, :, u, bass.ds(m, 1)]
                            ins = v.tensor_copy(gidx[:, u, TOPK * i:TOPK * (i + 1)], col[:, :, 0])
                        ins.then_inc(S["gidx_ready"], 1)

                    def step(q, par, first, last):
                        if half == 1:
                            for u in range(B):
                                gather_places(q, par, u)
                        for g in range(GROUPS):
                            i = unit(q, par, g)
                            v.wait_ge(S["sg_ready"], i + 1)
                            v.scalar_tensor_tensor(out=actv[:, g % 2],
                                                   in0=gu[g % 2][:, 1].rearrange("p (f t) -> p f t", f=FT),
                                                   scalar=up_inv[:, 1:2], in1=sg[:, g % 2],
                                                   op0=ALU.mult, op1=ALU.mult).then_inc(S["act_ready"], 1)
                            v.wait_ge(S["ah_ready"], i + 1)
                            v.tensor_tensor(al[:, g % 2], actv[:, g % 2], ah[:, g % 2], ALU.subtract
                                            ).then_inc(S["al_ready"], 1)
                            if g == 0 and not first:
                                token_outputs(*((q, 0) if par == 1 else (q - 1, 1)))
                            if half == 0:
                                for piece in pieces(g):
                                    low_routed(q, par, piece)
                            if half == 0 and first:
                                (combine_weights, positions, send, unit_experts)[g]()
                        if last:
                            token_outputs(q, par)

                    run_steps(v, step)

                @block.gpsimd
                def _(pool):
                    if half == 0:
                        pool.memset(R["earlier"], 1.0)
                        pool.memset(R["lower"], 1.0)
                        pool.memset(blank[:], 0).then_inc(const_chain, 1)
                        pool.wait_ge(const_chain, 1)
                        pool.affine_select(out=R["earlier"], in_=R["earlier"], compare_op=ALU.is_gt, fill=0.0, base=0,
                                           pattern=[[1, P]], channel_multiplier=-1)
                        pool.affine_select(out=R["lower"], in_=R["lower"], compare_op=ALU.is_gt, fill=0.0, base=0,
                                           pattern=[[1, EXPERTS], [-1, EXPERTS]], channel_multiplier=0)
                        pool.iota(R["steps128"], [[P, TT]], base=0, channel_multiplier=0,
                                  allow_small_or_imprecise_dtypes=True)
                        pool.iota(R["unit_no"], [[1, UNITS]], base=0, channel_multiplier=0,
                                  allow_small_or_imprecise_dtypes=True)
                        pool.iota(payload[:, :, :, 0], [[0, TOPK], [NCH * P, B], [P, NCH]], base=0, channel_multiplier=1
                                  ).then_inc(const_ready, 1)
                        pool.wait_ge(payload_ready, 1)
                        pool.wait_ge(blank_out, 16)
                        for kk in range(TOPK):
                            for t in range(TT):
                                pool.indirect_dma_start(
                                    out=slot_dram, out_offset=bass.IndirectOffsetOnAxis(ap=posi[:, kk, t:t + 1], axis=0),
                                    in_=payload[:, kk, t, :], in_offset=None).then_inc(slot_out, 16)
                        return

                    def step(q, par, first, last):
                        n = 2 * q + par
                        for u in range(B):
                            if not first:
                                pool.wait_ge(S["own_ready"], B * (n - 1) + u + 1)
                                pool.wait_ge(S["old_ready"], B * (n - 1) + u + 1)
                            wait_apart(pool, S["gidx_ready"], B * n + u + 1, S["pool_passed"])
                            for i in range(2 * TOPK):
                                pool.indirect_dma_start(
                                    out=gy[:, u, i], out_offset=None, in_=y_dram,
                                    in_offset=bass.IndirectOffsetOnAxis(ap=gidx[:, u, i:i + 1], axis=0)).then_inc(gy_in[u], 16)
                        for u in range(B):
                            pool.wait_ge(gy_in[u], 64 * (n + 1))
                            pool.wait_ge(xo_in[par], 16 * (q + 1))
                            pool.wait_ge(yo_out[u], 16 * n)
                            pool.tensor_tensor(yo[:, u], x1o[:, par, u], gy[:, u, 2], ALU.add).then_inc(S["oldsum_ready"], 1)
                            pool.wait_ge(S["oldsum_ready"], B * n + u + 1)
                            pool.tensor_tensor(yo[:, u], yo[:, u], gy[:, u, 3], ALU.add).then_inc(S["old_ready"], 1)

                    run_steps(pool, step)

        def routed():
            with ExitStack() as c:
                idx = sb(c, "idx", [P, 2, 1], I32)
                cw = sb(c, "cw", [P, 2])
                xg = sb(c, "xg", [P, 2, DIM])
                xh = sb(c, "xh", [P, 2, 2, KT, P], F16)
                sg = sb(c, "sgr", [P, 2, FFN])
                actv = sb(c, "actvr", [P, 2, FFN])
                ah = sb(c, "ahr", [P, 2, FT, P], F16)
                al = sb(c, "alr", [P, 2, FT, P], F16)
                ysb = sb(c, "ysb", [P, 2, DIM])
                gu = [c.enter_context(nc.psum_tensor(f"rgu{i}", [P, 2 * FFN], F32)) for i in range(2)]
                at = [c.enter_context(nc.psum_tensor(f"rat{i}", [P, FT, P], F32)) for i in range(2)]
                yp = [c.enter_context(nc.psum_tensor(f"ryp{i}", [P, DIM], F32)) for i in range(2)]
                xt = c.enter_context(nc.psum_tensor("xt", [P, KT, P], F32))
                names = "gu_full act_ready sg_ready at_full ah_ready al_ready y_full y_ready xt_full xh_ready xl_ready idx_ready cw_ready pool_passed"
                S = {x: sem(c, "r_" + x) for x in names.split()}
                xg_in = [sem(c, f"xg_in{i}") for i in range(2)]
                y_out = [sem(c, f"ry_out{i}") for i in range(2)]
                block = c.enter_context(nc.Block())

                def run_steps(eng, step):
                    step(0, 0, True)
                    step(0, 1, False)
                    with eng.Fori(1, SLOT_TILES // 2) as q:
                        step(q, 0, False)
                        step(q, 1, False)

                @block.sync
                def _(sp):
                    rows = y_dram.rearrange("(r p) c -> r p c", p=P)

                    def step(q, par, first):
                        r = 2 * q + par
                        sp.wait_ge(S["y_ready"], r + 1)
                        sp.dma_start(rows[r] if isinstance(r, int) else rows[bass.ds(r, 1)][0], ysb[:, par]
                                     ).then_inc(y_out[par], 16)

                    run_steps(sp, step)
                    for par in range(2):
                        sp.wait_ge(y_out[par], 16 * (SLOT_TILES // 2))

                @block.gpsimd
                def _(pool):
                    def gather(q, par):
                        r = 2 * q + par
                        wait_apart(pool, S["idx_ready"], r + 1, S["pool_passed"])
                        pool.indirect_dma_start(out=xg[:, par], out_offset=None, in_=xn_dram,
                                                in_offset=bass.IndirectOffsetOnAxis(ap=idx[:, par, 0:1], axis=0)
                                                ).then_inc(xg_in[par], 16)

                    gather(0, 0)
                    gather(0, 1)
                    for par in range(2):
                        pool.wait_ge(S["xt_full"], par + 1)
                        gather(1, par)

                    def step(q, par, first):
                        pool.wait_ge(S["xt_full"], 2 * q + par + 3)
                        gather(q + 2, par)

                    run_steps(pool, step)
                    for par in range(2):
                        pool.wait_ge(xg_in[par], 16 * (SLOT_TILES // 2 + 2))

                @block.tensor
                def _(pe):
                    def turn(q, par):
                        pe.wait_ge(xg_in[par], 16 * (q + 1))
                        pe.wait_ge(S["xl_ready"], 2 * q + par)
                        for kk in range(KT):
                            ins = pe.transpose(xt[:, kk, :], xg[:, par, kk * P:(kk + 1) * P], ident[:])
                        ins.then_inc(S["xt_full"], 1)

                    def xs(par):
                        return lambda kk, a: xh[:, par, a, kk, :]

                    def place(r):
                        e = pe.value_load(unit_e[0:1, bass.ds(r, 1)], min_val=GROUPS, max_val=GROUPS + EXPERTS - 1)
                        return bass.ds(e, 1)

                    turn(0, 0)
                    turn(0, 1)
                    pe.wait_ge(S["xl_ready"], 1)
                    gate_up_rows(pe, gu, 0, xs(0), WG[:, place(0)], range(3 * KT)).then_inc(S["gu_full"], 1)

                    def tile(q, par, first, own, nxt):
                        r = 2 * q + par
                        pe.wait_ge(S["xl_ready"], r + 2)
                        if not first:
                            pe.wait_ge(S["act_ready"], r)
                        gate_up_rows(pe, gu, 1 - par, xs(1 - par), WG[:, nxt], FIRST)
                        pe.wait_ge(S["act_ready"], r + 1)
                        for f in range(FT):
                            ins = pe.transpose(at[par][:, f, :], actv[:, par, f * P:(f + 1) * P], ident[:])
                        ins.then_inc(S["at_full"], 1)
                        turn(q + 1, par)
                        gate_up_rows(pe, gu, 1 - par, xs(1 - par), WG[:, nxt], REST).then_inc(S["gu_full"], 1)
                        if par == 0:
                            after_next = place(r + 2)
                        if not first:
                            pe.wait_ge(S["y_ready"], r - 1)
                        pe.wait_ge(S["al_ready"], r + 1)
                        down(pe, yp[par], (ah[:, par], al[:, par]), WD[:, own], True, True).then_inc(S["y_full"], 1)
                        return after_next if par == 0 else None

                    def pair(q, first):
                        even, odd = place(2 * q), place(2 * q + 1)
                        tile(q, 1, False, odd, tile(q, 0, first, even, odd))

                    pair(0, True)
                    with pe.Fori(1, SLOT_TILES // 2) as q:
                        pair(q, False)

                @block.scalar
                def _(act):
                    def x_high(q, par):
                        r = 2 * q + par
                        act.wait_ge(S["xt_full"], r + 1)
                        act.activation(xh[:, par, 0], xt[:], ACT.Copy, scale=X_SCALE).then_inc(S["xh_ready"], 1)

                    def y_evac(q, par):
                        r = 2 * q + par
                        act.wait_ge(S["y_full"], r + 1)
                        act.wait_ge(y_out[par], 16 * q)
                        act.activation(ysb[:, par], yp[par][:], ACT.Copy, scale=out_inv[:, 0:1]).then_inc(S["y_ready"], 1)

                    x_high(0, 0)
                    x_high(0, 1)

                    def step(q, par, first):
                        r = 2 * q + par
                        act.wait_ge(S["gu_full"], r + 1)
                        act.activation(sg[:, par], gu[par][:, 0:FFN], ACT.Silu, scale=gate_inv[:, 0:1]
                                       ).then_inc(S["sg_ready"], 1)
                        if not first:
                            y_evac(*((q, 0) if par == 1 else (q - 1, 1)))
                        act.wait_ge(S["at_full"], r + 1)
                        act.activation(ah[:, par], at[par][:], ACT.Copy).then_inc(S["ah_ready"], 1)
                        x_high(q + 1, par)

                    run_steps(act, step)
                    y_evac(SLOT_TILES // 2 - 1, 1)

                @block.vector
                def _(v):
                    def index(q, par):
                        r = 2 * q + par
                        v.tensor_copy(idx[:, par], slots[:, bass.ds(r, 1), 0]).then_inc(S["idx_ready"], 1)

                    def weight(q, par):
                        r = 2 * q + par
                        v.tensor_scalar(cw[:, par:par + 1], slots[:].bitcast(F32)[:, bass.ds(r, 1), 1], up_inv[:, 0:1], None,
                                        ALU.mult).then_inc(S["cw_ready"], 1)

                    def x_low(q, par):
                        r = 2 * q + par
                        v.wait_ge(S["xh_ready"], r + 1)
                        v.scalar_tensor_tensor(out=xh[:, par, 1], in0=xt[:], scalar=X_SCALE, in1=xh[:, par, 0],
                                               op0=ALU.mult, op1=ALU.subtract).then_inc(S["xl_ready"], 1)

                    index(0, 0)
                    index(0, 1)
                    weight(0, 0)
                    weight(0, 1)
                    for par in range(2):
                        v.wait_ge(xg_in[par], 16)
                        index(1, par)
                        x_low(0, par)

                    def step(q, par, first):
                        r = 2 * q + par
                        v.wait_ge(S["cw_ready"], r + 1)
                        v.wait_ge(S["sg_ready"], r + 1)
                        v.scalar_tensor_tensor(out=actv[:, par], in0=gu[par][:, FFN:2 * FFN], scalar=cw[:, par:par + 1],
                                               in1=sg[:, par], op0=ALU.mult, op1=ALU.mult).then_inc(S["act_ready"], 1)
                        v.wait_ge(S["ah_ready"], r + 1)
                        v.tensor_tensor(al[:, par], at[par][:], ah[:, par], ALU.subtract).then_inc(S["al_ready"], 1)
                        x_low(q + 1, par)
                        v.wait_ge(S["act_ready"], r + 1)
                        weight(q + 1, par)
                        v.wait_ge(xg_in[par], 16 * (q + 2))
                        index(q + 2, par)

                    run_steps(v, step)

        shared(0)
        routed()
        shared(1)


_INS = ["L0_attn_x", "L0_attn_qkv_w", "L0_attn_qkv_norm_w", "L0_attn_proj_w", "L0_attn_proj_norm_w",
        "L0_attn_norm_w", "L0_attn_s", "L0_ffn_w_gate", "L0_ffn_w_gate_up", "L0_ffn_w_down",
        "L0_ffn_w_sh_gate_up", "L0_ffn_w_sh_down"]


def kernel(**inputs):
    import numpy as _np
    import concourse.bacc as _bacc
    from concourse.bass_utils import run_bass_kernel_spmd as _run

    nc = _bacc.Bacc("TRN2", target_bir_lowering=False, num_devices=1)
    arrays, args = {}, []
    for name in _INS:
        a = _np.ascontiguousarray(inputs[name])
        arrays[f"in_{name}"] = a
        args.append(nc.dram_tensor(f"in_{name}", a.shape, mybir.dt.from_np(a.dtype), kind="ExternalInput").ap())
    shape = inputs["L0_attn_x"].shape
    out = nc.dram_tensor("out_0", shape, F32, kind="ExternalOutput").ap()
    build(nc, *args, out)
    r = _run(nc, [arrays], core_ids=[0])
    return r.results[0]["out_0"]
```

```python
from contextlib import ExitStack

import concourse.bass as bass
from concourse import mybir

ALU = mybir.AluOpType
ACT = mybir.ActivationFunctionType
AX = mybir.AxisListType
F32 = mybir.dt.float32
F16 = mybir.dt.float16
I32 = mybir.dt.int32

P = 128
DIM = 512
HEADS = 16
HD = DIM // HEADS
KT = DIM // P
HPT = P // HD
LN_EPS = 1e-5
F32_EPS = float(2.0 ** -23)
NORM_EPS = 1e-6
SCALE = float(HD) ** -0.5

X_SCALE = 2.0 ** 9
H_POW = 2.0 ** 9
W_POW = 2.0 ** 13

Q_SCALE = 2.0 ** -5
P_SCALE = 2.0 ** -18
Q_POW = 2.0 ** 5 * 2.0 ** 6

PASSES = ((0, 0), (0, 1), (1, 0))

EXPERTS = 8
TOPK = 2
FFN = 256
FT = FFN // P
PIECES = KT + FT
R_MAX = bass.bass_isa.ReduceOp.max


def exponent_floor(eng, out, in_):
    return eng.tensor_single_scalar(out.bitcast(I32), in_.bitcast(I32), 0x7F800000, ALU.bitwise_and)


TOKENS = 4096
SLOT_TILES = (TOKENS * TOPK // P + EXPERTS - 1 + 1) // 2 * 2
AHEAD = 4


class Ring:

    BANKS = 3
    FRONT = ["xnT0", "xnT1", "q0", "q1", "rt", "k0", "k1", "v0", "v1"]
    STEP = ["xnT0", "xnT1", "kTr0", "kv0", "q0", "q1", "kTr1", "rt", "onT0", "k0", "kv1", "k1", "proj0", "onT1",
            "v0", "v1", None, "proj1"]
    LAST = ["kTr0", "kv0", "kTr1", "onT0", "kv1", "proj0", "onT1", "proj1"]

    @classmethod
    def at(cls, name, step):
        def fills(names, bank):
            return sum(i % cls.BANKS == bank for i, n in enumerate(names) if n is not None)

        if step is None:
            i = cls.FRONT.index(name)
            return i % cls.BANKS, fills(cls.FRONT[:i], i % cls.BANKS)
        q, par, last = step
        i = (cls.LAST if last else cls.STEP).index(name)
        bank = i % cls.BANKS
        here = (cls.LAST if last else cls.STEP)[:i]
        return bank, (q * 2 * fills(cls.STEP, bank) + fills(cls.FRONT, bank) + par * fills(cls.STEP, bank)
                      + fills(here, bank))

    @classmethod
    def before(cls, name, step):
        names = cls.FRONT if step is None else cls.LAST if step[2] else cls.STEP
        i = names.index(name) - cls.BANKS
        if i < 0:
            return None if step is None else (("v1", 0), ("onT1", -1), ("proj1", -1))[i + cls.BANKS]
        return names[i], int(step is not None and names[i] in cls.FRONT)


def build(nc, x, qkv_w, qkv_nw, proj_w, proj_nw, norm_w, s, w_gate, w_gu, w_dn, w_sgu, w_sdn, out):
    B, N, C = x.shape
    NCH = N // P
    QKV = qkv_w.shape[0]
    E = w_gate.shape[1]
    QT = QKV // P
    x_steps = x.rearrange("b (n p) c -> n p b c", p=P)
    x1_dram = nc.dram_tensor("x1_dram", [B * N, C], F32, kind="Internal").ap()
    xn_dram = nc.dram_tensor("xn_dram", [B * N, C], F32, kind="Internal").ap()
    xT_dram = nc.dram_tensor("xT_dram", [NCH, P, KT, 2, B * P], F16, kind="Internal").ap()
    y_dram = nc.dram_tensor("y_dram", [SLOT_TILES * P, C], F32, kind="Internal").ap()
    slot_dram = nc.dram_tensor("slot_dram", [(SLOT_TILES + AHEAD) * P, 2], I32, kind="Internal").ap()
    out_steps = out.rearrange("b (n p) c -> n p b c", p=P)
    x1_steps = x1_dram.rearrange("(b n p) c -> n p b c", b=B, p=P)
    xn_steps = xn_dram.rearrange("(b n p) c -> n p b c", b=B, p=P)

    sgu = w_sgu.rearrange("(k p) (h g c) -> g h p k c", p=P, h=2, c=FFN)
    sdn = w_sdn.rearrange("(g f p) c -> g p f c", p=P, f=FT)

    setup_ctx = ExitStack()
    with ExitStack() as kept:
        def sb(ctx, name, shape, dt=F32):
            return ctx.enter_context(nc.sbuf_tensor(name, shape, dt))

        setup_sems = []

        def sem(ctx, name):
            s_ = ctx.enter_context(nc.semaphore(name))
            if ctx is setup_ctx:
                setup_sems.append(s_)
            return s_

        ident = sb(kept, "ident", [P, P])
        ones = sb(kept, "ones", [P, P])
        logits = sb(kept, "logits", [P, B, NCH, E])
        wmax = sb(kept, "wmax", [P, 4, NCH])
        wtop = sb(kept, "wtop", [P, 4])
        wall = sb(kept, "wall", [P, 4])
        wexp = sb(kept, "wexp", [P, 4])
        wrec = sb(kept, "wrec", [P, 4])
        wscale = sb(kept, "wscale", [P, 4])
        esq = sb(kept, "esq", [P, 2])
        gate_inv = sb(kept, "gate_inv", [P, 2])
        up_inv = sb(kept, "up_inv", [P, 2])
        out_inv = sb(kept, "out_inv", [P, 2])
        raw = sb(kept, "raw", [P, 2, PIECES, DIM])
        raw_in = [sem(kept, f"raw_in{i}") for i in range(2)]

        attn = ExitStack()
        qkvT = sb(attn, "qkvT", [P, KT, QKV], F16)
        projT = sb(attn, "projT", [P, KT, DIM], F16)
        wg16 = sb(attn, "wg16", [P, KT, 2, E], F16)
        ginv = sb(attn, "ginv", [P, 1])
        mask = sb(attn, "mask", [P, HEADS, P])
        lamq = sb(attn, "lamq", [P, KT, P])
        lamrev = sb(attn, "lamrev", [P, HEADS])
        lamT = sb(attn, "lamT", [P, KT])
        bmask = sb(attn, "bmask", [P, P])
        nw_b = sb(attn, "nw_b", [P, DIM])
        pnw_b = sb(attn, "pnw_b", [P, DIM])
        hw = sb(attn, "hw", [P, KT])
        alpha = sb(attn, "alpha", [P, 2])
        ident16 = sb(attn, "ident16", [P, P], F16)
        ounit = sb(attn, "ounit", [P, 1])
        ounit2 = sb(attn, "ounit2", [P, 1])
        aq = sb(attn, "aq", [P, 1])
        aq2 = sb(attn, "aq2", [P, 1])
        state = sb(attn, "state", [P, B, KT, P])

        WPARTS = (QKV + DIM) // DIM
        ROWS = 4
        xl = sb(attn, "xl", [P, 2, B, DIM])
        xl_in = [sem(attn, f"xl_in{i}") for i in range(2)]
        with setup_ctx as c:
            wg = sb(c, "wg", [P, KT, E])
            wgs = sb(c, "wgs", [P, KT, E])
            gmax = sb(c, "gmax", [P, 1])
            wnat = sb(c, "wnat", [P, QT + KT, DIM])
            above = sb(c, "above", [P, QT + KT, DIM], F16)
            low = sb(c, "low", [P, QT + KT, DIM], F16)
            minus16 = sb(c, "minus16", [P, P], F16)
            s_b = sb(c, "s_b", [P, HEADS])
            s_p = sb(c, "s_p", [P, KT])
            nsb = sb(c, "nsb", [P, HEADS])
            nsp = sb(c, "nsp", [P, KT])
            diff = sb(c, "diff", [P, P])
            valid = sb(c, "valid", [P, P])
            col = sb(c, "col", [P, 1])
            trow = sb(c, "trow", [P, P])
            qnw_b = sb(c, "qnw_b", [P, DIM])
            qnw_c = sb(c, "qnw_c", [P, KT])
            asum = sb(c, "asum", [P, WPARTS])
            wsum = sb(c, "wsum", [P, 2])
            mean = sb(c, "mean", [P, 2])
            quant = sb(c, "quant", [P, 2])
            dequant = sb(c, "dequant", [P, 2])
            nmax = sb(c, "nmax", [P, 4])
            nprod = sb(c, "nprod", [P, 3])
            nexp = sb(c, "nexp", [P, 3])
            nrec = sb(c, "nrec", [P, 3])
            scales = sb(c, "scales", [P, 3])
            iscales = sb(c, "iscales", [P, 2])
            rows = c.enter_context(nc.psum_tensor("rows", [P, ROWS, DIM], F32))
            tot = c.enter_context(nc.psum_tensor("tot", [P, WPARTS], F32))

            in_small = sem(c, "in_small")
            in_w = [sem(c, f"in_w{i}") for i in range(WPARTS)]
            pool_chain = sem(c, "pool_chain")
            ident_ready = sem(c, "ident_ready")
            id16_ready = sem(c, "id16_ready")
            iota_ready = sem(c, "iota_ready")
            sums_ready = sem(c, "sums_ready")
            tot_ready = sem(c, "tot_ready")
            dve = sem(c, "dve_chain")
            neg_ready = sem(c, "neg_ready")
            exp_ready = sem(c, "exp_ready")
            valid_ready = sem(c, "valid_ready")
            tern_ready = sem(c, "tern_ready")
            gmax_ready = sem(c, "gmax_ready")
            gall_ready = sem(c, "gall_ready")
            rows_full = sem(c, "rows_full")
            rows_free = sem(c, "rows_free")
            TILES = QT + KT

            def turned(t):
                w, t = (qkvT, t) if t < QT else (projT, t - QT)
                return w[:, :, t * P:(t + 1) * P]

            block = c.enter_context(nc.Block())

            @block.sync
            def _(sp):
                for i in range(WPARTS):
                    w, a = (qkv_w, i * DIM) if i < WPARTS - 1 else (proj_w, 0)
                    sp.dma_start(wnat[:, i * KT:(i + 1) * KT],
                                 w[a:a + DIM].rearrange("(n p) c -> p n c", p=P)).then_inc(in_w[i], 16)
                for n in range(2):
                    sp.dma_start(xl[:, n], x_steps[n]).then_inc(xl_in[n], 16)

            SMALL = 16 * (1 + HPT + 5)

            @block.scalar
            def _(act):
                with nc.allow_non_contiguous_dma(reason="small vectors laid out as columns"):
                    act.dma_start(s_b[:], s.rearrange("(a h) -> a h", a=1).to_broadcast([P, HEADS])).then_inc(in_small, 16)
                    for h in range(HPT):
                        act.dma_start(s_p[HD * h:HD * h + HD, :],
                                      s.rearrange("(g j) -> j g", j=HPT)[h:h + 1, :].to_broadcast([HD, KT])
                                      ).then_inc(in_small, 16)
                    for dst, src in ((qnw_b, qkv_nw), (nw_b, norm_w), (pnw_b, proj_nw)):
                        act.dma_start(dst[:], src.rearrange("(a h) -> a h", a=1).to_broadcast([P, DIM])).then_inc(in_small, 16)
                    act.dma_start(qnw_c[:], qkv_nw.rearrange("(k p) -> p k", p=P)).then_inc(in_small, 16)
                    act.dma_start(wg[:], w_gate.rearrange("(k p) e -> p k e", p=P)).then_inc(in_small, 16)
                for i in range(0, WPARTS, 2):
                    act.wait_ge(in_w[i], 16)
                    act.activation(low[:, i * KT:(i + 1) * KT], wnat[:, i * KT:(i + 1) * KT], ACT.Abs,
                                   accum_out=asum[:, i:i + 1]).then_inc(sums_ready, 1)
                act.wait_ge(neg_ready, 1)
                act.wait_ge(iota_ready, 1)
                act.wait_ge(valid_ready, 1)
                for g in range(KT):
                    act.activation(lamq[:, g, :], trow[:], ACT.Exp, scale=nsp[:, g:g + 1])
                act.activation(lamT[:], nsp[:], ACT.Exp, scale=float(P))
                act.activation(lamrev[:], nsb[:], ACT.Exp, scale=col[:, 0:1])
                for i, h in enumerate(mask_heads()):
                    ins = act.activation(mask[:, i, :], diff[:], ACT.Exp, scale=nsb[:, h:h + 1])
                ins.then_inc(exp_ready, 1)
                for t in range(TILES):
                    act.wait_ge(rows_full, t + 1)
                    act.activation(turned(t), rows[:, t % ROWS].rearrange("p (k c) -> p k c", k=KT), ACT.Copy
                                   ).then_inc(rows_free, 1)

            @block.gpsimd
            def _(pool):
                pool.memset(ident[:], 0.0)
                pool.memset(ident16[:], 0.0)
                pool.memset(minus16[:], 0.0)
                pool.memset(ones[:], 1.0)
                pool.memset(state[:], 0.0).then_inc(pool_chain, 1)
                pool.wait_ge(pool_chain, 1)
                pool.affine_select(out=ident[:], in_=ident[:], compare_op=ALU.not_equal, fill=1.0, base=0,
                                   pattern=[[-1, P]], channel_multiplier=1)
                pool.affine_select(out=ident16[:], in_=ident16[:], compare_op=ALU.not_equal, fill=1.0, base=0,
                                   pattern=[[-1, P]], channel_multiplier=1)
                pool.affine_select(out=minus16[:], in_=minus16[:], compare_op=ALU.not_equal, fill=-1.0, base=0,
                                   pattern=[[-1, P]], channel_multiplier=1).then_inc(ident_ready, 1)
                pool.iota(diff[:], [[1, P]], base=0, channel_multiplier=-1, allow_small_or_imprecise_dtypes=True)
                pool.iota(trow[:], [[1, P]], base=0, channel_multiplier=0, allow_small_or_imprecise_dtypes=True)
                pool.iota(col[:], [[0, 1]], base=P, channel_multiplier=-1, allow_small_or_imprecise_dtypes=True
                          ).then_inc(iota_ready, 1)
                pool.wait_ge(gmax_ready, 1)
                pool.partition_all_reduce(nmax[:, 3:4], gmax[:], P, R_MAX).then_inc(gall_ready, 1)
                pool.wait_ge(exp_ready, 1)
                pool.wait_ge(valid_ready, 1)
                pool.tensor_scalar(lamq[:], lamq[:], SCALE * P_SCALE, None, ALU.mult)
                pool.tensor_tensor(mask[:], mask[:], valid[:, None, :].to_broadcast([P, HEADS, P]), ALU.mult)

            @block.vector
            def _(v):
                steps = [0]

                def link(ins):
                    steps[0] += 1
                    ins.then_inc(dve, 1)
                    v.wait_ge(dve, steps[0])

                link(v.memset(bmask[:], 0.0))
                for h in range(HPT):
                    v.memset(bmask[HD * h:HD * h + HD, HD * h:HD * h + HD], 1.0)
                v.wait_ge(iota_ready, 1)
                link(v.tensor_scalar(valid[:], diff[:], 0.0, SCALE * P_SCALE, ALU.is_ge, ALU.mult))
                v.tensor_scalar(diff[:], diff[:], 0.0, None, ALU.max).then_inc(valid_ready, 1)
                for i in range(1, WPARTS, 2):
                    v.wait_ge(in_w[i], 16)
                    v.tensor_reduce(asum[:, i:i + 1], wnat[:, i * KT:(i + 1) * KT], AX.XY, ALU.add,
                                    apply_absolute_value=True).then_inc(sums_ready, 1)
                v.wait_ge(tot_ready, 1)
                v.tensor_copy(wsum[:, 1:2], tot[:, WPARTS - 1:])
                link(v.tensor_reduce(wsum[:, 0:1], tot[:, 0:WPARTS - 1], AX.X, ALU.add))
                v.tensor_scalar(mean[:, 0:1], wsum[:, 0:1], 1.0 / (QKV * DIM), 1e-5, ALU.mult, ALU.max)
                link(v.tensor_scalar(mean[:, 1:2], wsum[:, 1:2], 1.0 / (DIM * DIM), 1e-5, ALU.mult, ALU.max))
                link(v.reciprocal(quant[:], mean[:]))
                link(v.reciprocal(dequant[:], quant[:]))

                def ternary(i):
                    part = slice(i * KT, (i + 1) * KT)
                    w, q = wnat[:, part], quant[:, 1:2] if i == WPARTS - 1 else quant[:, 0:1]
                    v.tensor_scalar(low[:, part], w, q, -0.5, ALU.mult, ALU.is_lt)
                    v.tensor_scalar(above[:, part], w, q, 0.5, ALU.mult, ALU.is_gt).then_inc(tern_ready, 1)

                ternary(0)
                v.wait_ge(in_small, SMALL)
                v.tensor_scalar(nsb[:], s_b[:], -1.0, None, ALU.mult)
                v.tensor_scalar(nsp[:], s_p[:], -1.0, None, ALU.mult).then_inc(neg_ready, 1)
                for i in range(1, WPARTS):
                    ternary(i)
                v.tensor_reduce(gmax[:], wg[:], AX.XY, ALU.max, apply_absolute_value=True).then_inc(gmax_ready, 1)
                for i, t in enumerate((qnw_b, nw_b, pnw_b)):
                    ins = v.tensor_reduce(nmax[:, i:i + 1], t[:], AX.X, ALU.max, apply_absolute_value=True)
                link(ins)
                v.wait_ge(gall_ready, 1)
                link(v.tensor_scalar(nmax[:], nmax[:], 1e-12, None, ALU.max))
                v.tensor_copy(nprod[:, 0:1], nmax[:, 0:1])
                v.tensor_copy(nprod[:, 2:3], nmax[:, 3:4])
                link(v.tensor_tensor(nprod[:, 1:2], nmax[:, 1:2], nmax[:, 2:3], ALU.mult))
                link(exponent_floor(v, nexp[:], nprod[:]))
                link(v.reciprocal(nrec[:], nexp[:]))
                v.tensor_scalar(scales[:, 2:3], nrec[:, 2:3], W_POW, None, ALU.mult)
                link(v.tensor_scalar(scales[:, 0:2], nrec[:, 0:2], H_POW, None, ALU.mult))
                v.tensor_scalar(iscales[:], nexp[:, 0:2], 1.0 / H_POW, None, ALU.mult)
                v.tensor_scalar(ginv[:], nexp[:, 2:3], 1.0 / (W_POW * X_SCALE), None, ALU.mult)
                link(v.tensor_scalar(wgs[:], wg[:], scales[:, 2:3], None, ALU.mult))
                link(v.tensor_copy(wg16[:, :, 0], wgs[:]))
                v.tensor_tensor(wg16[:, :, 1], wgs[:], wg16[:, :, 0], ALU.subtract)
                v.tensor_scalar(hw[:], qnw_c[:], scales[:, 0:1], 1.0 / X_SCALE, ALU.mult, ALU.mult)
                v.tensor_scalar(pnw_b[:], pnw_b[:], scales[:, 1:2], None, ALU.mult)
                link(v.tensor_tensor(alpha[:], dequant[:], iscales[:], ALU.mult))
                link(v.tensor_scalar(aq[:], alpha[:, 0:1], Q_POW, None, ALU.mult))
                link(v.tensor_tensor(aq2[:], aq[:], aq[:], ALU.mult))
                link(v.tensor_tensor(ounit[:], aq[:], aq2[:], ALU.mult))
                v.scalar_tensor_tensor(out=ounit2[:], in0=ounit[:], scalar=1.0 / DIM, in1=ounit[:],
                                       op0=ALU.mult, op1=ALU.mult)

            @block.tensor
            def _(pe):
                pe.wait_ge(ident_ready, 1)
                pe.wait_ge(sums_ready, WPARTS)
                pe.matmul(tot[:], ones[:], asum[:], start=True, stop=True).then_inc(tot_ready, 1)
                for t in range(TILES):
                    pe.wait_ge(tern_ready, t // KT + 1)
                    if t >= ROWS:
                        pe.wait_ge(rows_free, t - ROWS + 1)
                    for k in range(KT):
                        cols = slice(k * P, (k + 1) * P)
                        pe.matmul(rows[:, t % ROWS, cols], above[:, t, cols], ident16[:], start=True, stop=False)
                        ins = pe.matmul(rows[:, t % ROWS, cols], low[:, t, cols], minus16[:], start=False, stop=True)
                    ins.then_inc(rows_full, 1)

        attention(nc, attn, sb, sem, locals())
        attn.close()
        experts(nc, sb, sem, locals())


def load_group(sp, k, g):
    raw, done = k["raw"][:, g % 2], k["raw_in"][g % 2]
    for h in range(2):
        sp.dma_start(raw[:, 0:KT, h * FFN:(h + 1) * FFN], k["sgu"][g, h]).then_inc(done, 16)
    sp.dma_start(raw[:, KT:], k["sdn"][g]).then_inc(done, 16)


def wait_apart(eng, sem, value, passed):
    eng.wait_ge(sem, value)
    eng.sem_inc(passed, 1)


def mask_heads():
    return [HPT * (2 * (s // 2) + gg) + 2 * (s % 2) + jj for s in range(4) for jj in range(2) for gg in range(2)]


def attention(nc, ctx, sb, sem, k):
    ident, logits = k["ident"], k["logits"]
    qkvT, projT, wg16, ginv, mask, lamq, lamrev, lamT, bmask = (k[x] for x in "qkvT projT wg16 ginv mask lamq lamrev lamT bmask".split())
    nw_b, pnw_b, hw, alpha, state = (k[x] for x in "nw_b pnw_b hw alpha state".split())
    ident16, ounit, ounit2, xl, xl_in = (k[x] for x in "ident16 ounit ounit2 xl xl_in".split())
    x_steps, x1_steps, xn_steps, NCH, B = k["x_steps"], k["x1_steps"], k["xn_steps"], k["NCH"], k["B"]
    wmax, xT_dram = k["wmax"], k["xT_dram"]
    wtop, wall, wexp, wrec, wscale, esq, gate_inv, up_inv, out_inv = (
        k[x] for x in "wtop wall wexp wrec wscale esq gate_inv up_inv out_inv".split())
    flat = [w.rearrange(f"{d} -> ({d})").rearrange("(p f) -> p f", p=P)
            for w, d in ((k["w_gu"], "e k c"), (k["w_dn"], "e k c"), (k["w_sgu"], "k c"), (k["w_sdn"], "k c"))]
    PART = [w.shape[1] // NCH for w in flat]
    START = [sum(PART[:i]) for i in range(5)]
    assert B == 2 and NCH % 2 == 0 and KT == 4

    with ExitStack() as c:
        T2 = B * P
        xr = sb(c, "xr", [P, B, DIM])
        xn = sb(c, "xn", [P, 2, B, DIM])
        xnT = sb(c, "xnT", [P, KT, T2])
        x16 = sb(c, "x16", [P, 2, KT, 2, T2], F16)
        wraw = sb(c, "wraw", [P, 2, START[4]])
        hh = sb(c, "hh", [P, KT, T2], F16)
        hl = sb(c, "hl", [P, KT, T2], F16)
        qT = sb(c, "qT", [P, KT, T2])
        q16 = sb(c, "q16", [P, 2, 2, KT, T2], F16)
        k16 = sb(c, "k16", [P, 2, 2, KT, T2], F16)
        qlam = sb(c, "qlam", [P, 2, KT, T2])
        v16 = sb(c, "v16", [P, 2, 2, B, DIM], F16)
        probs = sb(c, "probs", [P, 4, 4, P])
        p16 = sb(c, "p16", [P, B, 2, 4, 4, P], F16)
        kS = sb(c, "kS", [P, B, DIM])
        kS16 = sb(c, "kS16", [P, B, 2, DIM], F16)
        kvm = sb(c, "kvm", [P, B, KT, P])
        on = sb(c, "on", [P, B, DIM])
        on3 = sb(c, "on3", [P, B, DIM])
        yh = sb(c, "yh", [P, B, KT, P], F16)
        yl = sb(c, "yl", [P, B, KT, P], F16)
        x1 = sb(c, "x1", [P, B, DIM])
        junk = sb(c, "junk", [P, DIM])
        stats = sb(c, "stats", [P, B, 6])
        mv = sb(c, "mv", [P, 2, B, 2])
        ve = sb(c, "ve", [P, 2, B])
        sd = sb(c, "sd", [P, 2, B])
        rstd = sb(c, "rstd", [P, 2, B])
        rve = sb(c, "rve", [P, 2, B])
        hv = sb(c, "hv", [P, 2, B])
        hv2 = sb(c, "hv2", [P, 2, B])
        hsd = sb(c, "hsd", [P, 2, B])
        r = sb(c, "r", [P, 2, B])
        r2 = sb(c, "r2", [P, 2, B])
        r2m = sb(c, "r2m", [P, 2, B])
        rc = sb(c, "rc", [P, 2, B])
        rv = sb(c, "rv", [P, 2, B])
        kscale = sb(c, "kscale", [P, 2, B, HEADS])
        ss1 = sb(c, "ss1", [P, B])
        z1 = sb(c, "z1", [P, B])
        sq1 = sb(c, "sq1", [P, B])
        g1a = sb(c, "g1a", [P, B])
        g1 = sb(c, "g1", [P, B])
        ss2 = sb(c, "ss2", [P, B])
        z2 = sb(c, "z2", [P, B])
        sq2 = sb(c, "sq2", [P, B])
        g2a = sb(c, "g2a", [P, B])
        g2 = sb(c, "g2", [P, B])

        ring = [c.enter_context(nc.psum_tensor(f"ring{i}", [P, DIM], F32)) for i in range(Ring.BANKS)]
        sc = c.enter_context(nc.psum_tensor("sc", [P, 4, DIM], F32))
        o_ps = c.enter_context(nc.psum_tensor("o_ps", [P, DIM], F32))

        full = [sem(c, f"ring_full{i}") for i in range(Ring.BANKS)]
        xr_in = sem(c, "xr_in")
        xn_out = [sem(c, f"xn_out{i}") for i in range(2)]
        x1_out = [sem(c, f"x1_out{i}") for i in range(2)]
        xT_out = [sem(c, f"xT_out{i}") for i in range(2)]
        wraw_in = [sem(c, f"wraw_in{i}") for i in range(2)]
        names = ("xhigh_ready xlow_ready wmax_ready stats_ready stats_seen mv_ready ve_ready sd_ready rstd_ready xn_ready rve_ready hv_ready hv2_ready hsd_ready "
                 "r_ready r2_ready kscale_ready xnT_ready hh_ready h_ready q_ready k_ready v_ready qlam_ready "
                 "o_full logits_ready kvm_ready kS_ready ss1_ready z1_ready sq1_ready g1a_ready "
                 "g1_ready on_ready ss2_ready z2_ready sq2_ready g2a_ready g2_ready on3_ready yh_ready yl_ready "
                 "x1_ready decayed rv_ready qT_ready qh_ready kh_ready vh_ready ph_ready pl_ready ksh_ready ksl_ready "
                 "scale_chain top_ready all_ready")
        S = {n: sem(c, n) for n in names.split()}
        sc_full = [sem(c, f"sc_full{i}") for i in range(2)]
        sc_free = [sem(c, f"sc_free{i}") for i in range(2)]
        state_ready = [sem(c, f"state_ready{i}") for i in range(B)]

        block = c.enter_context(nc.Block())

        def run_steps(eng, prologue, step):
            prologue()
            step(0, 0, True, True)
            step(0, 1, True, True)
            with eng.Fori(1, NCH // 2 - 1) as q:
                step(q, 0, True, True)
                step(q, 1, True, True)
            step(NCH // 2 - 1, 0, True, False)
            step(NCH // 2 - 1, 1, False, False)

        def after(q, par):
            return (q, 1) if par == 0 else (q + 1, 0)

        READ = {"xnT": "xnT_ready", "rt": "logits_ready", "q": "q_ready", "k": "k_ready", "v": "v_ready",
                "kTr": "kS_ready", "kv": "kvm_ready", "onT": "yl_ready", "proj": "x1_ready"}

        def fill(pe, name, st):
            before = Ring.before(name, st)
            if before is not None:
                held, ahead = before
                n = ahead if st is None else 2 * st[0] + st[1] + ahead
                if held == "rt":
                    pe.wait_ge(S["logits_ready"], n + 1)
                else:
                    pe.wait_ge(S[READ[held[:-1]]], 2 * n + int(held[-1]) + 1)
            b, _ = Ring.at(name, st)
            return ring[b], full[b]

        def filled(eng, name, st):
            b, n = Ring.at(name, st)
            eng.wait_ge(full[b], n + 1)
            return ring[b]

        @block.sync
        def _(sp):
            def load_xl(q, par):
                n = 2 * q + par
                sp.dma_start(xl[:, par], x_steps[n] if isinstance(n, int) else x_steps[bass.ds(n, 1)][0]
                             ).then_inc(xl_in[par], 16)

            def load_xr(q, par):
                n = 2 * q + par
                sp.dma_start(xr[:], x_steps[n] if isinstance(n, int) else x_steps[bass.ds(n, 1)][0]
                             ).then_inc(xr_in, 16)

            def store_xn(q, par):
                n = 2 * q + par
                sp.wait_ge(S["xn_ready"], 2 * n + 2)
                sp.dma_start(xn_steps[n] if isinstance(n, int) else xn_steps[bass.ds(n, 1)][0], xn[:, par]
                             ).then_inc(xn_out[par], 16)

            def load_weights(q, par):
                n = 2 * q + par
                for w, size, a in zip(flat, PART, START):
                    sp.dma_start(wraw[:, par, a:a + size], w[:, bass.ds(n * size, size)]).then_inc(wraw_in[par], 16)

            def store_xT(q, par):
                n = 2 * q + par
                sp.wait_ge(S["xlow_ready"], n + 1)
                sp.dma_start(xT_dram[n] if isinstance(n, int) else xT_dram[bass.ds(n, 1)][0], x16[:, par]
                             ).then_inc(xT_out[par], 16)

            def prologue():
                for done_sem in k["setup_sems"]:
                    sp.sem_clear(done_sem)
                store_xn(0, 0)
                load_weights(0, 0)
                store_xT(0, 0)

            def step(q, par, front, norm):
                n = 2 * q + par
                if norm:
                    sp.wait_ge(S["xn_ready"], 2 * n + 2)
                    load_xl(q + 1, par)
                if not front:
                    for g in range(2):
                        load_group(sp, k, g)
                sp.wait_ge(S["x1_ready"], 2 * n)
                load_xr(q, par)
                if front:
                    store_xn(*after(q, par))
                    sp.wait_ge(S["wmax_ready"], n)
                    load_weights(*after(q, par))
                for u in range(B):
                    if u == 1 and front:
                        store_xT(*after(q, par))
                    sp.wait_ge(S["x1_ready"], 2 * n + u + 1)
                    dst = x1_steps[n] if isinstance(n, int) else x1_steps[bass.ds(n, 1)][0]
                    sp.dma_start(dst[:, u], x1[:, u]).then_inc(x1_out[u], 16)

            run_steps(sp, prologue, step)
            for par in range(2):
                sp.wait_ge(xn_out[par], 16 * (NCH // 2))
                sp.wait_ge(x1_out[par], 16 * NCH)
                sp.wait_ge(xT_out[par], 16 * (NCH // 2))

        @block.tensor
        def _(pe):
            def xn_turn(i, q, par, st):
                n = 2 * q + par
                pe.wait_ge(S["xn_ready"], 2 * n + 2)
                bank, done = fill(pe, f"xnT{i}", st)
                for kk in range(2):
                    for u in range(B):
                        a = (2 * kk + u) * P
                        ins = pe.transpose(bank[:, a:a + P], xn[:, par, u, (2 * i + kk) * P:(2 * i + kk + 1) * P], ident[:])
                ins.then_inc(done, 1)

            def router(q, par, st):
                n = 2 * q + par
                pe.wait_ge(S["xlow_ready"], n + 1)
                bank, done = fill(pe, "rt", st)
                for u in range(B):
                    for kk in range(KT):
                        for i, (a, b) in enumerate(PASSES):
                            ins = pe.matmul(bank[:, u * EXPERTS:(u + 1) * EXPERTS], x16[:, par, kk, a, u * P:(u + 1) * P],
                                            wg16[:, kk, b, :], start=(kk == 0 and i == 0), stop=(kk == KT - 1 and i == 2))
                ins.then_inc(done, 1)

            def project(name, q, par, st):
                n = 2 * q + par
                pe.wait_ge(S["h_ready"], n + 1)
                bank, done = fill(pe, name, st)
                i = int(name[1])
                if name[0] == "v":
                    for kk in range(KT):
                        for h in (hh, hl):
                            ins = pe.matmul(bank[:], h[:, kk, i * P:(i + 1) * P], qkvT[:, kk, 2 * DIM:3 * DIM],
                                            start=(kk == 0 and h is hh), stop=(kk == KT - 1 and h is hl))
                else:
                    for g in range(2):
                        a = (0 if name[0] == "q" else DIM) + (2 * i + g) * P
                        for kk in range(KT):
                            for h in (hh, hl):
                                ins = pe.matmul(bank[:, g * T2:(g + 1) * T2], qkvT[:, kk, a:a + P], h[:, kk, :],
                                                start=(kk == 0 and h is hh), stop=(kk == KT - 1 and h is hl))
                ins.then_inc(done, 1)

            def scores(u, q, par, sets):
                n = 2 * q + par
                if u == 0 and sets[0] == 0:
                    pe.wait_ge(S["q_ready"], 2 * n + 2)
                    pe.wait_ge(S["k_ready"], 2 * n + 2)
                for s in sets:
                    pair = s % 2
                    pe.wait_ge(sc_free[pair], 4 * n + 2 * u + s // 2)
                    for gg in range(2):
                        for i, (a, b) in enumerate(PASSES):
                            for jj in range(2):
                                g, j = 2 * (s // 2) + gg, 2 * pair + jj
                                rows = slice(HD * j, HD * j + HD)
                                ins = pe.matmul(sc[:, j, gg * P:(gg + 1) * P], k16[rows, par, a, g, u * P:(u + 1) * P],
                                                q16[rows, par, b, g, u * P:(u + 1) * P], start=(i == 0), stop=(i == 2))
                    ins.then_inc(sc_full[pair], 1)

            def k_turn(u, q, par, st):
                bank, done = fill(pe, f"kTr{u}", st)
                for g in range(KT):
                    for a in range(2):
                        ins = pe.matmul(bank[:, g * P:(g + 1) * P], k16[:, par, a, g, u * P:(u + 1) * P], ident16[:],
                                        start=(a == 0), stop=(a == 1))
                ins.then_inc(done, 1)

            def outputs(u, q, par):
                n = 2 * q + par
                pe.wait_ge(S["on_ready"], 2 * n + u)
                pe.wait_ge(S["qlam_ready"], n + 1)
                pe.wait_ge(state_ready[u], n)
                pe.wait_ge(S["v_ready"], 2 * n + 2)
                for g in range(KT):
                    pe.matmul(o_ps[:, g * P:(g + 1) * P], qlam[:, par, g, u * P:(u + 1) * P], state[:, u, g, :],
                              start=(g == 0), stop=False, skip_group_check=True)
                heads = mask_heads()
                for s in range(4):
                    pe.wait_ge(S["pl_ready"], 8 * n + 4 * u + s + 1)
                    for i in range(4):
                        h = heads[4 * s + i]
                        for a, b in PASSES:
                            ins = pe.matmul(o_ps[:, HD * h:HD * h + HD], p16[:, u, a, s, i, :],
                                            v16[:, par, b, u, HD * h:HD * h + HD], start=False,
                                            stop=(s == 3 and i == 3 and (a, b) == PASSES[-1]), skip_group_check=True)
                ins.then_inc(S["o_full"], 1)

            def outer(u, q, par, st):
                n = 2 * q + par
                pe.wait_ge(S["ksl_ready"], 2 * n + u + 1)
                bank, done = fill(pe, f"kv{u}", st)
                for g in range(KT):
                    cols = slice(g * P, (g + 1) * P)
                    for i, (a, b) in enumerate(PASSES):
                        ins = pe.matmul(bank[:, cols], kS16[:, u, a, cols], v16[:, par, b, u, cols],
                                        start=(i == 0), stop=(i == 2))
                ins.then_inc(done, 1)

            def o_turn(u, q, par, st):
                n = 2 * q + par
                pe.wait_ge(S["on3_ready"], 2 * n + u + 1)
                bank, done = fill(pe, f"onT{u}", st)
                for g in range(KT):
                    ins = pe.transpose(bank[:, g * P:(g + 1) * P], on3[:, u, g * P:(g + 1) * P], ident[:])
                ins.then_inc(done, 1)

            def proj(u, q, par, st):
                n = 2 * q + par
                pe.wait_ge(S["yl_ready"], 2 * n + u + 1)
                bank, done = fill(pe, f"proj{u}", st)
                for g in range(KT):
                    for y in (yh, yl):
                        ins = pe.matmul(bank[:], y[:, u, g, :], projT[:, g, :],
                                        start=(g == 0 and y is yh), stop=(g == KT - 1 and y is yl))
                ins.then_inc(done, 1)

            def prologue():
                xn_turn(0, 0, 0, None)
                xn_turn(1, 0, 0, None)
                for name in ("q0", "q1"):
                    project(name, 0, 0, None)
                router(0, 0, None)
                for name in ("k0", "k1"):
                    project(name, 0, 0, None)
                scores(0, 0, 0, (0, 1, 2, 3))
                for name in ("v0", "v1"):
                    project(name, 0, 0, None)

            def step(q, par, front, norm):
                st = (q, par, not front)
                nxt = after(q, par)
                if front:
                    xn_turn(0, *nxt, st)
                    xn_turn(1, *nxt, st)
                k_turn(0, q, par, st)
                scores(1, q, par, (0, 1))
                outputs(0, q, par)
                scores(1, q, par, (2, 3))
                outer(0, q, par, st)
                if front:
                    project("q0", *nxt, st)
                    project("q1", *nxt, st)
                k_turn(1, q, par, st)
                outputs(1, q, par)
                if front:
                    router(*nxt, st)
                o_turn(0, q, par, st)
                if front:
                    project("k0", *nxt, st)
                outer(1, q, par, st)
                if front:
                    project("k1", *nxt, st)
                proj(0, q, par, st)
                if front:
                    scores(0, *nxt, (0, 1))
                o_turn(1, q, par, st)
                if front:
                    project("v0", *nxt, st)
                    scores(0, *nxt, (2, 3))
                    project("v1", *nxt, st)
                proj(1, q, par, st)

            run_steps(pe, prologue, step)

        @block.scalar
        def _(act):
            def norm_roots(q, par):
                n = 2 * q + par
                act.wait_ge(S["ve_ready"], n + 1)
                act.activation(sd[:, par], ve[:, par], ACT.Sqrt).then_inc(S["sd_ready"], 1)
                act.wait_ge(S["hv2_ready"], n + 1)
                act.activation(hsd[:, par], hv2[:, par], ACT.Sqrt).then_inc(S["hsd_ready"], 1)

            def take_xnT(i, q, par, st):
                n = 2 * q + par
                if i == 0:
                    act.wait_ge(S["h_ready"], n)
                    act.wait_ge(S["xlow_ready"], n)
                bank = filled(act, f"xnT{i}", st)
                act.activation(xnT[:, 2 * i:2 * i + 2, :], bank[:].rearrange("p (k t) -> p k t", k=2), ACT.Copy,
                               scale=X_SCALE
                               ).then_inc(S["xnT_ready"], 1)

            def x_high(q, par):
                n = 2 * q + par
                act.wait_ge(S["xnT_ready"], 2 * n + 2)
                act.wait_ge(xT_out[par], 16 * q)
                act.activation(x16[:, par, :, 0], xnT[:], ACT.Copy).then_inc(S["xhigh_ready"], 1)

            def h_high(q, par):
                n = 2 * q + par
                act.wait_ge(S["xnT_ready"], 2 * n + 2)
                act.wait_ge(S["v_ready"], 2 * n)
                for kk in range(KT):
                    ins = act.activation(hh[:, kk], xnT[:, kk], ACT.Copy, scale=hw[:, kk:kk + 1])
                ins.then_inc(S["hh_ready"], 1)

            def take(name, q, par, st):
                n = 2 * q + par
                bank = filled(act, name, st)
                i, ready = int(name[1]), S[name[0] + "h_ready"]
                if name[0] == "v":
                    act.wait_ge(S["rv_ready"], n + 1)
                    act.activation(v16[:, par, 0, i, :], bank[:], ACT.Copy, scale=rv[:, par, i:i + 1]).then_inc(ready, 1)
                    return
                source = bank[:].rearrange("p (k t) -> p k t", k=2)
                dst = q16 if name[0] == "q" else k16
                if name[0] == "q":
                    act.wait_ge(S["qlam_ready"], n)
                    act.activation(qT[:, 2 * i:2 * i + 2, :], source, ACT.Copy, scale=Q_SCALE).then_inc(S["qT_ready"], 1)
                act.activation(dst[:, par, 0, 2 * i:2 * i + 2, :], source, ACT.Copy, scale=Q_SCALE).then_inc(ready, 1)

            def probs_high(u, q, par, sets):
                n = 2 * q + par
                for s in sets:
                    act.wait_ge(sc_free[s % 2], 4 * n + 2 * u + s // 2 + 1)
                    act.activation(p16[:, u, 0, s], probs[:, s], ACT.Copy).then_inc(S["ph_ready"], 1)

            def kS_high(u, q, par):
                n = 2 * q + par
                act.wait_ge(S["kS_ready"], 2 * n + u + 1)
                act.activation(kS16[:, u, 0], kS[:, u], ACT.Copy).then_inc(S["ksh_ready"], 1)

            def o_square(u, q, par):
                n = 2 * q + par
                act.wait_ge(S["o_full"], 2 * n + u + 1)
                act.activation(junk[:], o_ps[:], ACT.Square, accum_out=ss1[:, u:u + 1]).then_inc(S["ss1_ready"], 1)

            def o_root(u, q, par):
                n = 2 * q + par
                act.wait_ge(S["z1_ready"], 2 * n + u + 1)
                act.activation(sq1[:, u:u + 1], z1[:, u:u + 1], ACT.Sqrt).then_inc(S["sq1_ready"], 1)

            def on_squares(u, q, par):
                n = 2 * q + par
                act.wait_ge(S["on_ready"], 2 * n + u + 1)
                act.activation(junk[:], on[:, u], ACT.Square, accum_out=ss2[:, u:u + 1]).then_inc(S["ss2_ready"], 1)
                act.wait_ge(S["z2_ready"], 2 * n + u + 1)
                act.activation(sq2[:, u:u + 1], z2[:, u:u + 1], ACT.Sqrt).then_inc(S["sq2_ready"], 1)

            def y_high(u, q, par, st):
                bank = filled(act, f"onT{u}", st)
                act.activation(yh[:, u], bank[:].rearrange("p (k t) -> p k t", k=KT), ACT.Copy
                               ).then_inc(S["yh_ready"], 1)

            def prologue():
                norm_roots(0, 0)
                take_xnT(0, 0, 0, None)
                take_xnT(1, 0, 0, None)
                h_high(0, 0)
                x_high(0, 0)
                for name in ("q0", "q1", "k0", "k1"):
                    take(name, 0, 0, None)
                probs_high(0, 0, 0, (0, 1, 2, 3))
                norm_roots(0, 1)
                for name in ("v0", "v1"):
                    take(name, 0, 0, None)

            def step(q, par, front, norm):
                st = (q, par, not front)
                nxt = after(q, par)
                if front:
                    take_xnT(0, *nxt, st)
                    take_xnT(1, *nxt, st)
                    h_high(*nxt)
                kS_high(0, q, par)
                probs_high(1, q, par, (0, 1, 2, 3))
                if front:
                    x_high(*nxt)
                o_square(0, q, par)
                o_root(0, q, par)
                if front:
                    take("q0", *nxt, st)
                    take("q1", *nxt, st)
                on_squares(0, q, par)
                kS_high(1, q, par)
                o_square(1, q, par)
                y_high(0, q, par, st)
                if front:
                    take("k0", *nxt, st)
                o_root(1, q, par)
                if front:
                    take("k1", *nxt, st)
                on_squares(1, q, par)
                if front:
                    probs_high(0, *nxt, (0, 1))
                if norm:
                    norm_roots(q + 1, par)
                y_high(1, q, par, st)
                if front:
                    take("v0", *nxt, st)
                    take("v1", *nxt, st)
                    probs_high(0, *nxt, (2, 3))

            run_steps(act, prologue, step)

        def kS_low(eng, u, q, par):
            n = 2 * q + par
            eng.wait_ge(S["ksh_ready"], 2 * n + u + 1)
            eng.tensor_tensor(kS16[:, u, 1], kS[:, u], kS16[:, u, 0], ALU.subtract).then_inc(S["ksl_ready"], 1)

        @block.vector
        def _(v):
            def row_stats(u, q, par):
                v.wait_ge(xl_in[par], 16 * (q + 1))
                v.bn_stats(stats[:, u], xl[:, par, u]).then_inc(S["stats_ready"], 1)

            def norm_stats(q, par):
                n = 2 * q + par
                v.wait_ge(S["stats_ready"], 2 * n + 2)
                v.sem_inc(S["stats_seen"], 1)
                v.bn_aggr(mv[:, par, 0], stats[:, 0])
                v.bn_aggr(mv[:, par, 1], stats[:, 1]).then_inc(S["mv_ready"], 1)
                v.wait_ge(S["mv_ready"], n + 1)
                var = mv[:, par, :, 1]
                v.tensor_scalar(ve[:, par], var, LN_EPS, None, ALU.add).then_inc(S["ve_ready"], 1)
                v.wait_ge(S["ve_ready"], n + 1)
                v.reciprocal(rve[:, par], ve[:, par]).then_inc(S["rve_ready"], 1)
                v.wait_ge(S["rve_ready"], n + 1)
                v.tensor_tensor(hv[:, par], var, rve[:, par], ALU.mult).then_inc(S["hv_ready"], 1)
                v.wait_ge(S["hv_ready"], n + 1)
                v.tensor_scalar(hv2[:, par], hv[:, par], F32_EPS, None, ALU.add).then_inc(S["hv2_ready"], 1)

            def norm(q, par):
                n = 2 * q + par
                v.wait_ge(S["sd_ready"], n + 1)
                v.reciprocal(rstd[:, par], sd[:, par]).then_inc(S["rstd_ready"], 1)
                v.wait_ge(S["rstd_ready"], n + 1)
                v.wait_ge(xn_out[par], 16 * q)
                for u in range(B):
                    v.tensor_scalar(xn[:, par, u], xl[:, par, u], mv[:, par, u, 0:1], rstd[:, par, u:u + 1],
                                    ALU.subtract, ALU.mult).then_inc(S["xn_ready"], 1)

            def norm_factors(q, par):
                n = 2 * q + par
                v.wait_ge(S["hsd_ready"], n + 1)
                v.reciprocal(r[:, par], hsd[:, par]).then_inc(S["r_ready"], 1)
                v.wait_ge(S["r_ready"], n + 1)
                v.tensor_tensor(r2[:, par], r[:, par], r[:, par], ALU.mult).then_inc(S["r2_ready"], 1)
                v.tensor_scalar(rv[:, par], r[:, par], Q_SCALE, None, ALU.mult).then_inc(S["rv_ready"], 1)
                v.tensor_scalar(rc[:, par], r[:, par], ounit[:, 0:1], None, ALU.mult)
                v.wait_ge(S["r2_ready"], n + 1)
                v.tensor_scalar(r2m[:, par], r2[:, par], ounit2[:, 0:1], None, ALU.mult)
                for u in range(B):
                    ins = v.tensor_scalar(kscale[:, par, u], lamrev[:], r[:, par, u:u + 1], None, ALU.mult)
                ins.then_inc(S["kscale_ready"], 1)

            def h_low(q, par):
                n = 2 * q + par
                v.wait_ge(S["hh_ready"], n + 1)
                for kk in range(KT):
                    ins = v.scalar_tensor_tensor(out=hl[:, kk], in0=xnT[:, kk], scalar=hw[:, kk:kk + 1], in1=hh[:, kk],
                                                 op0=ALU.mult, op1=ALU.subtract)
                ins.then_inc(S["h_ready"], 1)

            def low(name, q, par, st):
                n = 2 * q + par
                i = int(name[1])
                v.wait_ge(S[name[0] + "h_ready"], 2 * n + i + 1)
                bank = filled(v, name, st)
                if name[0] == "v":
                    source, (high_, low_) = bank[:], (v16[:, par, a, i, :] for a in range(2))
                else:
                    source = bank[:].rearrange("p (k t) -> p k t", k=2)
                    dst = q16 if name[0] == "q" else k16
                    high_, low_ = (dst[:, par, a, 2 * i:2 * i + 2, :] for a in range(2))
                v.scalar_tensor_tensor(out=low_, in0=source, scalar=rv[:, par, i:i + 1] if name[0] == "v" else Q_SCALE,
                                       in1=high_, op0=ALU.mult, op1=ALU.subtract).then_inc(S[name[0] + "_ready"], 1)

            def take_logits(q, par, st):
                n = 2 * q + par
                bank = filled(v, "rt", st)
                dst = logits[:, :, n, :] if isinstance(n, int) else logits[:, :, bass.ds(n, 1), :][:, :, 0, :]
                v.tensor_scalar(dst, bank[:, 0:B * EXPERTS].rearrange("p (u e) -> p u e", u=B), ginv[:, 0:1], None, ALU.mult
                                ).then_inc(S["logits_ready"], 1)

            def weight_maxima(q, par, some):
                n = 2 * q + par
                v.wait_ge(wraw_in[par], 64 * (q + 1))
                for i in some:
                    ins = v.tensor_reduce(wmax[:, i, bass.ds(n, 1)], wraw[:, par, START[i]:START[i + 1]], AX.X, ALU.max,
                                          apply_absolute_value=True)
                if 0 in some:
                    ins.then_inc(S["wmax_ready"], 1)

            def weight_scales():
                linked_so_far = [0]

                def linked(ins):
                    linked_so_far[0] += 1
                    ins.then_inc(S["scale_chain"], 1)
                    v.wait_ge(S["scale_chain"], linked_so_far[0])

                v.wait_ge(S["wmax_ready"], NCH)
                v.tensor_reduce(wtop[:], wmax[:], AX.X, ALU.max).then_inc(S["top_ready"], 1)
                v.wait_ge(S["all_ready"], 1)
                linked(v.tensor_scalar(wall[:], wall[:], 1e-12, None, ALU.max))
                linked(exponent_floor(v, wexp[:], wall[:]))
                linked(v.reciprocal(wrec[:], wexp[:]))
                v.tensor_scalar(wscale[:], wrec[:], W_POW, None, ALU.mult)
                gu, dn = wexp[:].rearrange("p (s m) -> p m s", s=2)[:, 0], wexp[:].rearrange("p (s m) -> p m s", s=2)[:, 1]
                v.tensor_scalar(gate_inv[:], gu, 1.0 / (W_POW * X_SCALE), None, ALU.mult)
                v.tensor_scalar(up_inv[:], wrec[:].rearrange("p (s m) -> p m s", s=2)[:, 0],
                                2.0 ** -5 / (W_POW * X_SCALE), None, ALU.mult)
                linked(v.tensor_tensor(esq[:], gu, gu, ALU.mult))
                v.scalar_tensor_tensor(out=out_inv[:], in0=esq[:], scalar=2.0 ** 5 / W_POW, in1=dn,
                                       op0=ALU.mult, op1=ALU.mult)

            def decayed_scores(u, q, par, sets, first=False):
                n = 2 * q + par
                v.wait_ge(S["kscale_ready"], n + 1)
                for s in sets:
                    pair = s % 2
                    v.wait_ge(sc_full[pair], 4 * n + 2 * u + s // 2 + 1)
                    if not first:
                        v.wait_ge(S["pl_ready"], 8 * n + 4 * u + s - 3)
                    v.scalar_tensor_tensor(out=probs[:, s].rearrange("p (j g) t -> p j (g t)", j=2),
                                           in0=sc[:, 2 * pair:2 * pair + 2, 0:2 * P],
                                           scalar=r[:, par, u:u + 1],
                                           in1=mask[:, 4 * s:4 * s + 4].rearrange("p (j g) t -> p j (g t)", j=2),
                                           op0=ALU.mult, op1=ALU.mult).then_inc(sc_free[pair], 1)

            def scaled_k(u, q, par, st):
                bank = filled(v, f"kTr{u}", st)
                v.tensor_tensor(kS[:, u].rearrange("p (h d) -> p h d", d=HD),
                                bank[:].rearrange("p (h d) -> p h d", d=HD),
                                kscale[:, par, u, :, None].to_broadcast([P, HEADS, HD]), ALU.mult
                                ).then_inc(S["kS_ready"], 1)

            def masked_kv(u, q, par, st):
                n = 2 * q + par
                bank = filled(v, f"kv{u}", st)
                v.wait_ge(state_ready[u], n)
                v.tensor_tensor(kvm[:, u], bank[:].rearrange("p (g e) -> p g e", g=KT),
                                bmask[:, None, :].to_broadcast([P, KT, P]), ALU.mult).then_inc(S["kvm_ready"], 1)

            def o_mean(u, q, par):
                n = 2 * q + par
                c1 = slice(u, u + 1)
                m = 2 * n + u + 1
                v.wait_ge(S["ss1_ready"], m)
                v.tensor_scalar(z1[:, c1], ss1[:, c1], r2m[:, par, c1], NORM_EPS, ALU.mult, ALU.add
                                ).then_inc(S["z1_ready"], 1)

            def normed(u, q, par):
                n = 2 * q + par
                c1 = slice(u, u + 1)
                m = 2 * n + u + 1
                v.wait_ge(S["sq1_ready"], m)
                v.reciprocal(g1a[:, c1], sq1[:, c1]).then_inc(S["g1a_ready"], 1)
                v.wait_ge(S["g1a_ready"], m)
                v.tensor_tensor(g1[:, c1], g1a[:, c1], rc[:, par, c1], ALU.mult).then_inc(S["g1_ready"], 1)
                v.wait_ge(S["g1_ready"], m)
                v.scalar_tensor_tensor(out=on[:, u], in0=o_ps[:], scalar=g1[:, c1], in1=nw_b[:],
                                       op0=ALU.mult, op1=ALU.mult).then_inc(S["on_ready"], 1)

            def second_norm(u, q, par):
                n = 2 * q + par
                c1 = slice(u, u + 1)
                m = 2 * n + u + 1
                v.wait_ge(S["ss2_ready"], m)
                v.tensor_scalar(z2[:, c1], ss2[:, c1], 1.0 / DIM, F32_EPS, ALU.mult, ALU.add).then_inc(S["z2_ready"], 1)
                v.wait_ge(S["sq2_ready"], m)
                v.reciprocal(g2a[:, c1], sq2[:, c1]).then_inc(S["g2a_ready"], 1)
                v.wait_ge(S["g2a_ready"], m)
                v.tensor_tensor(g2[:, c1], g2a[:, c1], alpha[:, 1:2], ALU.mult).then_inc(S["g2_ready"], 1)

            def y_low(u, q, par, st):
                n = 2 * q + par
                v.wait_ge(S["yh_ready"], 2 * n + u + 1)
                bank = filled(v, f"onT{u}", st)
                v.tensor_tensor(yl[:, u], bank[:].rearrange("p (k t) -> p k t", k=KT), yh[:, u], ALU.subtract
                                ).then_inc(S["yl_ready"], 1)

            def residual(u, q, par, st):
                n = 2 * q + par
                c1 = slice(u, u + 1)
                bank = filled(v, f"proj{u}", st)
                v.wait_ge(S["g2_ready"], 2 * n + u + 1)
                v.wait_ge(xr_in, 16 * (n + 1))
                v.wait_ge(x1_out[u], 16 * n)
                v.scalar_tensor_tensor(out=x1[:, u], in0=bank[:], scalar=g2[:, c1], in1=xr[:, u],
                                       op0=ALU.mult, op1=ALU.add).then_inc(S["x1_ready"], 1)

            def prologue():
                for u in range(B):
                    row_stats(u, 0, 0)
                norm_stats(0, 0)
                norm(0, 0)
                norm_factors(0, 0)
                h_low(0, 0)
                for u in range(B):
                    row_stats(u, 0, 1)
                for name in ("q0", "q1"):
                    low(name, 0, 0, None)
                take_logits(0, 0, None)
                norm_stats(0, 1)
                for name in ("k0", "k1"):
                    low(name, 0, 0, None)
                decayed_scores(0, 0, 0, (0, 1, 2, 3), first=True)
                norm(0, 1)
                for name in ("v0", "v1"):
                    low(name, 0, 0, None)
                norm_factors(0, 1)

            def step(q, par, front, has_norm):
                st = (q, par, not front)
                nxt = after(q, par)
                scaled_k(0, q, par, st)
                decayed_scores(1, q, par, (0, 1))
                if front:
                    h_low(*nxt)
                decayed_scores(1, q, par, (2, 3))
                weight_maxima(q, par, (1, 2, 3))
                masked_kv(0, q, par, st)
                o_mean(0, q, par)
                normed(0, q, par)
                if has_norm:
                    row_stats(0, q + 1, par)
                if front:
                    low("q0", *nxt, st)
                if has_norm:
                    row_stats(1, q + 1, par)
                if front:
                    low("q1", *nxt, st)
                scaled_k(1, q, par, st)
                second_norm(0, q, par)
                kS_low(v, 1, q, par)
                if front:
                    take_logits(*nxt, st)
                y_low(0, q, par, st)
                o_mean(1, q, par)
                if front:
                    low("k0", *nxt, st)
                normed(1, q, par)
                if has_norm:
                    norm_stats(q + 1, par)
                if front:
                    low("k1", *nxt, st)
                masked_kv(1, q, par, st)
                second_norm(1, q, par)
                weight_maxima(q, par, (0,))
                if front:
                    decayed_scores(0, *nxt, (0, 1))
                residual(0, q, par, st)
                if has_norm:
                    norm(q + 1, par)
                y_low(1, q, par, st)
                if front:
                    low("v0", *nxt, st)
                    decayed_scores(0, *nxt, (2, 3))
                    low("v1", *nxt, st)
                else:
                    weight_scales()
                residual(1, q, par, st)
                if has_norm:
                    norm_factors(q + 1, par)

            run_steps(v, prologue, step)

        @block.gpsimd
        def _(pool):
            def x_low(q, par):
                n = 2 * q + par
                pool.wait_ge(S["xhigh_ready"], n + 1)
                pool.tensor_tensor(x16[:, par, :, 1], xnT[:], x16[:, par, :, 0], ALU.subtract
                                   ).then_inc(S["xlow_ready"], 1)

            def decayed_q(q, par):
                n = 2 * q + par
                pool.wait_ge(S["qT_ready"], 2 * n + 2)
                pool.tensor_tensor(qlam[:, par].rearrange("p g (u t) -> p g u t", u=B),
                                   qT[:].rearrange("p g (u t) -> p g u t", u=B),
                                   lamq[:, :, None, :].to_broadcast([P, KT, B, P]), ALU.mult
                                   ).then_inc(S["qlam_ready"], 1)

            def update(u, q, par):
                n = 2 * q + par
                pool.wait_ge(S["kvm_ready"], 2 * n + u + 1)
                pool.tensor_tensor(state[:, u], state[:, u], lamT[:, :, None].to_broadcast([P, KT, P]), ALU.mult
                                   ).then_inc(S["decayed"], 1)
                pool.wait_ge(S["decayed"], 2 * n + u + 1)
                pool.tensor_tensor(state[:, u], state[:, u], kvm[:, u], ALU.add).then_inc(state_ready[u], 1)

            def weighted(u, q, par):
                n = 2 * q + par
                pool.wait_ge(S["on_ready"], 2 * n + u + 1)
                pool.tensor_tensor(on3[:, u], on[:, u], pnw_b[:], ALU.mult).then_inc(S["on3_ready"], 1)

            def probs_low(u, q, par):
                n = 2 * q + par
                for s in range(4):
                    pool.wait_ge(S["ph_ready"], 8 * n + 4 * u + s + 1)
                    pool.tensor_tensor(p16[:, u, 1, s], probs[:, s], p16[:, u, 0, s], ALU.subtract
                                       ).then_inc(S["pl_ready"], 1)

            def prologue():
                x_low(0, 0)
                decayed_q(0, 0)
                probs_low(0, 0, 0)

            def step(q, par, front, norm):
                kS_low(pool, 0, q, par)
                probs_low(1, q, par)
                if front:
                    x_low(*after(q, par))
                weighted(0, q, par)
                update(0, q, par)
                if front:
                    decayed_q(*after(q, par))
                weighted(1, q, par)
                update(1, q, par)
                if front:
                    probs_low(0, *after(q, par))

            run_steps(pool, prologue, step)
            pool.wait_ge(S["top_ready"], 1)
            pool.partition_all_reduce(wall[:], wtop[:], P, R_MAX).then_inc(S["all_ready"], 1)


def experts(nc, sb, sem, k):
    ident, ones, logits, wmax = k["ident"], k["ones"], k["logits"], k["wmax"]
    x1_steps, out_steps, xT_dram, xn_dram, y_dram, slot_dram = (
        k[x] for x in "x1_steps out_steps xT_dram xn_dram y_dram slot_dram".split())
    w_gu, w_dn, w_sgu, w_sdn, NCH, B = (k[x] for x in "w_gu w_dn w_sgu w_sdn NCH B".split())
    GROUPS = w_sdn.shape[0] // FFN
    HALF = NCH // 2
    TT = B * NCH
    UNITS = SLOT_TILES + AHEAD
    raw, raw_in = k["raw"], k["raw_in"]
    wscale, gate_inv, up_inv, out_inv = k["wscale"], k["gate_inv"], k["up_inv"], k["out_inv"]
    sgu, sdn = k["sgu"], k["sdn"]
    rgu = w_gu.rearrange("e (k p) c -> e p k c", p=P)
    rdn = w_dn.rearrange("e (f p) c -> e p f c", p=P)

    with ExitStack() as c:
        WG = sb(c, "WG", [P, GROUPS + EXPERTS, KT, 2, 2 * FFN], F16)
        WD = sb(c, "WD", [P, GROUPS + EXPERTS, FT, 2, DIM], F16)
        posi = sb(c, "posi", [P, TOPK, TT], I32)
        slots = sb(c, "slots", [P, UNITS, 2], I32)
        unit_e = sb(c, "unit_e", [P, UNITS], I32)
        xT = sb(c, "xT", [P, 2, KT, 2, B * P], F16)
        x1 = sb(c, "x1s", [P, 2, B, DIM])
        x_ins = [[sem(c, f"x_in{i}_{half}") for i in range(2)] for half in range(2)]

        idx = sb(c, "idx", [P, 2, 1], I32)
        xg = sb(c, "xg", [P, 2, DIM])
        idx_ready = sem(c, "idx_ready")
        xg_in = [sem(c, f"xg_in{i}") for i in range(2)]

        def index(v, q, par):
            r = 2 * q + par
            v.tensor_copy(idx[:, par], slots[:, bass.ds(r, 1), 0]).then_inc(idx_ready, 1)

        def gather(pool, q, par, passed):
            r = 2 * q + par
            wait_apart(pool, idx_ready, r + 1, passed)
            pool.indirect_dma_start(out=xg[:, par], out_offset=None, in_=xn_dram,
                                    in_offset=bass.IndirectOffsetOnAxis(ap=idx[:, par, 0:1], axis=0)
                                    ).then_inc(xg_in[par], 16)

        def at_step(a, n):
            return a[n] if isinstance(n, int) else a[bass.ds(n, 1)][0]

        def load_tokens(sp, half, par, n):
            sp.dma_start(xT[:, par], at_step(xT_dram, n)).then_inc(x_ins[half][par], 16)
            sp.dma_start(x1[:, par], at_step(x1_steps, n)).then_inc(x_ins[half][par], 16)

        def gate_up(pe, gu, x, w, tokens):
            for h in range(2):
                for f in range(FT):
                    a0 = h * FFN + f * P
                    for kk in range(KT):
                        for a, b in PASSES:
                            ins = pe.matmul(gu[:, h, f * tokens:(f + 1) * tokens],
                                            w[:, kk, b, a0:a0 + P],
                                            x[:, kk, a], start=(kk == 0 and (a, b) == PASSES[0]),
                                            stop=(kk == KT - 1 and (a, b) == PASSES[-1]))
            return ins

        def gate_up_rows(pe, gu, bank, x, w, parts):
            done = [(kk, a, b) for kk in range(KT) for a, b in PASSES]
            for i in parts:
                kk, a, b = done[i]
                ins = pe.matmul(gu[bank][:], x(kk, a), w[:, 0, kk, b, :],
                                start=(i == 0), stop=(i == len(done) - 1))
            return ins

        def down(pe, y, act_hl, w, first, last):
            for f in range(FT):
                for a, b in PASSES:
                    ins = pe.matmul(y[:], act_hl[a][:, f, :], w[:, f, b, :] if len(w.shape) == 4 else w[:, 0, f, b, :],
                                    start=(first and f == 0 and (a, b) == PASSES[0]),
                                    stop=(last and f == FT - 1 and (a, b) == PASSES[-1]))
            return ins

        FIRST, REST = range(0, 6), range(6, 3 * KT)

        def shared(half):
            n0 = half * HALF
            with ExitStack() as c:
                sg = sb(c, f"sg_{half}", [P, FT, B * P])
                actv = sb(c, f"actv_{half}", [P, 2, FT, B * P])
                ah = sb(c, f"ah_{half}", [P, 2, FT, B * P], F16)
                al = sb(c, f"al_{half}", [P, 2, FT, B * P], F16)
                ys = sb(c, f"ys_{half}", [P, B, DIM])
                gu = [c.enter_context(nc.psum_tensor(f"gu{i}_{half}", [P, 2, FT * B * P], F32)) for i in range(2)]
                yp = [c.enter_context(nc.psum_tensor(f"yp{i}_{half}", [P, DIM], F32)) for i in range(2)]
                names = "gu_full act_ready sg_ready ah_ready al_ready y_full y_read sp_passed pool_passed"
                S = {x: sem(c, x) for x in names.split()}
                x_in = x_ins[half]
                y_out = [sem(c, f"y_out{i}") for i in range(B)]
                if half == 0:
                    high = sem(c, "high")
                    split = sem(c, "split")
                    room = WG[:, GROUPS + EXPERTS - 5:].rearrange("p g k s c -> p (g k s c)").bitcast(F32)
                    R, used_room = {}, 0
                    for x, shape in dict(
                            beats=[TT, EXPERTS, EXPERTS], ties=[TT, EXPERTS, EXPERTS], mx=[TT], shifted=[TT, EXPERTS],
                            pexp=[TT, EXPERTS], psum_=[TT], prec=[TT], prob=[TT, EXPERTS], rank=[TT, EXPERTS],
                            chosen=[TOPK, TT, EXPERTS], sel=[TT, EXPERTS], wsel=[TT, EXPERTS], wsum=[TT], wrecip=[TT],
                            comb=[TT, EXPERTS], cumA=[TT, EXPERTS], cumB=[TT, EXPERTS], tots=[TT, EXPERTS],
                            used=[EXPERTS, TT], tiles=[EXPERTS], lower=[EXPERTS, EXPERTS], before=[EXPERTS, EXPERTS],
                            base=[EXPERTS], ends=[EXPERTS], pos=[TT, EXPERTS], posk=[TOPK, TT], unitf=[UNITS],
                            steps128=[TT], unit_no=[UNITS], earlier=[P]).items():
                        size = 1
                        for d in shape:
                            size *= d
                        names_ = "abc"[:len(shape)]
                        flat_ = room[:, used_room:used_room + size]
                        R[x] = flat_ if len(shape) == 1 else flat_.rearrange(
                            f"p ({' '.join(names_)}) -> p {' '.join(names_)}", **dict(zip(names_[1:], shape[1:])))
                        used_room += size
                    over = room[:, 0:2 * TT * EXPERTS * EXPERTS]
                    R["picked"] = over[:, 0:TOPK * TT * EXPERTS].rearrange("p (k t e) -> p k t e", k=TOPK, t=TT)
                    R["pickedc"] = over[:, TOPK * TT * EXPERTS:2 * TOPK * TT * EXPERTS].rearrange(
                        "p (k t e) -> p k t e", k=TOPK, t=TT)
                    R["passed"] = over[:, 2 * TOPK * TT * EXPERTS:2 * TOPK * TT * EXPERTS + UNITS * EXPERTS].rearrange(
                        "p (n e) -> p n e", e=EXPERTS)
                    payload = sb(c, f"payload_{half}", [P, TOPK, TT, 2], I32)
                    blank = sb(c, f"blank_{half}", [P, UNITS * 2], I32)
                    rp = c.enter_context(nc.psum_tensor("rp", [P, 2, TT * EXPERTS], F32))
                    rc = sem(c, "routing_chain")
                    const_ready = sem(c, "const_ready")
                    const_chain = sem(c, "const_chain")
                    shifted_ready = sem(c, "shifted_ready")
                    pexp_ready = sem(c, "pexp_ready")
                    sel_ready = sem(c, "sel_ready")
                    counts_ready = sem(c, "counts_ready")
                    payload_ready = sem(c, "payload_ready")
                    blank_out = sem(c, "blank_out")
                    slot_out = sem(c, "slot_out")
                    slot_in = sem(c, "slot_in")
                else:
                    gidx = sb(c, f"gidx_{half}", [P, B, 2 * TOPK], I32)
                    room = raw[:].rearrange("p b i c -> p (b i) c")
                    gy = room[:, 0:2 * B * TOPK].rearrange("p (u i) c -> p u i c", u=B)
                    x1o = room[:, 2 * B * TOPK:2 * B * TOPK + 2 * B].rearrange("p (s u) c -> p s u c", s=2)
                    yo = xg
                    S |= {x: sem(c, x) for x in "gidx_ready ysum_ready own_ready oldsum_ready old_ready".split()}
                    gy_in = [sem(c, f"gy_in{i}") for i in range(B)]
                    xo_in = [sem(c, f"xo_in{i}") for i in range(2)]
                    yo_out = [sem(c, f"yo_out{i}") for i in range(B)]

                def run_steps(eng, step):
                    step(0, 0, True, False)
                    step(0, 1, False, False)
                    with eng.Fori(1, HALF // 2 - 1) as q:
                        step(q, 0, False, False)
                        step(q, 1, False, False)
                    step(HALF // 2 - 1, 0, False, False)
                    step(HALF // 2 - 1, 1, False, True)

                def unit(q, par, g):
                    return GROUPS * (2 * q + par) + g

                def early(q, par):
                    return isinstance(q, int) and 2 * q + par < 2

                def pieces(g, late_only):
                    if late_only:
                        late = g - GROUPS // 2
                        return range(late * PIECES // 2, (late + 1) * PIECES // 2) if late >= 0 else ()
                    more = PIECES - GROUPS
                    return range(g + min(g, more), g + 1 + min(g + 1, more))

                block = c.enter_context(nc.Block())

                @block.sync
                def _(sp):
                    def load(q, par):
                        n = 2 * q + par
                        if half == 0 or not (isinstance(n, int) and n == 0):
                            load_tokens(sp, half, par, n + n0)
                        if half == 1:
                            sp.dma_start(x1o[:, par], at_step(x1_steps, n)).then_inc(xo_in[par], 16)

                    def raw_shared(g):
                        sp.wait_ge(split, PIECES * (g - 1))
                        load_group(sp, k, g)

                    def raw_routed(q, par):
                        e = 2 * q + par
                        wait_apart(sp, split, PIECES * (e + GROUPS - 1), S["sp_passed"])
                        sp.dma_start(raw[:, par, 0:KT], at_step(rgu, e)).then_inc(raw_in[par], 16)
                        sp.dma_start(raw[:, par, KT:], at_step(rdn, e)).then_inc(raw_in[par], 16)
                        sp.sem_inc(raw_in[par], 16)

                    load(0, 0)
                    if half == 0:
                        for g in range(2, GROUPS):
                            raw_shared(g)

                    def step(q, par, first, last):
                        n = 2 * q + par
                        if half == 0:
                            raw_routed(q, par)
                            if last:
                                sp.wait_ge(slot_out, 16 * TOPK * TT)
                                sp.dma_start(slots[:], slot_dram.rearrange("(a p) b -> p a b", p=P)).then_inc(slot_in, 16)
                        if not last:
                            q1, p1 = (q, 1) if par == 0 else (q + 1, 0)
                            if not first:
                                sp.wait_ge(S["y_read"], B * n)
                                if half == 1:
                                    sp.wait_ge(S["old_ready"], B * n)
                            load(q1, p1)
                        if first and half == 0:
                            sp.wait_ge(const_ready, 1)
                            sp.dma_start(slot_dram.rearrange("(p a) b -> p (a b)", p=P), blank[:]).then_inc(blank_out, 16)
                        for u in range(B):
                            if half == 0:
                                sp.wait_ge(S["y_read"], B * n + u + 1)
                                dst = at_step(x1_steps, n + n0)
                            else:
                                sp.wait_ge(S["own_ready"], B * n + u + 1)
                                dst = at_step(out_steps, n + n0)
                            sp.dma_start(dst[:, u], ys[:, u]).then_inc(y_out[u], 16)
                            if half == 1:
                                sp.wait_ge(S["old_ready"], B * n + u + 1)
                                sp.dma_start(at_step(out_steps, n)[:, u], yo[:, u]).then_inc(yo_out[u], 16)

                    run_steps(sp, step)
                    if half == 0:
                        sp.wait_ge(slot_in, 16)
                    for u in range(B):
                        sp.wait_ge(y_out[u], 16 * HALF)
                        if half == 1:
                            sp.wait_ge(yo_out[u], 16 * HALF)

                @block.tensor
                def _(pe):
                    if half == 0:
                        pe.wait_ge(split, PIECES)
                    pe.wait_ge(x_in[0], 32)
                    gate_up(pe, gu[0], xT[:, 0], WG[:, 0], B * P).then_inc(S["gu_full"], 1)

                    def step(q, par, first, last):
                        n = 2 * q + par
                        for g in range(GROUPS):
                            i = unit(q, par, g)
                            if not (last and g == GROUPS - 1):
                                g1 = (g + 1) % GROUPS
                                q1, p1 = (q, par) if g1 else (q, 1) if par == 0 else (q + 1, 0)
                                if g1 == 0:
                                    pe.wait_ge(x_in[p1], 32 * (q1 + 1))
                                elif half == 0 and first:
                                    pe.wait_ge(split, PIECES * (g1 + 1))
                                if not (first and g == 0):
                                    pe.wait_ge(S["act_ready"], i)
                                gate_up(pe, gu[g1 % 2], xT[:, p1], WG[:, g1], B * P).then_inc(S["gu_full"], 1)
                            pe.wait_ge(S["al_ready"], i + 1)
                            for u in range(B):
                                if g == 0 and not first:
                                    pe.wait_ge(S["y_read"], B * (n - 1) + u + 1)
                                rows = slice(u * P, (u + 1) * P)
                                ins = down(pe, yp[u], (ah[:, g % 2, :, rows], al[:, g % 2, :, rows]), WD[:, g],
                                           g == 0, g == GROUPS - 1)
                                if g == GROUPS - 1:
                                    ins.then_inc(S["y_full"], 1)
                            if half == 0 and isinstance(i, int) and i == GROUPS:
                                pe.wait_ge(sel_ready, 1)
                                pe.wait_ge(const_ready, 1)
                                flat = R["sel"].rearrange("p t e -> p (t e)")
                                pe.matmul(rp[:, 0, :], R["earlier"], flat, start=True, stop=True)
                                pe.matmul(rp[:, 1, :], ones[:], flat, start=True, stop=True).then_inc(counts_ready, 1)

                    run_steps(pe, step)

                @block.scalar
                def _(act):
                    def high_part(place, b, i, gu_scale, dn_scale):
                        dst = WG[:, place, i, 0, :] if i < KT else WD[:, place, i - KT, 0, :]
                        act.activation(dst, raw[:, b, i], ACT.Copy, scale=gu_scale if i < KT else dn_scale).then_inc(high, 1)

                    def high_group(g):
                        act.wait_ge(raw_in[g % 2], 48 * (g // 2 + 1))
                        for i in range(PIECES):
                            high_part(g, g % 2, i, wscale[:, 2:3], wscale[:, 3:4])

                    def high_routed(q, par, i):
                        e = 2 * q + par
                        place = e + GROUPS
                        if i == 0:
                            act.wait_ge(raw_in[par], 48 * (q + 1 + GROUPS // 2))
                        if isinstance(e, int):
                            high_part(place, par, i, wscale[:, 0:1], wscale[:, 1:2])
                            return
                        dst = WG[:, bass.ds(place, 1), i, 0, :] if i < KT else WD[:, bass.ds(place, 1), i - KT, 0, :]
                        act.activation(dst, raw[:, par:par + 1, i], ACT.Copy,
                                       scale=wscale[:, 0:1] if i < KT else wscale[:, 1:2]).then_inc(high, 1)

                    if half == 0:
                        high_group(0)
                        act.wait_ge(shifted_ready, 1)
                        act.activation(R["pexp"], R["shifted"], ACT.Exp).then_inc(pexp_ready, 1)
                        high_group(1)

                    def step(q, par, first, last):
                        for g in range(GROUPS):
                            i = unit(q, par, g)
                            act.wait_ge(S["gu_full"], i + 1)
                            act.activation(sg[:], gu[g % 2][:, 0].rearrange("p (f t) -> p f t", f=FT), ACT.Silu,
                                           scale=gate_inv[:, 1:2]).then_inc(S["sg_ready"], 1)
                            act.wait_ge(S["act_ready"], i + 1)
                            act.activation(ah[:, g % 2], actv[:, g % 2], ACT.Copy).then_inc(S["ah_ready"], 1)
                            if half == 0:
                                if first and g < GROUPS - 2:
                                    high_group(g + 2)
                                for piece in pieces(g, early(q, par)):
                                    high_routed(q, par, piece)

                    run_steps(act, step)

                @block.vector
                def _(v):
                    steps = [0]

                    def link(ins):
                        steps[0] += 1
                        ins.then_inc(rc, 1)
                        v.wait_ge(rc, steps[0])

                    def low_part(place, b, i, gu_scale, dn_scale):
                        w = WG[:, place, i] if i < KT else WD[:, place, i - KT]
                        v.scalar_tensor_tensor(out=w[:, 1, :], in0=raw[:, b, i], scalar=gu_scale if i < KT else dn_scale,
                                               in1=w[:, 0, :], op0=ALU.mult, op1=ALU.subtract).then_inc(split, 1)

                    def low_group(g):
                        for i in range(PIECES):
                            v.wait_ge(high, PIECES * g + i + 1)
                            low_part(g, g % 2, i, wscale[:, 2:3], wscale[:, 3:4])

                    def low_routed(q, par, i):
                        e = 2 * q + par
                        v.wait_ge(high, PIECES * (e + GROUPS) + i + 1)
                        if isinstance(e, int):
                            low_part(e + GROUPS, par, i, wscale[:, 0:1], wscale[:, 1:2])
                            return
                        at_e = bass.ds(e + GROUPS, 1)
                        w = (WG[:, at_e, i, :, :] if i < KT else WD[:, at_e, i - KT, :, :])
                        v.scalar_tensor_tensor(out=w[:, 0, 1, :], in0=raw[:, par, i],
                                               scalar=wscale[:, 0:1] if i < KT else wscale[:, 1:2],
                                               in1=w[:, 0, 0, :], op0=ALU.mult, op1=ALU.subtract).then_inc(split, 1)

                    lg = logits[:].rearrange("p u n e -> p (u n) e")
                    FULL = [P, TT, EXPERTS, EXPERTS]

                    def probabilities():
                        v.wait_ge(pexp_ready, 1)
                        link(v.tensor_reduce(R["psum_"], R["pexp"], AX.X, ALU.add))
                        link(v.reciprocal(R["prec"], R["psum_"]))
                        link(v.tensor_tensor(R["prob"], R["pexp"], R["prec"][:, :, None].to_broadcast([P, TT, EXPERTS]),
                                             ALU.mult))

                    def compare():
                        of, by = R["prob"][:, :, :, None], R["prob"][:, :, None, :]
                        v.wait_ge(const_ready, 1)
                        v.tensor_tensor(R["beats"], by.to_broadcast(FULL), of.to_broadcast(FULL), ALU.is_gt)
                        link(v.tensor_tensor(R["ties"], by.to_broadcast(FULL), of.to_broadcast(FULL), ALU.is_equal))

                    def compare_equal():
                        link(v.tensor_tensor(R["ties"], R["ties"], R["lower"][:, None].to_broadcast(FULL), ALU.mult))
                        link(v.tensor_tensor(R["beats"], R["beats"], R["ties"], ALU.add))

                    def ranks():
                        link(v.tensor_reduce(R["rank"], R["beats"], AX.X, ALU.add))
                        for i in range(TOPK):
                            v.tensor_scalar(R["chosen"][:, i], R["rank"], float(i), None, ALU.is_equal)
                        v.tensor_scalar(R["sel"], R["rank"], float(TOPK), None, ALU.is_lt).then_inc(sel_ready, 1)
                        v.wait_ge(sel_ready, 1)

                    def combine_weights():
                        link(v.tensor_tensor(R["wsel"], R["sel"], R["prob"], ALU.mult))
                        link(v.tensor_reduce(R["wsum"], R["wsel"], AX.X, ALU.add))
                        link(v.reciprocal(R["wrecip"], R["wsum"]))
                        link(v.tensor_tensor(R["comb"], R["wsel"], R["wrecip"][:, :, None].to_broadcast([P, TT, EXPERTS]),
                                             ALU.mult))

                    def positions():
                        v.wait_ge(counts_ready, 1)
                        link(v.tensor_copy(R["tots"], rp[:, 1, :].rearrange("p (t e) -> p t e", e=EXPERTS)))
                        a, b, d = R["tots"], R["cumA"], 1
                        while d < TT:
                            v.tensor_copy(b[:, 0:d], a[:, 0:d])
                            link(v.tensor_tensor(b[:, d:], a[:, d:], a[:, 0:TT - d], ALU.add))
                            a, b, d = b, (R["cumB"] if b is R["cumA"] else R["cumA"]), 2 * d
                        v_counts = a[:, TT - 1]
                        link(v.tensor_tensor(R["used"], v_counts[:, :, None].to_broadcast([P, EXPERTS, TT]),
                                             R["steps128"][:, None, :].to_broadcast([P, EXPERTS, TT]), ALU.is_gt))
                        link(v.tensor_reduce(R["tiles"], R["used"], AX.X, ALU.add))
                        link(v.tensor_tensor(R["before"], R["lower"],
                                             R["tiles"][:, None, :].to_broadcast([P, EXPERTS, EXPERTS]), ALU.mult))
                        link(v.tensor_reduce(R["base"], R["before"], AX.X, ALU.add))
                        v.tensor_tensor(R["ends"], R["base"], R["tiles"], ALU.add)
                        link(v.tensor_tensor(R["pos"], a[:], R["tots"], ALU.subtract))
                        link(v.tensor_tensor(R["pos"], R["pos"], rp[:, 0, :].rearrange("p (t e) -> p t e", e=EXPERTS),
                                             ALU.add))
                        link(v.tensor_scalar(R["base"], R["base"], float(P), None, ALU.mult))
                        link(v.tensor_tensor(R["pos"], R["pos"], R["base"][:, None, :].to_broadcast([P, TT, EXPERTS]),
                                             ALU.add))

                    def send():
                        whole = [P, TOPK, TT, EXPERTS]
                        v.tensor_tensor(R["picked"], R["chosen"], R["pos"][:, None].to_broadcast(whole), ALU.mult)
                        link(v.tensor_tensor(R["pickedc"], R["chosen"], R["comb"][:, None].to_broadcast(whole), ALU.mult))
                        v.tensor_reduce(payload[:].bitcast(F32)[:, :, :, 1], R["pickedc"], AX.X, ALU.add)
                        link(v.tensor_reduce(R["posk"], R["picked"], AX.X, ALU.add))
                        v.tensor_copy(posi[:], R["posk"]).then_inc(payload_ready, 1)

                    def unit_experts():
                        full = [P, UNITS, EXPERTS]
                        link(v.tensor_tensor(R["passed"], R["ends"][:, None, :].to_broadcast(full),
                                             R["unit_no"][:, :, None].to_broadcast(full), ALU.is_le))
                        link(v.tensor_reduce(R["unitf"], R["passed"], AX.X, ALU.add))
                        v.tensor_scalar(unit_e[:], R["unitf"], float(EXPERTS - 1), float(GROUPS), ALU.min, ALU.add)

                    if half == 0:
                        link(v.tensor_reduce(R["mx"], lg, AX.X, ALU.max))
                        v.tensor_tensor(R["shifted"], lg, R["mx"][:, :, None].to_broadcast([P, TT, EXPERTS]), ALU.subtract
                                        ).then_inc(shifted_ready, 1)
                        low_group(0)
                        low_group(1)

                    def token_outputs(q, par):
                        n = 2 * q + par
                        for u in range(B):
                            v.wait_ge(S["y_full"], B * n + u + 1)
                            v.wait_ge(x_in[par], 32 * (q + 1))
                            v.wait_ge(y_out[u], 16 * n)
                            v.scalar_tensor_tensor(out=ys[:, u], in0=yp[u][:], scalar=out_inv[:, 1:2], in1=x1[:, par, u],
                                                   op0=ALU.mult, op1=ALU.add).then_inc(S["y_read"], 1)
                        if half == 1:
                            for u in range(B):
                                v.wait_ge(S["y_read"], B * n + u + 1)
                                v.wait_ge(gy_in[u], 64 * (n + 1))
                                v.tensor_tensor(ys[:, u], ys[:, u], gy[:, u, 0], ALU.add).then_inc(S["ysum_ready"], 1)
                                v.wait_ge(S["ysum_ready"], B * n + u + 1)
                                v.tensor_tensor(ys[:, u], ys[:, u], gy[:, u, 1], ALU.add).then_inc(S["own_ready"], 1)

                    def gather_places(q, par, u):
                        n = 2 * q + par
                        v.wait_ge(gy_in[u], 64 * n)
                        for i, m in enumerate((n + n0, n)):
                            col = posi[:].rearrange("p k (u n) -> p k u n", u=B)[:, :, u, bass.ds(m, 1)]
                            ins = v.tensor_copy(gidx[:, u, TOPK * i:TOPK * (i + 1)], col[:, :, 0])
                        ins.then_inc(S["gidx_ready"], 1)

                    def step(q, par, first, last):
                        if half == 1:
                            for u in range(B):
                                gather_places(q, par, u)
                        for g in range(GROUPS):
                            i = unit(q, par, g)
                            v.wait_ge(S["sg_ready"], i + 1)
                            v.scalar_tensor_tensor(out=actv[:, g % 2],
                                                   in0=gu[g % 2][:, 1].rearrange("p (f t) -> p f t", f=FT),
                                                   scalar=up_inv[:, 1:2], in1=sg[:],
                                                   op0=ALU.mult, op1=ALU.mult).then_inc(S["act_ready"], 1)
                            v.wait_ge(S["ah_ready"], i + 1)
                            v.tensor_tensor(al[:, g % 2], actv[:, g % 2], ah[:, g % 2], ALU.subtract
                                            ).then_inc(S["al_ready"], 1)
                            if g == 0 and not first:
                                token_outputs(*((q, 0) if par == 1 else (q - 1, 1)))
                            if half == 0:
                                if first and g < GROUPS - 2:
                                    low_group(g + 2)
                                for piece in pieces(g, early(q, par)):
                                    low_routed(q, par, piece)
                            if half == 0 and isinstance(i, int) and i < 2 * GROUPS:
                                (probabilities, compare, compare_equal, ranks, combine_weights, positions, send,
                                 unit_experts)[i]()
                            if half == 0 and last and g == 1:
                                v.wait_ge(slot_in, 16)
                                index(v, 0, 0)
                                index(v, 0, 1)
                        if last:
                            token_outputs(q, par)

                    run_steps(v, step)

                @block.gpsimd
                def _(pool):
                    if half == 0:
                        pool.memset(R["earlier"], 1.0)
                        pool.memset(R["lower"], 1.0)
                        pool.memset(blank[:], 0).then_inc(const_chain, 1)
                        pool.wait_ge(const_chain, 1)
                        pool.affine_select(out=R["earlier"], in_=R["earlier"], compare_op=ALU.is_gt, fill=0.0, base=0,
                                           pattern=[[1, P]], channel_multiplier=-1)
                        pool.affine_select(out=R["lower"], in_=R["lower"], compare_op=ALU.is_gt, fill=0.0, base=0,
                                           pattern=[[1, EXPERTS], [-1, EXPERTS]], channel_multiplier=0)
                        pool.iota(R["steps128"], [[P, TT]], base=0, channel_multiplier=0,
                                  allow_small_or_imprecise_dtypes=True)
                        pool.iota(R["unit_no"], [[1, UNITS]], base=0, channel_multiplier=0,
                                  allow_small_or_imprecise_dtypes=True)
                        pool.iota(payload[:, :, :, 0], [[0, TOPK], [NCH * P, B], [P, NCH]], base=0, channel_multiplier=1
                                  ).then_inc(const_ready, 1)
                        pool.wait_ge(payload_ready, 1)
                        pool.wait_ge(blank_out, 16)
                        for kk in range(TOPK):
                            for t in range(TT):
                                pool.indirect_dma_start(
                                    out=slot_dram, out_offset=bass.IndirectOffsetOnAxis(ap=posi[:, kk, t:t + 1], axis=0),
                                    in_=payload[:, kk, t, :], in_offset=None).then_inc(slot_out, 16)
                        for par in range(2):
                            gather(pool, 0, par, S["pool_passed"])
                        return

                    def step(q, par, first, last):
                        n = 2 * q + par
                        for u in range(B):
                            if not first:
                                pool.wait_ge(S["own_ready"], B * (n - 1) + u + 1)
                                pool.wait_ge(S["old_ready"], B * (n - 1) + u + 1)
                            wait_apart(pool, S["gidx_ready"], B * n + u + 1, S["pool_passed"])
                            for i in range(2 * TOPK):
                                pool.indirect_dma_start(
                                    out=gy[:, u, i], out_offset=None, in_=y_dram,
                                    in_offset=bass.IndirectOffsetOnAxis(ap=gidx[:, u, i:i + 1], axis=0)).then_inc(gy_in[u], 16)
                        for u in range(B):
                            pool.wait_ge(gy_in[u], 64 * (n + 1))
                            pool.wait_ge(xo_in[par], 16 * (q + 1))
                            pool.wait_ge(yo_out[u], 16 * n)
                            pool.tensor_tensor(yo[:, u], x1o[:, par, u], gy[:, u, 2], ALU.add).then_inc(S["oldsum_ready"], 1)
                            pool.wait_ge(S["oldsum_ready"], B * n + u + 1)
                            pool.tensor_tensor(yo[:, u], yo[:, u], gy[:, u, 3], ALU.add).then_inc(S["old_ready"], 1)

                    run_steps(pool, step)

        def routed():
            with ExitStack() as c:
                cw = sb(c, "cw", [P, 2])
                xh = sb(c, "xh", [P, 2, 2, KT, P], F16)
                sg = sb(c, "sgr", [P, 2, FFN])
                actv = sb(c, "actvr", [P, 2, FFN])
                ah = sb(c, "ahr", [P, 2, FT, P], F16)
                al = sb(c, "alr", [P, 2, FT, P], F16)
                ysb = sb(c, "ysb", [P, 2, DIM])
                gu = [c.enter_context(nc.psum_tensor(f"rgu{i}", [P, 2 * FFN], F32)) for i in range(2)]
                at = [c.enter_context(nc.psum_tensor(f"rat{i}", [P, FT, P], F32)) for i in range(2)]
                yp = [c.enter_context(nc.psum_tensor(f"ryp{i}", [P, DIM], F32)) for i in range(2)]
                xt = c.enter_context(nc.psum_tensor("xt", [P, KT, P], F32))
                names = "gu_full act_ready sg_ready at_full ah_ready al_ready y_full y_ready xt_full xh_ready xl_ready cw_ready pool_passed"
                S = {x: sem(c, "r_" + x) for x in names.split()}
                y_out = [sem(c, f"ry_out{i}") for i in range(2)]
                block = c.enter_context(nc.Block())

                def run_steps(eng, step):
                    step(0, 0, True)
                    step(0, 1, False)
                    with eng.Fori(1, SLOT_TILES // 2) as q:
                        step(q, 0, False)
                        step(q, 1, False)

                @block.sync
                def _(sp):
                    rows = y_dram.rearrange("(r p) c -> r p c", p=P)
                    load_tokens(sp, 1, 0, HALF)

                    def step(q, par, first):
                        r = 2 * q + par
                        sp.wait_ge(S["y_ready"], r + 1)
                        sp.dma_start(rows[r] if isinstance(r, int) else rows[bass.ds(r, 1)][0], ysb[:, par]
                                     ).then_inc(y_out[par], 16)

                    run_steps(sp, step)
                    for par in range(2):
                        sp.wait_ge(y_out[par], 16 * (SLOT_TILES // 2))

                @block.gpsimd
                def _(pool):
                    for par in range(2):
                        pool.wait_ge(S["xt_full"], par + 1)
                        gather(pool, 1, par, S["pool_passed"])

                    def step(q, par, first):
                        pool.wait_ge(S["xt_full"], 2 * q + par + 3)
                        gather(pool, q + 2, par, S["pool_passed"])

                    run_steps(pool, step)
                    for par in range(2):
                        pool.wait_ge(xg_in[par], 16 * (SLOT_TILES // 2 + 2))

                @block.tensor
                def _(pe):
                    def turn(q, par):
                        pe.wait_ge(xg_in[par], 16 * (q + 1))
                        pe.wait_ge(S["xl_ready"], 2 * q + par)
                        for kk in range(KT):
                            ins = pe.transpose(xt[:, kk, :], xg[:, par, kk * P:(kk + 1) * P], ident[:])
                        ins.then_inc(S["xt_full"], 1)

                    def xs(par):
                        return lambda kk, a: xh[:, par, a, kk, :]

                    def place(r):
                        e = pe.value_load(unit_e[0:1, bass.ds(r, 1)], min_val=GROUPS, max_val=GROUPS + EXPERTS - 1)
                        return bass.ds(e, 1)

                    turn(0, 0)
                    turn(0, 1)
                    pe.wait_ge(S["xl_ready"], 1)
                    gate_up_rows(pe, gu, 0, xs(0), WG[:, place(0)], range(3 * KT)).then_inc(S["gu_full"], 1)

                    def tile(q, par, first, places):
                        r = 2 * q + par
                        own, nxt = places[-2:]
                        pe.wait_ge(S["xl_ready"], r + 2)
                        if not first:
                            pe.wait_ge(S["act_ready"], r)
                        gate_up_rows(pe, gu, 1 - par, xs(1 - par), WG[:, nxt], FIRST)
                        pe.wait_ge(S["act_ready"], r + 1)
                        for f in range(FT):
                            ins = pe.transpose(at[par][:, f, :], actv[:, par, f * P:(f + 1) * P], ident[:])
                        ins.then_inc(S["at_full"], 1)
                        turn(q + 1, par)
                        gate_up_rows(pe, gu, 1 - par, xs(1 - par), WG[:, nxt], REST).then_inc(S["gu_full"], 1)
                        if len(places) <= UNROLL:
                            places.append(place(r + 2))
                        if not first:
                            pe.wait_ge(S["y_ready"], r - 1)
                        pe.wait_ge(S["al_ready"], r + 1)
                        down(pe, yp[par], (ah[:, par], al[:, par]), WD[:, own], True, True).then_inc(S["y_full"], 1)

                    UNROLL = 8

                    def some(h, first):
                        places = [place(UNROLL * h), place(UNROLL * h + 1)]
                        for i in range(UNROLL):
                            tile(UNROLL // 2 * h + i // 2, i % 2, first and i == 0, places)

                    some(0, True)
                    with pe.Fori(1, SLOT_TILES // UNROLL) as h:
                        some(h, False)

                @block.scalar
                def _(act):
                    def x_high(q, par):
                        r = 2 * q + par
                        act.wait_ge(S["xt_full"], r + 1)
                        act.activation(xh[:, par, 0], xt[:], ACT.Copy, scale=X_SCALE).then_inc(S["xh_ready"], 1)

                    def y_evac(q, par):
                        r = 2 * q + par
                        act.wait_ge(S["y_full"], r + 1)
                        act.wait_ge(y_out[par], 16 * q)
                        act.activation(ysb[:, par], yp[par][:], ACT.Copy, scale=out_inv[:, 0:1]).then_inc(S["y_ready"], 1)

                    x_high(0, 0)
                    x_high(0, 1)

                    def step(q, par, first):
                        r = 2 * q + par
                        act.wait_ge(S["gu_full"], r + 1)
                        act.activation(sg[:, par], gu[par][:, 0:FFN], ACT.Silu, scale=gate_inv[:, 0:1]
                                       ).then_inc(S["sg_ready"], 1)
                        if not first:
                            y_evac(*((q, 0) if par == 1 else (q - 1, 1)))
                        act.wait_ge(S["at_full"], r + 1)
                        act.activation(ah[:, par], at[par][:], ACT.Copy).then_inc(S["ah_ready"], 1)
                        x_high(q + 1, par)

                    run_steps(act, step)
                    y_evac(SLOT_TILES // 2 - 1, 1)

                @block.vector
                def _(v):
                    def weight(q, par):
                        r = 2 * q + par
                        v.tensor_scalar(cw[:, par:par + 1], slots[:].bitcast(F32)[:, bass.ds(r, 1), 1], up_inv[:, 0:1], None,
                                        ALU.mult).then_inc(S["cw_ready"], 1)

                    def x_low(q, par):
                        r = 2 * q + par
                        v.wait_ge(S["xh_ready"], r + 1)
                        v.scalar_tensor_tensor(out=xh[:, par, 1], in0=xt[:], scalar=X_SCALE, in1=xh[:, par, 0],
                                               op0=ALU.mult, op1=ALU.subtract).then_inc(S["xl_ready"], 1)

                    weight(0, 0)
                    weight(0, 1)
                    for par in range(2):
                        v.wait_ge(xg_in[par], 16)
                        index(v, 1, par)
                        x_low(0, par)

                    def step(q, par, first):
                        r = 2 * q + par
                        v.wait_ge(S["cw_ready"], r + 1)
                        v.wait_ge(S["sg_ready"], r + 1)
                        v.scalar_tensor_tensor(out=actv[:, par], in0=gu[par][:, FFN:2 * FFN], scalar=cw[:, par:par + 1],
                                               in1=sg[:, par], op0=ALU.mult, op1=ALU.mult).then_inc(S["act_ready"], 1)
                        v.wait_ge(S["ah_ready"], r + 1)
                        v.tensor_tensor(al[:, par], at[par][:], ah[:, par], ALU.subtract).then_inc(S["al_ready"], 1)
                        x_low(q + 1, par)
                        v.wait_ge(S["act_ready"], r + 1)
                        weight(q + 1, par)
                        v.wait_ge(xg_in[par], 16 * (q + 2))
                        index(v, q + 2, par)

                    run_steps(v, step)

        shared(0)
        routed()
        shared(1)


_INS = ["L0_attn_x", "L0_attn_qkv_w", "L0_attn_qkv_norm_w", "L0_attn_proj_w", "L0_attn_proj_norm_w",
        "L0_attn_norm_w", "L0_attn_s", "L0_ffn_w_gate", "L0_ffn_w_gate_up", "L0_ffn_w_down",
        "L0_ffn_w_sh_gate_up", "L0_ffn_w_sh_down"]


def kernel(**inputs):
    import numpy as _np
    import concourse.bacc as _bacc
    from concourse.bass_utils import run_bass_kernel_spmd as _run

    nc = _bacc.Bacc("TRN2", target_bir_lowering=False, num_devices=1)
    arrays, args = {}, []
    for name in _INS:
        a = _np.ascontiguousarray(inputs[name])
        arrays[f"in_{name}"] = a
        args.append(nc.dram_tensor(f"in_{name}", a.shape, mybir.dt.from_np(a.dtype), kind="ExternalInput").ap())
    shape = inputs["L0_attn_x"].shape
    out = nc.dram_tensor("out_0", shape, F32, kind="ExternalOutput").ap()
    build(nc, *args, out)
    r = _run(nc, [arrays], core_ids=[0])
    return r.results[0]["out_0"]
```
